# Optimizing a Trainium2 kernel written in Bass

```python
import numpy as np
import jax
import jax.numpy as jnp

def _softmax(x, axis=-1):
    return jax.nn.softmax(x, axis=axis)

def _gelu(x):
    return jax.nn.gelu(x, approximate=True)

def _silu(x):
    return jax.nn.silu(x)

def _sigmoid(x):
    return jax.nn.sigmoid(x)

def _layernorm(x, axis=-1, eps=1e-05):
    m = jnp.mean(x, axis=axis, keepdims=True)
    v = jnp.var(x, axis=axis, keepdims=True)
    return (x - m) / jnp.sqrt(v + eps)

def _scatter_add(tgt, idx, src, axis=0):
    return tgt.at[idx].add(src)

def _segment_sum(src, seg, n):
    return jax.ops.segment_sum(src, seg, n)
kernel_name = 'mk_prb_d1_jaxref_r8_91d995'

def setup_inputs(seed: int=0):
    np.random.seed(seed)
    _w = jnp.asarray

    def _L0_attn_setup():
        import jax, jax.numpy as jnp
        import numpy as np
        EMBED_DIM = 128
        HEADS = 16
        HEAD_DIM = EMBED_DIM // HEADS
        TOP_K_RATIO = 0.7
        NEG_FILL = -10000.0
        key = jax.random.key(seed)
        ks = jax.random.split(key, 5)
        B, T, E = (2, 256, EMBED_DIM)
        x = jax.random.normal(ks[0], (B, T, E), dtype=jnp.float32)
        s1 = 1.0 / np.sqrt(E)
        qkv_w = jax.random.uniform(ks[1], (3 * E, E), jnp.float32, -s1, s1)
        qkv_b = jax.random.uniform(ks[2], (3 * E,), jnp.float32, -s1, s1)
        out_w = jax.random.uniform(ks[3], (E, E), jnp.float32, -s1, s1)
        out_b = jax.random.uniform(ks[4], (E,), jnp.float32, -s1, s1)
        return {'x': x, 'qkv_w': qkv_w, 'qkv_b': qkv_b, 'out_w': out_w, 'out_b': out_b}
    _L0_attn_in = _L0_attn_setup()

    def _L0_ffn_setup():
        import jax, jax.numpy as jnp
        import numpy as np
        DIM = 128
        DEPTH = 6
        HEADS = 16
        DIM_HEAD = 64
        WINDOW = 32
        INNER = HEADS * DIM_HEAD
        DIM_INNER = int(DIM * 4 * 2 / 3)
        QK_SCALE = 8.0

        def shift_tokens(t):
            a, s = jnp.split(t, 2, -1)
            s = jnp.pad(s, ((0, 0), (1, 0), (0, 0)))[:, :-1]
            return jnp.concatenate([a, s], -1)

        def l2norm(t):
            return t / jnp.maximum(jnp.linalg.norm(t, axis=-1, keepdims=True), 1e-12)

        def rotate_half(x):
            x1, x2 = jnp.split(x, 2, -1)
            return jnp.concatenate([-x2, x1], -1)

        def rotary_tables(n):
            half = jnp.arange(0, DIM_HEAD, 2, dtype=jnp.float32)
            inv_freq = 1.0 / 10000.0 ** (half / DIM_HEAD)
            t = jnp.arange(n, dtype=jnp.float32)
            freqs = t[:, None] * inv_freq[None, :]
            freqs = jnp.concatenate([freqs, freqs], -1)
            base_scale = (half + 0.4 * DIM_HEAD) / (1.4 * DIM_HEAD)
            power = (t - n // 2) / (WINDOW // 2)
            scale = base_scale[None, :] ** power[:, None]
            scale = jnp.concatenate([scale, scale], -1)
            return (freqs, scale)

        def local_attention(q, k, v):
            b, h, n, d = q.shape
            w = WINDOW
            nw = n // w
            bq = q.reshape(b, h, nw, w, d)
            bk = k.reshape(b, h, nw, w, d)
            bv = v.reshape(b, h, nw, w, d)

            def look(t):
                p = jnp.pad(t, ((0, 0), (0, 0), (1, 0), (0, 0), (0, 0)))
                return jnp.concatenate([p[:, :, :nw], p[:, :, 1:]], axis=3)
            bk2, bv2 = (look(bk), look(bv))
            seq = jnp.arange(n).reshape(nw, w)
            seq_p = jnp.pad(seq, ((1, 0), (0, 0)), constant_values=-1)
            jt = jnp.concatenate([seq_p[:nw], seq_p[1:]], axis=1)
            it = seq[:, :, None]
            jb = jt[:, None, :]
            mask = (it < jb) | (it > jb + w) | (jb == -1)
            sim = jnp.einsum('bhwie,bhwje->bhwij', bq, bk2) * QK_SCALE
            sim = jnp.where(mask, -jnp.finfo(sim.dtype).max, sim)
            attn = jax.nn.softmax(sim, -1)
            out = jnp.einsum('bhwij,bhwje->bhwie', attn, bv2)
            return out.reshape(b, h, n, d)

        def attn_layer(x, Wqkv, qs, ksc, Wo):
            b, n, _ = x.shape
            qkv = x @ Wqkv
            q, k, v = jnp.split(qkv, 3, -1)
            sh = lambda t: t.reshape(b, n, HEADS, DIM_HEAD).transpose(0, 2, 1, 3)
            q, k, v = (sh(q), sh(k), sh(v))
            q = l2norm(q) * qs
            k = l2norm(k) * ksc
            freqs, scale = rotary_tables(n)
            cos, sin = (jnp.cos(freqs), jnp.sin(freqs))
            q = q * cos * scale + rotate_half(q) * sin * scale
            inv = 1.0 / scale
            k = k * cos * inv + rotate_half(k) * sin * inv
            out = local_attention(q, k, v)
            out = out.transpose(0, 2, 1, 3).reshape(b, n, INNER)
            return out @ Wo

        def ffn_layer(x, g, bln, W1, b1, W2, b2):
            mu = x.mean(-1, keepdims=True)
            var = ((x - mu) ** 2).mean(-1, keepdims=True)
            xn = (x - mu) / jnp.sqrt(var + 1e-05) * g + bln
            hg = xn @ W1 + b1
            a, gate = jnp.split(hg, 2, -1)
            return a * jax.nn.gelu(gate, approximate=False) @ W2 + b2
        key = jax.random.key(seed)
        ks = jax.random.split(key, 8)
        B, N = (2, 256)
        init = lambda k, shape: jax.random.normal(k, shape, jnp.float32) * 0.02
        return {'x': jax.random.normal(ks[0], (B, N, DIM), jnp.float32), 'Wqkv': init(ks[1], (DEPTH, DIM, 3 * INNER)), 'q_scale': jnp.ones((DEPTH, DIM_HEAD), jnp.float32), 'k_scale': jnp.ones((DEPTH, DIM_HEAD), jnp.float32), 'Wo': init(ks[2], (DEPTH, INNER, DIM)), 'ln_g': jnp.ones((DEPTH, DIM), jnp.float32), 'ln_b': jnp.zeros((DEPTH, DIM), jnp.float32), 'W1': init(ks[3], (DEPTH, DIM, 2 * DIM_INNER)), 'b1': jnp.zeros((DEPTH, 2 * DIM_INNER), jnp.float32), 'W2': init(ks[4], (DEPTH, DIM_INNER, DIM)), 'b2': jnp.zeros((DEPTH, DIM), jnp.float32)}
    _L0_ffn_in = _L0_ffn_setup()
    _d = {'L0_attn_x': _L0_attn_in['x'], 'L0_attn_qkv_w': _L0_attn_in['qkv_w'], 'L0_attn_qkv_b': _L0_attn_in['qkv_b'], 'L0_attn_out_w': _L0_attn_in['out_w'], 'L0_attn_out_b': _L0_attn_in['out_b'], 'L0_ffn_Wqkv': _L0_ffn_in['Wqkv'], 'L0_ffn_q_scale': _L0_ffn_in['q_scale'], 'L0_ffn_k_scale': _L0_ffn_in['k_scale'], 'L0_ffn_Wo': _L0_ffn_in['Wo'], 'L0_ffn_ln_g': _L0_ffn_in['ln_g'], 'L0_ffn_ln_b': _L0_ffn_in['ln_b'], 'L0_ffn_W1': _L0_ffn_in['W1'], 'L0_ffn_b1': _L0_ffn_in['b1'], 'L0_ffn_W2': _L0_ffn_in['W2'], 'L0_ffn_b2': _L0_ffn_in['b2']}
    _x0 = _d['L0_attn_x']
    _d['L0_attn_x'] = jax.random.normal(jax.random.fold_in(jax.random.key(seed), 1), (2, 1024, 128), dtype=_x0.dtype)
    del _x0
    return _d

def reference(L0_attn_x, L0_attn_qkv_w, L0_attn_qkv_b, L0_attn_out_w, L0_attn_out_b, L0_ffn_Wqkv, L0_ffn_q_scale, L0_ffn_k_scale, L0_ffn_Wo, L0_ffn_ln_g, L0_ffn_ln_b, L0_ffn_W1, L0_ffn_b1, L0_ffn_W2, L0_ffn_b2):

    def _L0_attn_ref(x, qkv_w, qkv_b, out_w, out_b):
        import jax, jax.numpy as jnp
        import numpy as np
        EMBED_DIM = 128
        HEADS = 16
        HEAD_DIM = EMBED_DIM // HEADS
        TOP_K_RATIO = 0.7
        NEG_FILL = -10000.0
        B, T, E = x.shape
        H, D = (HEADS, HEAD_DIM)
        k_top = max(1, int(TOP_K_RATIO * T))
        qkv = x @ qkv_w.T + qkv_b
        q, k, v = jnp.split(qkv, 3, axis=-1)
        split = lambda t: t.reshape(B, T, H, D).transpose(0, 2, 1, 3)
        q, k, v = (split(q), split(k), split(v))
        scores = jnp.einsum('bhqd,bhkd->bhqk', q, k) * D ** (-0.5)
        topk_vals, topk_idx = jax.lax.top_k(scores, k_top)
        sparse = jnp.full_like(scores, NEG_FILL)
        bi = jnp.arange(B)[:, None, None, None]
        hi = jnp.arange(H)[None, :, None, None]
        ti = jnp.arange(T)[None, None, :, None]
        sparse = sparse.at[bi, hi, ti, topk_idx].set(topk_vals)
        attn = jax.nn.softmax(sparse, axis=-1)
        ctx = jnp.einsum('bhqk,bhkd->bhqd', attn, v)
        ctx = ctx.transpose(0, 2, 1, 3).reshape(B, T, E)
        return ctx @ out_w.T + out_b

    def _L0_ffn_ref(x, Wqkv, q_scale, k_scale, Wo, ln_g, ln_b, W1, b1, W2, b2):
        import jax, jax.numpy as jnp
        import numpy as np
        DIM = 128
        DEPTH = 6
        HEADS = 16
        DIM_HEAD = 64
        WINDOW = 32
        INNER = HEADS * DIM_HEAD
        DIM_INNER = int(DIM * 4 * 2 / 3)
        QK_SCALE = 8.0

        def shift_tokens(t):
            a, s = jnp.split(t, 2, -1)
            s = jnp.pad(s, ((0, 0), (1, 0), (0, 0)))[:, :-1]
            return jnp.concatenate([a, s], -1)

        def l2norm(t):
            return t / jnp.maximum(jnp.linalg.norm(t, axis=-1, keepdims=True), 1e-12)

        def rotate_half(x):
            x1, x2 = jnp.split(x, 2, -1)
            return jnp.concatenate([-x2, x1], -1)

        def rotary_tables(n):
            half = jnp.arange(0, DIM_HEAD, 2, dtype=jnp.float32)
            inv_freq = 1.0 / 10000.0 ** (half / DIM_HEAD)
            t = jnp.arange(n, dtype=jnp.float32)
            freqs = t[:, None] * inv_freq[None, :]
            freqs = jnp.concatenate([freqs, freqs], -1)
            base_scale = (half + 0.4 * DIM_HEAD) / (1.4 * DIM_HEAD)
            power = (t - n // 2) / (WINDOW // 2)
            scale = base_scale[None, :] ** power[:, None]
            scale = jnp.concatenate([scale, scale], -1)
            return (freqs, scale)

        def local_attention(q, k, v):
            b, h, n, d = q.shape
            w = WINDOW
            nw = n // w
            bq = q.reshape(b, h, nw, w, d)
            bk = k.reshape(b, h, nw, w, d)
            bv = v.reshape(b, h, nw, w, d)

            def look(t):
                p = jnp.pad(t, ((0, 0), (0, 0), (1, 0), (0, 0), (0, 0)))
                return jnp.concatenate([p[:, :, :nw], p[:, :, 1:]], axis=3)
            bk2, bv2 = (look(bk), look(bv))
            seq = jnp.arange(n).reshape(nw, w)
            seq_p = jnp.pad(seq, ((1, 0), (0, 0)), constant_values=-1)
            jt = jnp.concatenate([seq_p[:nw], seq_p[1:]], axis=1)
            it = seq[:, :, None]
            jb = jt[:, None, :]
            mask = (it < jb) | (it > jb + w) | (jb == -1)
            sim = jnp.einsum('bhwie,bhwje->bhwij', bq, bk2) * QK_SCALE
            sim = jnp.where(mask, -jnp.finfo(sim.dtype).max, sim)
            attn = jax.nn.softmax(sim, -1)
            out = jnp.einsum('bhwij,bhwje->bhwie', attn, bv2)
            return out.reshape(b, h, n, d)

        def attn_layer(x, Wqkv, qs, ksc, Wo):
            b, n, _ = x.shape
            qkv = x @ Wqkv
            q, k, v = jnp.split(qkv, 3, -1)
            sh = lambda t: t.reshape(b, n, HEADS, DIM_HEAD).transpose(0, 2, 1, 3)
            q, k, v = (sh(q), sh(k), sh(v))
            q = l2norm(q) * qs
            k = l2norm(k) * ksc
            freqs, scale = rotary_tables(n)
            cos, sin = (jnp.cos(freqs), jnp.sin(freqs))
            q = q * cos * scale + rotate_half(q) * sin * scale
            inv = 1.0 / scale
            k = k * cos * inv + rotate_half(k) * sin * inv
            out = local_attention(q, k, v)
            out = out.transpose(0, 2, 1, 3).reshape(b, n, INNER)
            return out @ Wo

        def ffn_layer(x, g, bln, W1, b1, W2, b2):
            mu = x.mean(-1, keepdims=True)
            var = ((x - mu) ** 2).mean(-1, keepdims=True)
            xn = (x - mu) / jnp.sqrt(var + 1e-05) * g + bln
            hg = xn @ W1 + b1
            a, gate = jnp.split(hg, 2, -1)
            return a * jax.nn.gelu(gate, approximate=False) @ W2 + b2
        for i in range(DEPTH):
            x = attn_layer(shift_tokens(x), Wqkv[i], q_scale[i], k_scale[i], Wo[i]) + x
            x = ffn_layer(shift_tokens(x), ln_g[i], ln_b[i], W1[i], b1[i], W2[i], b2[i]) + x
        return x
    x = L0_attn_x
    xn = _layernorm(x, axis=-1)
    x = x + _L0_attn_ref(xn, L0_attn_qkv_w, L0_attn_qkv_b, L0_attn_out_w, L0_attn_out_b) + _L0_ffn_ref(xn, L0_ffn_Wqkv, L0_ffn_q_scale, L0_ffn_k_scale, L0_ffn_Wo, L0_ffn_ln_g, L0_ffn_ln_b, L0_ffn_W1, L0_ffn_b1, L0_ffn_W2, L0_ffn_b2)
    return x

_drawn_inputs = setup_inputs


def setup_inputs(seed=0):
    import zlib

    import numpy as np

    out = dict(_drawn_inputs(seed))
    spreads = {'L0_ffn_q_scale': (1.0, 0.6),
     'L0_ffn_k_scale': (1.0, 0.6),
     'L0_ffn_ln_g': (1.0, 0.6),
     'L0_ffn_ln_b': (0.0, 0.8),
     'L0_ffn_b1': (0.0, 0.8),
     'L0_ffn_b2': (0.0, 0.1)}
    factors = {'L0_attn_qkv_w': 3.864,
     'L0_attn_qkv_b': 3.338,
     'L0_ffn_W1': 3.643,
     'L0_ffn_W2': 3.576,
     'L0_attn_out_b': 6.671}
    for name, (base, spread) in spreads.items():
        noise = np.random.default_rng([zlib.crc32(name.encode()), seed]).standard_normal(out[name].shape)
        drawn = base * np.exp(spread * noise) if base else spread * noise
        out[name] = jnp.asarray(drawn.astype(out[name].dtype))
    for name, factor in factors.items():
        out[name] = (out[name] * factor).astype(out[name].dtype)
    return out
```

```python
from contextlib import ExitStack

import concourse.bass as bass
from concourse import mybir

F32 = mybir.dt.float32
BF16 = mybir.dt.bfloat16
I32 = mybir.dt.int32
ALU = mybir.AluOpType
ACT = mybir.ActivationFunctionType
AX = mybir.AxisListType
ds = bass.ds

P = 128
BANK = 512
EPS = 1e-5

B, T = 2, 1024
TOK = B * T
TILES = TOK // P
HEADS, HD = 16, 8
K_TOP = int(0.7 * T)
FILL = -10000.0
GROUPS = B * HEADS
QT = T // P
HALF = QT // 2
KBLK = T // P
UNITS = GROUPS * QT
SC = 2.0 ** -40
EXP_SCALE = HD ** -0.5 / SC
Z = -0.5221
DENSITY = 0.3481
WINDOW = 8
SQRT_BITS = float(0x1fbd1df5)
NEXT_UP = 2.0 ** -24 * 1.0001


class Steps:

    def __init__(self, eng, sem, base=0):
        self.eng, self.sem, self.base, self.n = eng, sem, base, 0

    def did(self, ins):
        self.n += 1
        ins.then_inc(self.sem, 1)

    def wait(self):
        self.eng.wait_ge(self.sem, self.base + self.n)


def front(nc, ctx, A, M):
    sb = lambda n, s, d=F32: ctx.enter_context(nc.sbuf_tensor(n, s, d))
    sem = lambda n: ctx.enter_context(nc.semaphore(n))
    ps = M["ps"]
    with ExitStack() as own:
        osb = lambda n, s, d=F32: own.enter_context(nc.sbuf_tensor(n, s, d))
        x0 = osb("x0", [P, TOK])
        xc = osb("xc", [P, TOK])
        sq = osb("sq", [P, TOK])
        xn = osb("xn", [P, TOK])
        w = osb("w_qkv_a", [P, 3 * P])
        bq = osb("bq", [P, 1])
        bk = osb("bk", [P, 1])
        bqs = osb("bqs", [P, 1])
        bv = osb("bv", [P, P])
        s_ld = sem("front_loads")
        s_set = sem("front_constants")
        s_mean = sem("front_mean")
        s_xc = sem("front_centred")
        s_sq = sem("front_squared")
        s_var = sem("front_var")
        s_sd = sem("front_sd")
        s_rs = sem("front_rstd")
        s_xn = sem("front_normed")
        s_qk = sem("front_qk")
        s_qke = sem("front_qk_out")
        s_v = sem("front_v")
        s_ve = sem("front_v_out")
        s_end = sem("front_credits")
        G = TOK // BANK
        col = lambda t, g: t[:, BANK * g:BANK * (g + 1)]
        bank = lambda b: ps[:, BANK * b:BANK * (b + 1)]
        with nc.Block() as block:

            @block.sync
            def _(sp):
                loads = [(x0, A["x_t"]), (w, A["a_w"]), (bq, A["a_bq"]), (bk, A["a_bk"]), (bv, A["a_bv"]),
                         (M["hmask"], A["c_hmask"]), (M["ident"], A["c_ident"]), (M["iota8"], A["c_iota8"])]
                for t, a in loads:
                    sp.dma_start(t[:], a).then_inc(s_ld, 16)
                for name in ("pt_out", "pv_done", "ctx_out"):
                    sp.sem_inc(M[name], 2)
                sp.wait_ge(s_ld, 16 * len(loads))
                sp.nop().then_inc(s_end, 1)

            @block.vector
            def _(dve):
                nc.vector.memset(M["mean_w"][:], 1.0 / P).then_inc(s_set, 1)
                nc.vector.memset(M["eps"][:], EPS).then_inc(s_set, 1)
                nc.vector.memset(M["xa"][:], 0.0).then_inc(s_set, 1)
                nc.vector.memset(M["vh"][:], 1.0).then_inc(s_set, 1)
                nc.vector.memset(M["flags"][:], 0.0).then_inc(s_set, 1)
                dve.wait_ge(s_end, 1)
                nc.vector.tensor_scalar(bqs[:], bq[:], SC, None, ALU.mult).then_inc(s_set, 1)
                for g in range(G):
                    dve.wait_ge(s_mean, g + 1)
                    nc.vector.tensor_tensor(col(xc, g), col(x0, g), bank(g), ALU.subtract).then_inc(s_xc, 1)
                for g in range(G):
                    dve.wait_ge(s_sd, g + 1)
                    nc.vector.reciprocal(col(sq, g), col(sq, g)).then_inc(s_rs, 1)
                    dve.wait_ge(s_rs, g + 1)
                    nc.vector.tensor_tensor(col(xn, g), col(xc, g), col(sq, g), ALU.mult).then_inc(s_xn, 1)
                for g in range(G):
                    dve.wait_ge(s_v, 4 * g + 4)
                    nc.vector.tensor_tensor(
                        M["v"][:, 4 * g:4 * g + 4, :], bank(g).rearrange("p (t f) -> p t f", t=4),
                        bv[:].unsqueeze(1).to_broadcast([P, 4, P]), ALU.add).then_inc(s_ve, 1)

            @block.tensor
            def _(pe):
                pe.wait_ge(s_end, 1)
                pe.wait_ge(s_set, 1)
                for g in range(G):
                    nc.tensor.matmul(bank(g), M["mean_w"][:], col(x0, g), start=True, stop=True).then_inc(s_mean, 1)
                for g in range(G):
                    pe.wait_ge(s_sq, g + 1)
                    nc.tensor.matmul(bank(4 + g), M["mean_w"][:], col(sq, g), start=True, stop=True).then_inc(s_var, 1)
                for g in range(G):
                    pe.wait_ge(s_xn, g + 1)
                    nc.tensor.matmul(bank(g), w[:, 0:P], col(xn, g), start=True, stop=True).then_inc(s_qk, 1)
                    nc.tensor.matmul(bank(4 + g), w[:, P:2 * P], col(xn, g), start=True, stop=True).then_inc(s_qk, 1)
                for t in range(TILES):
                    if t % 4 == 0:
                        pe.wait_ge(s_qke, 2 * (t // 4) + 2)
                    nc.tensor.matmul(ps[:, P * t:P * (t + 1)], xn[:, P * t:P * (t + 1)], w[:, 2 * P:3 * P],
                                     start=True, stop=True).then_inc(s_v, 1)

            @block.scalar
            def _(act):
                act.wait_ge(s_set, 6)
                for g in range(G):
                    act.wait_ge(s_xc, g + 1)
                    nc.scalar.activation(col(sq, g), col(xc, g), ACT.Square).then_inc(s_sq, 1)
                for g in range(G):
                    act.wait_ge(s_var, g + 1)
                    nc.scalar.activation(col(sq, g), bank(4 + g), ACT.Sqrt, bias=M["eps"][:]).then_inc(s_sd, 1)
                for g in range(G):
                    act.wait_ge(s_qk, 2 * g + 2)
                    nc.scalar.activation(col(M["q_t"], g), bank(g), ACT.Identity, bias=bqs[:], scale=SC).then_inc(s_qke, 1)
                    nc.scalar.activation(col(M["k_t"], g), bank(4 + g), ACT.Identity, bias=bk[:]).then_inc(s_qke, 1)

            @block.gpsimd
            def _(pool):
                for g in range(G):
                    pool.wait_ge(s_xn, g + 1)
                    if g == 0:
                        pool.wait_ge(s_set, 3)
                    b, at = g * BANK // T, g * BANK % T
                    nc.gpsimd.tensor_copy(M["xa"][:, b, 1 + at:1 + at + BANK], col(xn, g))


def topk_attention(nc, ctx, M):
    ps = M["ps"]
    sem = lambda n: ctx.enter_context(nc.semaphore(n))
    s_qm = sem("qm_ready")
    s_vh = sem("vh_ready")
    s_sc = sem("scores_ready")
    s_ev = sem("scores_in_sbuf")
    s_nt = sem("threshold_ready")
    s_ct = sem("count_ready")
    s_mx = sem("exp_bias_ready")
    s_ex = sem("exp_ready")
    s_p = sem("probs_ready")
    s_pt = sem("probs_t_ready")
    s_h = sem("dve_head_steps")
    s_t = sem("dve_tail_steps")
    s_c = sem("dve_context_steps")
    s_pe, s_pv, s_cx = (M[n] for n in ("pt_out", "pv_done", "ctx_out"))
    with ExitStack() as own:
        sb = lambda n, s, d=F32: own.enter_context(nc.sbuf_tensor(n, s, d))
        S = sb("scores", [P, 2, QT, T])
        E = sb("exps", [P, QT, T])
        U = sb("signed", [P, 2, T])
        Y = sb("pushed", [P, 2, T])
        PT = sb("probs_t", [P, 2, KBLK, P])
        junk_a = sb("junk_act", [P, QT, T], BF16)
        junk_d = Y[:].bitcast(BF16).rearrange("p a (b t) -> p (a b) t", b=2)
        qm = sb("q_masked", [P, 2, T])
        st = lambda n: sb(n, [P, 2, QT])
        tot, cnt, mx, nb = (st(n) for n in ("row_sum", "count", "row_max", "exp_bias"))
        pt = sb("points", [P, 2, 4, 2, QT])
        step, diff, diff2 = (sb(n, [P, 2, QT]) for n in ("step", "diff", "diff_far"))
        sig, tmp = sb("sigma", [P, QT]), sb("tmp", [P, QT])
        cross = sb("crossed", [P, 2, QT], I32)
        side, sgn, x, nud, idx, idx2 = (st(n) for n in ("side", "sgn", "signed_thr", "nudged", "idx", "idx_next"))
        thr, num, kth, nxt, bad, tmp2 = (st(n) for n in ("thr", "exact_num", "kth", "next_value", "bad", "off"))
        bn = sb("bn", [P, 2, QT, 6])
        top8 = sb("top8", [P, QT, 8])
        hit = sb("hit", [P, HALF, 8])
        pick = sb("pick", [P, HALF, 8])
        rden = sb("rden", [P, 2, HALF])

        def sl(xy):
            return slice(HALF * xy, HALF * (xy + 1))

        def scores(pe, n, g):
            b = n // HEADS
            pe.wait_ge(s_qm, n + 1)
            for j in range(QT):
                if not (isinstance(n, int) and 8 * n + j < 2):
                    pe.wait_ge(s_ev, QT * n + j - 1)
                for h in range(2):
                    mm = nc.tensor.matmul(ps[:, BANK * (2 * (j % 2) + h):BANK * (2 * (j % 2) + h + 1)],
                                          qm[:, g, P * j:P * (j + 1)],
                                          M["k_t"][:, ds(b * T + BANK * h, BANK)], start=True, stop=True)
                mm.then_inc(s_sc, 1)

        def probs_t(pe, n, j):
            pe.wait_ge(s_p, QT * n + j + 1)
            for h in range(2):
                pe.wait_ge(s_pe, 2 * QT * n + 2 * j + h + 1)
                for c in range(4):
                    mm = nc.tensor.transpose(ps[:, BANK * (4 + h) + P * c:BANK * (4 + h) + P * (c + 1)],
                                             E[:, j, P * (4 * h + c):P * (4 * h + c + 1)], M["ident"][:])
                mm.then_inc(s_pt, 1)

        def pv(pe, n, g, j):
            if j == 0:
                pe.wait_ge(s_vh, n + 1)
            if j % HALF == 0:
                pe.wait_ge(s_cx, 2 * n + j // HALF + 1)
            pe.wait_ge(s_pe, 2 * QT * n + 2 * j + 4)
            o = BANK * (6 + j // HALF) + 16 * (j % HALF)
            for c in range(KBLK):
                mm = nc.tensor.matmul(ps[:, o:o + HD + 1], PT[:, j % 2, c, :], M["vh"][:, g, c, :],
                                      start=(c == 0), stop=(c == KBLK - 1))
            mm.then_inc(s_pv, 1)

        def pe_tail(pe, n, g):
            probs_t(pe, n, 0)
            for j in range(QT):
                if j + 1 < QT:
                    probs_t(pe, n, j + 1)
                pv(pe, n, g, j)

        def evacuate(act, n, g, xy):
            for j in range(HALF * xy, HALF * (xy + 1)):
                act.wait_ge(s_sc, QT * n + j + 1)
                nc.scalar.activation(S[:, g, j, :], ps[:, 2 * BANK * (j % 2):2 * BANK * (j % 2 + 1)], ACT.Identity,
                                     accum_out=tot[:, g, j:j + 1]).then_inc(s_ev, 1)

        def count(act, n, g, k):
            act.wait_ge(s_nt, 4 * n + k + 1)
            if not (isinstance(n, int) and n + k == 0):
                act.wait_ge(s_ct, 3 * n + k)
            for j in range(QT):
                ins = nc.scalar.activation(junk_a[:, j, :], S[:, g, j, :], ACT.Sign, bias=pt[:, g, k, 0, j:j + 1],
                                           accum_out=cnt[:, g, j:j + 1])
            ins.then_inc(s_ct, 1)

        def exps(act, n, g, xy):
            act.wait_ge(s_mx, n + 1)
            for j in range(HALF * xy, HALF * (xy + 1)):
                ins = nc.scalar.activation(E[:, j, :], S[:, g, j, :], ACT.Exp, bias=nb[:, g, j:j + 1], scale=EXP_SCALE)
            ins.then_inc(s_ex, 1)

        def evacuate_t(act, n, g, xy):
            for j in range(HALF * xy, HALF * (xy + 1)):
                act.wait_ge(s_pv, QT * n + j + 1)
                for h in range(2):
                    act.wait_ge(s_pt, 2 * QT * n + 2 * j + h + 1)
                    nc.scalar.activation(PT[:, j % 2, 4 * h:4 * h + 4, :], ps[:, BANK * (4 + h):BANK * (5 + h)],
                                         ACT.Identity).then_inc(s_pe, 1)

        def act_period(act, n1, g1, n, g):
            H = lambda f, *a: f(act, n1, g1, *a) if n1 is not None else None
            L = lambda f, *a: f(act, n, g, *a) if n is not None else None
            H(evacuate, 0)
            H(evacuate, 1)
            L(exps, 0)
            H(count, 0)
            L(exps, 1)
            H(count, 1)
            L(evacuate_t, 0)
            H(count, 2)
            L(evacuate_t, 1)

        V = nc.vector

        def first_threshold(dve, own_, n, g):
            for j in range(QT):
                dve.wait_ge(s_ev, QT * n + j + 1)
                ins = V.bn_stats(bn[:, g, j, :], S[:, g, j, 0:BANK])
            own_.did(ins)
            own_.wait()
            own_.did(V.tensor_tensor(sig[:], bn[:, g, :, 2], bn[:, g, :, 5], ALU.add))
            own_.wait()
            own_.did(V.tensor_scalar(sig[:].bitcast(I32), sig[:].bitcast(I32), 0.5,
                                     SQRT_BITS - 4.5 * 2 ** 23, ALU.mult, ALU.add))
            own_.wait()
            own_.did(V.tensor_scalar(tmp[:], sig[:], -Z, None, ALU.mult))
            own_.did(V.tensor_scalar(step[:, 0, :], sig[:], 1.0 / (2 * T * DENSITY), None, ALU.mult))
            own_.did(V.memset(step[:, 1, :], 1.0))
            own_.wait()
            V.scalar_tensor_tensor(out=pt[:, g, 0, 0, :], in0=tot[:, g, :], scalar=-1.0 / T, in1=tmp[:],
                                   op0=ALU.mult, op1=ALU.add).then_inc(s_nt, 1)

        def next_threshold(dve, own_, n, g, k):
            new, old = pt[:, g, k], pt[:, g, max(k - 1, 0)]
            dve.wait_ge(s_ct, 3 * n + k + 1)
            own_.did(V.tensor_scalar(pt[:, g, k, 1, :], cnt[:, g, :], float(T - 2 * K_TOP), None, ALU.add))
            own_.wait()
            if k > 0:
                own_.did(V.tensor_tensor(diff[:], new, old, ALU.subtract))
                own_.did(V.tensor_tensor(tmp[:], new[:, 1, :], old[:, 1, :], ALU.mult))
                own_.wait()
                own_.did(V.tensor_scalar(cross[:, k - 1, :], tmp[:], 0.0, None, ALU.is_lt))
                crossed = lambda c: cross[:, c, :].unsqueeze(1).to_broadcast([P, 2, QT])
                if k == 2:
                    own_.did(V.tensor_tensor(diff2[:], diff[:], step[:], ALU.add))
                    own_.wait()
                    dve.sem_inc(M["passed"], 1)
                    own_.did(V.copy_predicated(step[:], crossed(0), diff2[:]))
                own_.wait()
                dve.sem_inc(M["passed"], 1)
                own_.did(V.copy_predicated(step[:], crossed(k - 1), diff[:]))
                own_.wait()
            own_.did(V.reciprocal(tmp[:], step[:, 1, :]))
            own_.wait()
            own_.did(V.tensor_tensor(tmp[:], tmp[:], step[:, 0, :], ALU.mult))
            own_.wait()
            own_.did(V.tensor_tensor(tmp[:], tmp[:], pt[:, g, k, 1, :], ALU.mult))
            own_.wait()
            V.tensor_tensor(pt[:, g, k + 1, 0, :], pt[:, g, k, 0, :], tmp[:], ALU.subtract).then_inc(s_nt, 1)

        def row_max(dve, own_, n, g):
            for j in range(QT):
                ins = V.tensor_reduce(mx[:, g, j:j + 1], S[:, g, j, :], AX.X, ALU.max)
            own_.did(ins)
            own_.wait()
            V.tensor_scalar(nb[:, g, :], mx[:, g, :], -EXP_SCALE, None, ALU.mult).then_inc(s_mx, 1)

        def exact_count(dve, own_, n, g, xy):
            c = sl(xy)
            dve.wait_ge(s_nt, 4 * n + 4)
            own_.did(V.tensor_scalar(thr[:, g, c], pt[:, g, 3, 0, c], -1.0, None, ALU.mult))
            own_.wait()
            for j in range(HALF * xy, HALF * (xy + 1)):
                ins = V.tensor_scalar(junk_d[:, j % HALF, :], S[:, g, j, :], thr[:, g, j:j + 1], None, ALU.is_ge, ALU.add,
                                      accum_out=num[:, g, j:j + 1])
            own_.did(ins)
            own_.wait()
            own_.did(V.tensor_scalar(side[:, g, c], num[:, g, c], K_TOP - 0.5, None, ALU.is_ge))
            own_.wait()
            own_.did(V.tensor_scalar(sgn[:, g, c], side[:, g, c], -2.0, 1.0, ALU.mult, ALU.add))
            own_.wait()
            own_.did(V.tensor_tensor(x[:, g, c], sgn[:, g, c], thr[:, g, c], ALU.mult))
            own_.did(V.scalar_tensor_tensor(out=idx[:, g, c], in0=num[:, g, c], scalar=K_TOP - 0.5, in1=sgn[:, g, c],
                                            op0=ALU.subtract, op1=ALU.mult))
            own_.wait()
            own_.did(V.scalar_tensor_tensor(out=nud[:, g, c], in0=x[:, g, c], scalar=-1.0, in1=x[:, g, c],
                                            op0=ALU.mult, op1=ALU.max))
            own_.did(V.tensor_scalar(idx[:, g, c], idx[:, g, c], -1.0, -0.5, ALU.mult, ALU.add))
            own_.wait()
            own_.did(V.scalar_tensor_tensor(out=nud[:, g, c], in0=nud[:, g, c], scalar=NEXT_UP, in1=side[:, g, c],
                                            op0=ALU.mult, op1=ALU.mult))
            own_.did(V.tensor_tensor(idx2[:, g, c], idx[:, g, c], sgn[:, g, c], ALU.add))
            own_.wait()
            own_.did(V.tensor_tensor(nud[:, g, c], nud[:, g, c], x[:, g, c], ALU.add))
            own_.wait()

        def near_values(dve, own_, n, g, xy, pair):
            def signed(j):
                own_.did(V.tensor_scalar(U[:, j % 2, :], S[:, g, j, :], sgn[:, g, j:j + 1], None, ALU.mult))

            def pushed(j):
                own_.did(V.scalar_tensor_tensor(out=Y[:, j % 2, :], in0=U[:, j % 2, :], scalar=nud[:, g, j:j + 1],
                                                in1=U[:, j % 2, :], op0=ALU.is_ge, op1=ALU.subtract, reverse1=True))

            def largest(j):
                own_.did(V.max(top8[:, j, :], Y[:, j % 2, :]))

            j = HALF * xy
            if pair == 0:
                signed(j)
                signed(j + 1)
                own_.wait()
                pushed(j)
                pushed(j + 1)
                own_.wait()
                signed(j + 2)
                signed(j + 3)
                largest(j)
                largest(j + 1)
            else:
                own_.wait()
                pushed(j + 2)
                pushed(j + 3)
                own_.wait()
                own_.did(hits(g, xy, idx))
                largest(j + 2)
                largest(j + 3)

        def hits(g, xy, at):
            return V.tensor_tensor(hit[:], M["iota8"][:].unsqueeze(1).to_broadcast([P, HALF, 8]),
                                   at[:, g, sl(xy)].unsqueeze(2).to_broadcast([P, HALF, 8]), ALU.is_equal)

        def take(own_, g, xy, out):
            c = sl(xy)
            own_.did(V.tensor_tensor(pick[:], hit[:], top8[:, c, :], ALU.mult))
            own_.wait()
            own_.did(V.tensor_reduce(out[:, g, c], pick[:], AX.X, ALU.add))
            own_.wait()

        def select(dve, own_, n, g, xy):
            c = sl(xy)
            own_.wait()
            take(own_, g, xy, kth)
            own_.did(V.tensor_tensor(thr[:, g, c], kth[:, g, c], sgn[:, g, c], ALU.mult))
            own_.did(hits(g, xy, idx2))
            own_.wait()
            take(own_, g, xy, nxt)
            own_.did(V.tensor_tensor(bad[:, g, c], kth[:, g, c], nxt[:, g, c], ALU.is_equal))
            own_.did(V.tensor_tensor(tmp2[:, g, c], idx[:, g, c], side[:, g, c], ALU.subtract))
            own_.wait()
            for value, bound, op in ((tmp2, WINDOW - 1.5, ALU.is_gt),
                                     (mx, 2.0 ** -13, ALU.is_gt),
                                     (mx, 0.9 * FILL / EXP_SCALE, ALU.is_lt),
                                     (tot, -(2.0 ** -2), ALU.is_lt)):
                own_.did(V.scalar_tensor_tensor(out=bad[:, g, c], in0=value[:, g, c], scalar=bound, in1=bad[:, g, c],
                                                op0=op, op1=ALU.add))
                own_.wait()
            own_.did(V.scalar_tensor_tensor(out=M["flags"][:, ds(QT * n + HALF * xy, HALF)], in0=x[:, g, c],
                                            scalar=0.0, in1=bad[:, g, c], op0=ALU.is_equal, op1=ALU.add))

        def probs(dve, own_, n, g, xy):
            dve.wait_ge(s_ex, 2 * n + xy + 1)
            for j in range(HALF * xy, HALF * (xy + 1)):
                V.scalar_tensor_tensor(out=E[:, j, :], in0=S[:, g, j, :], scalar=thr[:, g, j:j + 1], in1=E[:, j, :],
                                       op0=ALU.is_ge, op1=ALU.mult).then_inc(s_p, 1)

        def context(dve, own_, n, g, xy):
            b, h = n // HEADS, n % HEADS
            dve.wait_ge(s_pv, 2 + QT * n + HALF * (xy + 1))
            out = ps[:, BANK * (6 + xy):BANK * (6 + xy) + 16 * HALF].rearrange("p (j e) -> p j e", j=HALF)
            own_.did(V.tensor_scalar(rden[:, xy, :], out[:, :, HD], 1e-30, None, ALU.max))
            own_.wait()
            own_.did(V.reciprocal(rden[:, xy, :], rden[:, xy, :]))
            own_.wait()
            V.tensor_tensor(M["ctx"][:, ds(b * QT + HALF * xy, HALF), ds(h * HD, HD)], out[:, :, 0:HD],
                            rden[:, xy, :].unsqueeze(2).to_broadcast([P, HALF, HD]), ALU.mult).then_inc(s_cx, 1)

        HEAD_STEPS = 6 + 4 + 8 + 10 + 1
        TAIL_STEPS = 2 * (11 + 3 * HALF + 14)

        def dve_period(dve, n1, g1, n, g, before, gb):
            head = Steps(dve, s_h, HEAD_STEPS * n1) if n1 is not None else None
            tail = Steps(dve, s_t, TAIL_STEPS * n) if n is not None else None
            late = Steps(dve, s_c, 4 * before) if before is not None else None
            H = lambda f, *a: f(dve, head, n1, g1, *a) if n1 is not None else None
            L = lambda f, *a: f(dve, tail, n, g, *a) if n is not None else None
            L(exact_count, 0)
            H(first_threshold)
            L(near_values, 0, 0)
            L(near_values, 0, 1)
            H(next_threshold, 0)
            L(select, 0)
            L(probs, 0)
            if before is not None:
                context(dve, late, before, gb, 0)
                context(dve, late, before, gb, 1)
            L(exact_count, 1)
            H(next_threshold, 1)
            L(near_values, 1, 0)
            L(near_values, 1, 1)
            L(select, 1)
            L(probs, 1)
            H(next_threshold, 2)
            H(row_max)
            assert head is None or head.n == HEAD_STEPS
            assert tail is None or tail.n == TAIL_STEPS

        with nc.Block() as block:

            @block.gpsimd
            def _(pool):
                def operands(n, g):
                    b, h = n // HEADS, n % HEADS
                    if not isinstance(n, int):
                        pool.wait_ge(s_sc, QT * n - QT)
                    nc.gpsimd.tensor_tensor(qm[:, g, :], M["q_t"][:, ds(b * T, T)],
                                            M["hmask"][:, ds(h, 1)].to_broadcast([P, T]),
                                            ALU.mult).then_inc(s_qm, 1)
                    if not isinstance(n, int):
                        pool.wait_ge(s_pv, QT * n - QT + 2)
                    nc.gpsimd.tensor_copy(M["vh"][:, g, :, 0:HD],
                                          M["v"][:, ds(b * QT, QT), ds(h * HD, HD)]).then_inc(s_vh, 1)

                operands(0, 0)
                operands(1, 1)
                with pool.Fori(1, GROUPS // 2) as i:
                    operands(2 * i, 0)
                    operands(2 * i + 1, 1)

            def periods(eng, Fori, period):
                period(0, 0, None, None, None, None)
                period(1, 1, 0, 0, None, None)
                with Fori(0, GROUPS // 2 - 1) as i:
                    period(2 * i + 2, 0, 2 * i + 1, 1, 2 * i, 0)
                    period(2 * i + 3, 1, 2 * i + 2, 0, 2 * i + 1, 1)
                period(None, None, GROUPS - 1, 1, GROUPS - 2, 0)

            @block.tensor
            def _(pe):
                def period(n1, g1, n, g, before, gb):
                    if n1 is not None:
                        scores(pe, n1, g1)
                    if n is not None:
                        pe_tail(pe, n, g)
                periods(pe, pe.Fori, period)

            @block.scalar
            def _(act):
                periods(act, act.Fori, lambda n1, g1, n, g, before, gb: act_period(act, n1, g1, n, g))

            @block.vector
            def _(dve):
                periods(dve, dve.Fori, lambda *a: dve_period(dve, *a))
                late = Steps(dve, s_c, 4 * (GROUPS - 1))
                context(dve, late, GROUPS - 1, 1, 0)
                context(dve, late, GROUPS - 1, 1, 1)


def repair(nc, M):
    ps = M["ps"]
    V = nc.vector
    DROP = T - K_TOP
    ROUNDS, AT = DROP // 8, DROP % 8
    FILL_SC = FILL / EXP_SCALE
    with ExitStack() as own:
        sb = lambda n, s, d=F32: own.enter_context(nc.sbuf_tensor(n, s, d))
        sem = lambda n: own.enter_context(nc.semaphore(n))
        marks, marked = sb("unit_marks", [1, UNITS], I32), sb("any_mark", [1, 1], I32)
        marks_f, marked_f = sb("unit_marks_f", [1, UNITS]), sb("any_mark_f", [1, 1])
        before, before_f = sb("marks_before", [1, UNITS], I32), sb("marks_before_f", [1, UNITS])
        qr, vr = sb("q_unit", [P, P]), sb("v_unit", [P, KBLK, HD + 1])
        S, W, X, E = (sb(n, [P, T]) for n in ("r_scores", "r_left", "r_sparse", "r_exps"))
        ones, rank, keep = (sb(n, [P, T]) for n in ("r_ones", "r_rank", "r_keep"))
        pt = sb("r_probs_t", [P, KBLK, P])
        t8 = sb("r_top8", [P, 8])
        thr, above, room, m, nb, rden = (sb(n, [P, 1]) for n in ("r_thr", "r_above", "r_room", "r_max", "r_bias", "r_den"))
        s_n = sem("marks_summed")
        s_m = sem("marks_ready")
        s_op = sem("r_operands")
        s_sc = sem("r_scores_ready")
        s_x = sem("r_sparse_ready")
        s_e = sem("r_exps_ready")
        s_t = sem("r_turned")
        s_te = sem("r_turned_out")
        s_pv = sem("r_products")
        s_d = sem("r_dve_steps")
        s_done = sem("r_unit_done")
        DVE_STEPS = 2 + 2 * ROUNDS + 12

        def units(eng, work):
            eng.wait_ge(s_m, 8)
            some = eng.value_load(marked[0:1, 0:1], min_val=0, max_val=1)
            with eng.If(some > 0):
                with eng.Fori(0, UNITS) as u:
                    mark = eng.value_load(marks[0:1, ds(u, 1)], min_val=0, max_val=1)
                    with eng.If(mark > 0):
                        work(u, eng.value_load(before[0:1, ds(u, 1)], min_val=0, max_val=UNITS - 1))
                    with eng.Else():
                        eng.sem_inc(M["passed"], 1)
                    eng.sem_inc(M["passed"], 1)
            with eng.Else():
                eng.sem_inc(M["passed"], 1)
            eng.sem_inc(M["passed"], 1)

        with nc.Block() as block:

            @block.gpsimd
            def _(pool):
                nc.gpsimd.memset(vr[:], 1.0).then_inc(s_m, 1)
                nc.gpsimd.memset(ones[:], 1.0).then_inc(s_m, 1)
                pool.sem_inc(s_done, 1)

                def work(u, k):
                    n, j = u // QT, u % QT
                    b, h = n // HEADS, n % HEADS
                    pool.wait_ge(s_done, k + 1)
                    nc.gpsimd.tensor_tensor(qr[:], M["q_t"][:, ds(b * T + j * P, P)],
                                            M["hmask"][:, ds(h, 1)].to_broadcast([P, P]), ALU.mult).then_inc(s_op, 1)
                    nc.gpsimd.tensor_copy(vr[:, :, 0:HD], M["v"][:, ds(b * QT, QT), ds(h * HD, HD)]).then_inc(s_op, 1)
                units(pool, work)

            @block.tensor
            def _(pe):
                nc.tensor.matmul(ps[0:1, 0:UNITS], M["mean_w"][:, 0:1], M["flags"][:], start=True, stop=True).then_inc(s_n, 1)

                def work(u, k):
                    n = u // QT
                    b = n // HEADS
                    pe.wait_ge(s_op, 2 * k + 2)
                    for h in range(2):
                        mm = nc.tensor.matmul(ps[:, BANK * h:BANK * (h + 1)], qr[:], M["k_t"][:, ds(b * T + BANK * h, BANK)],
                                              start=True, stop=True)
                    mm.then_inc(s_sc, 1)
                    pe.wait_ge(s_e, k + 1)
                    for c in range(KBLK):
                        mm = nc.tensor.transpose(ps[:, 2 * BANK + P * c:2 * BANK + P * (c + 1)], E[:, P * c:P * (c + 1)],
                                                 M["ident"][:])
                    mm.then_inc(s_t, 1)
                    pe.wait_ge(s_te, k + 1)
                    for c in range(KBLK):
                        mm = nc.tensor.matmul(ps[:, 4 * BANK:4 * BANK + HD + 1], pt[:, c, :], vr[:, c, :],
                                              start=(c == 0), stop=(c == KBLK - 1))
                    mm.then_inc(s_pv, 1)
                units(pe, work)

            @block.scalar
            def _(act):
                def work(u, k):
                    act.wait_ge(s_x, k + 1)
                    nc.scalar.activation(E[:], X[:], ACT.Exp, bias=nb[:], scale=EXP_SCALE).then_inc(s_e, 1)
                    act.wait_ge(s_t, k + 1)
                    nc.scalar.activation(pt[:], ps[:, 2 * BANK:4 * BANK], ACT.Identity).then_inc(s_te, 1)
                units(act, work)

            @block.sync
            def _(sp):
                sp.wait_ge(s_m, 8)

            @block.vector
            def _(dve):
                dve.wait_ge(s_n, 1)
                V.tensor_scalar(marks_f[:], ps[0:1, 0:UNITS], 0.0, None, ALU.is_gt).then_inc(s_m, 1)
                dve.wait_ge(s_m, 3)
                V.tensor_copy(marks[:], marks_f[:]).then_inc(s_m, 1)
                V.tensor_reduce(marked_f[:], marks_f[:], AX.X, ALU.max).then_inc(s_m, 1)
                V.tensor_tensor_scan(before_f[:], ones[0:1, 0:UNITS], marks_f[:], -1.0, ALU.mult, ALU.add).then_inc(s_m, 1)
                dve.wait_ge(s_m, 6)
                V.tensor_copy(marked[:], marked_f[:]).then_inc(s_m, 1)
                V.tensor_scalar(before[:], before_f[:], 0.0, None, ALU.max).then_inc(s_m, 1)

                def work(u, k):
                    n, j = u // QT, u % QT
                    b, h = n // HEADS, n % HEADS
                    st = Steps(dve, s_d, DVE_STEPS * k)

                    def ready():
                        st.wait()
                        dve.sem_inc(M["passed"], 1)
                    dve.wait_ge(s_sc, k + 1)
                    st.did(V.tensor_copy(S[:], ps[:, 0:T]))
                    ready()
                    st.did(V.tensor_scalar(W[:], S[:], -1.0, None, ALU.mult))
                    ready()
                    with dve.Fori(0, ROUNDS) as i:
                        dve.wait_ge(s_d, DVE_STEPS * k + 2 * i + 2)
                        dve.sem_inc(M["passed"], 1)
                        V.max(t8[:], W[:]).then_inc(s_d, 1)
                        dve.wait_ge(s_d, DVE_STEPS * k + 2 * i + 3)
                        dve.sem_inc(M["passed"], 1)
                        V.match_replace(out=W[:], in_to_replace=t8[:], in_values=W[:], imm_value=-3.0e38).then_inc(s_d, 1)
                    st.n += 2 * ROUNDS
                    ready()
                    st.did(V.max(t8[:], W[:]))
                    ready()
                    st.did(V.tensor_scalar(thr[:], t8[:, AT:AT + 1], -1.0, None, ALU.mult))
                    ready()
                    st.did(V.tensor_scalar(X[:], S[:], thr[:], None, ALU.is_gt, ALU.add, accum_out=above[:]))
                    st.did(V.tensor_scalar(keep[:], S[:], thr[:], None, ALU.is_equal))
                    ready()
                    st.did(V.tensor_scalar(room[:], above[:], -1.0, float(K_TOP), ALU.mult, ALU.add))
                    st.did(V.tensor_tensor_scan(rank[:], ones[:], keep[:], 0.0, ALU.mult, ALU.add))
                    ready()
                    st.did(V.scalar_tensor_tensor(out=keep[:], in0=rank[:], scalar=room[:], in1=keep[:],
                                                  op0=ALU.is_le, op1=ALU.mult))
                    ready()
                    st.did(V.tensor_tensor(keep[:], keep[:], X[:], ALU.add))
                    ready()
                    st.did(V.memset(X[:], FILL_SC))
                    ready()
                    V.copy_predicated(X[:], keep[:].bitcast(I32), S[:]).then_inc(s_d, 1)
                    st.n += 1
                    ready()
                    st.did(V.tensor_reduce(m[:], X[:], AX.X, ALU.max))
                    ready()
                    V.tensor_scalar(nb[:], m[:], -EXP_SCALE, None, ALU.mult).then_inc(s_x, 1)
                    dve.wait_ge(s_pv, k + 1)
                    out = ps[:, 4 * BANK:4 * BANK + HD + 1]
                    st.did(V.reciprocal(rden[:], out[:, HD:HD + 1]))
                    ready()
                    V.tensor_scalar(M["ctx"][:, ds(b * QT + j, 1), ds(h * HD, HD)].rearrange("p a e -> p (a e)"),
                                    out[:, 0:HD], rden[:], None, ALU.mult).then_inc(s_done, 1)
                    assert st.n == DVE_STEPS, st.n
                units(dve, work)


DEPTH = 6
BH, BD = 16, 64
INNER = BH * BD
WIN = 32
PAIRS = BH // 2
DI = int(P * 4 * 2 / 3)
CH = [(0, P), (P, P), (2 * P, DI - 2 * P)]
QK_SCALE = 8.0
MASKED = -1e30
G = TOK // BANK
RSQRT_BITS = float(0x5f3759df)
QK = 2 * INNER


def local_transformer(nc, ctx, A, M):
    ps = M["ps"]
    sem = lambda n: ctx.enter_context(nc.semaphore(n))
    xa, xb = M["xa"], M["xb"]
    V = nc.vector
    with ExitStack() as own:
        sb = lambda n, s, d=F32: own.enter_context(nc.sbuf_tensor(n, s, d))
        w_qkv = sb("w_qkv", [P, 3 * INNER])
        w_o = sb("w_o", [P, PAIRS, P])
        w1 = sb("w_1", [P, 2 * DI])
        w2 = sb("w_2", [P, 3, P])
        b1 = sb("b_1", [P, 6])
        vecs = sb("ln_g_ln_b_b2", [P, 3])
        scales = sb("qk_scales", [P, 4, BD])
        rot = sb("rotary", [P, 4, QT, BD])
        rot_l = sb("rotary_scaled", [P, 4, QT, BD])
        mask = sb("masks", [P, QT, 2 * WIN])
        xst = sb("x_tile", [P, 2, P])
        sq = sb("squares", [P, 2 * BH, BD])
        qk = sb("qk_normed", [P, 2 * BH, BD])
        rc = sb("qk_cos", [P, 2 * BH, BD])
        rs = sb("qk_sin", [P, 2 * BH, BD])
        ss, a_half, yr, tr = (sb(n, [P, 2 * BH]) for n in ("sum_sq", "neg_half", "rnorm", "newton"))
        q_t = sb("q_tt", [P, PAIRS, P])
        k_t = sb("k_tt", [P, 2, PAIRS, WIN + P])
        vt = sb("v_tok", [P, 2, 2, 512])
        v2 = sb("v_windows", [P, 2, 4, 512])
        sm = sb("sims", [P, BH, 2 * WIN])
        pe_ = sb("exps_b", [P, BH, 2 * WIN])
        pt = sb("exps_t", [P, PAIRS, P])
        cn = sb("ctx_b", [P, PAIRS, 2, BD])
        ct = sb("ctx_bt", [P, PAIRS, P])
        mxb, sumb, rsum = (sb(n, [P, BH]) for n in ("max_b", "sum_b", "rsum_b"))
        xs = sb("x_shifted", [P, TOK])
        xc = sb("x_centred", [P, TOK])
        xq = sb("x_square", [P, TOK])
        gel = sb("gelu", [P, 3, BANK])
        hid = sb("hidden", [P, 3, BANK])

        s_fix = sem("b_constants")
        s_const = sem("b_memsets")
        s_wq = sem("b_w_qkv")
        s_wo = sem("b_w_o")
        s_wf = sem("b_w_mlp")
        s_sc = sem("b_scales")
        s_rot = sem("b_rotary_ready")
        s_xst = sem("b_x_tile_ready")
        s_q = sem("b_qk_projected")
        s_v = sem("b_v_projected")
        s_sq = sem("b_squared")
        s_qn = sem("b_qk_normed")
        s_cos = sem("b_cos_ready")
        s_r = sem("b_rotated")
        s_f = sem("b_ring_filled")
        s_c = sem("b_ring_emptied")
        s_halo = sem("b_k_halo")
        s_s = sem("b_scores")
        s_min = sem("b_masked")
        s_sub = sem("b_less_max")
        s_e = sem("b_exps")
        s_v2 = sem("b_v_windows_ready")
        s_pv = sem("b_pv")
        s_co = sem("b_ctx")
        s_y = sem("b_out_projected")
        s_yo = sem("b_attention_added")
        s_1 = sem("b_dve_norm_steps")
        s_2 = sem("b_dve_softmax_steps")
        s_x = sem("b_shifted")
        s_mean = sem("b_mean")
        s_xc = sem("b_centred")
        s_xq = sem("b_squares")
        s_var = sem("b_var")
        s_sd = sem("b_sd")
        s_rd = sem("b_dve_mlp_steps")
        s_xn = sem("b_ln_ready")
        s_g = sem("b_gate")
        s_a = sem("b_up")
        s_ge = sem("b_gelu")
        s_h = sem("b_hidden")
        s_o = sem("b_mlp_out")
        s_fo = sem("b_layer_done")

        tile_at = lambda t: (t // QT, (t % QT) * P)
        ring = lambda i: ps[:, BANK * (4 + i % 2):BANK * (5 + i % 2)]
        CREDIT = 12
        R_V, R_TQ, R_TK, R_PT, R_CT = 4, 0, 2, 6, 8

        def ring_at(l, t, kind, i):
            if kind == R_V:
                return 160 * l + 2 + 10 * (t - 1) + R_V + i
            base = 160 * l + 2 + 10 * t + kind + i
            return base - 2 * (isinstance(t, int) and t == TILES - 1 and kind > R_V)

        def emptied(at):
            return at + 1 + CREDIT

        def v_at(l, t, i):
            return 160 * l + i if isinstance(t, int) and t == 0 else ring_at(l, t, R_V, i)

        def layers(eng, section):
            with eng.Fori(0, DEPTH) as l:
                section(l)

        def periods(eng, l, period):
            period(l, 0, 0, None, None)
            with eng.Fori(0, TILES // 2 - 1) as i:
                period(l, 2 * i + 1, 1, 2 * i, 0)
                period(l, 2 * i + 2, 0, 2 * i + 1, 1)
            period(l, TILES - 1, 1, TILES - 2, 0)
            period(l, None, None, TILES - 1, 1)

        with nc.Block() as block:

            @block.sync
            def _(sp):
                sp.dma_start(rot[:], A["b_rot"]).then_inc(s_fix, 16)
                sp.dma_start(mask[:], A["b_mask"]).then_inc(s_fix, 16)
                for s, k in ((s_v, 4), (s_qn, 2), (s_c, CREDIT), (s_yo, 1), (s_co, 1), (s_fo, G), (s_s, 2),
                             (s_f, 2), (s_pv, 2), (s_h, 3), (s_ge, 3), (s_o, 1), (s_e, 1), (s_v2, 32 * 16)):
                    sp.sem_inc(s, k)

                def weights_attention(l):
                    sp.dma_start(w_qkv[:], A["b_wqkv"][ds(l, 1)].rearrange("l p n -> (l p) n")).then_inc(s_wq, 16)
                    sp.dma_start(scales[:], A["b_scales"][ds(l, 1)].rearrange("l p a d -> (l p) a d")).then_inc(s_sc, 16)

                def weights_out(l):
                    sp.dma_start(w_o[:], A["b_wo"][ds(l, 1)].rearrange("l p c n -> (l p) c n")).then_inc(s_wo, 16)

                def weights_mlp(l):
                    for t, a in ((w1, "b_w1"), (w2, "b_w2"), (b1, "b_b1"), (vecs, "b_vecs")):
                        src = A[a][ds(l, 1)]
                        src = src.rearrange("l p c n -> (l p) c n") if a == "b_w2" else src.rearrange("l p n -> (l p) n")
                        sp.dma_start(t[:], src).then_inc(s_wf, 16)

                def v_windows(l, t1, p):
                    n = TILES * l + t1
                    sp.wait_ge(s_pv, n + 1)
                    sp.sem_inc(M["passed"], 1)
                    sp.wait_ge(s_c, emptied(v_at(l, t1, 1)))
                    for par in range(2):
                        for w in range(4):
                            lo = 64 * par
                            src = vt[WIN * w:WIN * (w + 1), p, par, :]
                            old = vt[WIN * (w - 1):WIN * w, p, par, :] if w else vt[3 * WIN:, 1 - p, par, :]
                            sp.dma_start(v2[lo + WIN:lo + 2 * WIN, p, w, :], src).then_inc(s_v2, 16)
                            sp.dma_start(v2[lo:lo + WIN, p, w, :], old).then_inc(s_v2, 16)

                weights_attention(0)
                weights_out(0)
                weights_mlp(0)
                sp.wait_ge(s_const, 3)

                def period(l, t1, p1, t, p):
                    if t1 is not None:
                        v_windows(l, t1, p1)

                def section(l):
                    period(l, 0, 0, None, None)
                    with sp.Fori(0, TILES // 2 - 1) as i:
                        period(l, 2 * i + 1, 1, None, None)
                        period(l, 2 * i + 2, 0, None, None)
                    period(l, TILES - 1, 1, None, None)
                    sp.sem_inc(M["passed"], 1)
                    nxt = (l + 1) % DEPTH
                    sp.wait_ge(s_v, 4 + 2 * TILES * (l + 1))
                    sp.sem_inc(M["passed"], 1)
                    sp.wait_ge(s_rot, 4 * (l + 1))
                    sp.sem_inc(M["passed"], 1)
                    weights_attention(nxt)
                    sp.wait_ge(s_y, TILES * (l + 1))
                    sp.sem_inc(M["passed"], 1)
                    weights_out(nxt)
                    sp.wait_ge(s_fo, G + G * (l + 1))
                    sp.sem_inc(M["passed"], 1)
                    weights_mlp(nxt)
                layers(sp, section)
                sp.wait_ge(s_wq, 16 * (DEPTH + 1))
                sp.wait_ge(s_sc, 16 * (DEPTH + 1))
                sp.wait_ge(s_wo, 16 * (DEPTH + 1))
                sp.wait_ge(s_wf, 64 * (DEPTH + 1))

            @block.gpsimd
            def _(pool):
                nc.gpsimd.memset(k_t[:], 0.0).then_inc(s_const, 1)
                nc.gpsimd.memset(vt[:], 0.0).then_inc(s_const, 1)
                nc.gpsimd.memset(xb[:], 0.0).then_inc(s_const, 1)
                pool.wait_ge(s_fix, 32)
                pool.wait_ge(s_const, 3)

                def cosines(l, t1):
                    n = TILES * l + t1
                    for i in range(2):
                        pool.wait_ge(s_qn, 2 * n + i + 3)
                        if i == 0:
                            if not (isinstance(t1, int) and t1 == 0):
                                pool.wait_ge(s_r, 2 * n)
                        nc.gpsimd.tensor_tensor(
                            rc[:, BH * i:BH * (i + 1), :], qk[:, BH * i:BH * (i + 1), :],
                            rot_l[:, 2 * i, ds(t1 % QT, 1), :].to_broadcast([P, BH, BD]), ALU.mult).then_inc(s_cos, 1)

                def period(l, t1, p1, t, p):
                    if t1 is not None:
                        cosines(l, t1)

                def section(l):
                    pool.wait_ge(s_sc, 16 * (l + 1))
                    pool.wait_ge(s_fo, G * (l + 1))
                    for i in range(4):
                        nc.gpsimd.tensor_tensor(rot_l[:, i], rot[:, i], scales[:, ds(i, 1), :].to_broadcast([P, QT, BD]),
                                                ALU.mult).then_inc(s_rot, 1)
                    pool.wait_ge(s_rot, 4 * (l + 1))
                    periods(pool, l, period)
                layers(pool, section)

            @block.tensor
            def _(pe):
                def project(l, t1, p1):
                    n = TILES * l + t1
                    pe.wait_ge(s_xst, 2 * n + 2)
                    for i in range(4):
                        if i % 2 == 0:
                            pe.wait_ge(s_qn, 2 * n + i // 2 + 1)
                        mm = nc.tensor.matmul(ps[:, BANK * i:BANK * (i + 1)], xst[:, p1, :],
                                              w_qkv[:, BANK * i:BANK * (i + 1)], start=True, stop=True)
                        if i % 2:
                            mm.then_inc(s_q, 1)
                    for i in range(2):
                        pe.wait_ge(s_c, emptied(v_at(l, t1, i) - 2))
                        nc.tensor.matmul(ring(i), xst[:, p1, :], w_qkv[:, QK + BANK * i:QK + BANK * (i + 1)],
                                         start=True, stop=True).then_inc(s_v, 1)

                def turn(l, t, kind, src):
                    for i in range(2):
                        pe.wait_ge(s_c, emptied(ring_at(l, t, kind, i) - 2))
                        for c in range(4):
                            mm = nc.tensor.transpose(ring(i)[:, P * c:P * (c + 1)], src(4 * i + c), M["ident"][:])
                        mm.then_inc(s_f, 1)

                def attend(l, t, p, project_next):
                    n = TILES * l + t
                    pe.wait_ge(s_r, 2 * n + 1)
                    pe.wait_ge(s_yo, n + 1)
                    turn(l, t, R_TQ, lambda c: rs[:, 2 * c:2 * c + 2, :])
                    pe.wait_ge(s_r, 2 * n + 2)
                    turn(l, t, R_TK, lambda c: rs[:, BH + 2 * c:BH + 2 * c + 2, :])
                    pe.wait_ge(s_halo, n + 1)
                    pe.wait_ge(s_co, n + 1)
                    pe.wait_ge(s_c, emptied(ring_at(l, t, R_TK, 1)))
                    pe.sem_inc(M["passed"], 1)
                    for h in range(BH):
                        lo = 64 * (h % 2)
                        for w in range(4):
                            mm = nc.tensor.matmul(
                                ps[WIN * w:WIN * (w + 1), BANK * (6 + h % 2) + 64 * (h // 2):BANK * (6 + h % 2) + 64 * (h // 2 + 1)],
                                q_t[lo:lo + 64, h // 2, WIN * w:WIN * (w + 1)],
                                k_t[lo:lo + 64, p, h // 2, WIN * w:WIN * (w + 2)], start=True, stop=True)
                    mm.then_inc(s_s, 1)
                    project_next()
                    pe.wait_ge(s_e, n + 2)
                    turn(l, t, R_PT, lambda c: pe_[:, 2 * c:2 * c + 2, :])
                    pe.wait_ge(s_min, n + 1)
                    pe.wait_ge(s_v2, 256 * (n + 1) + 512)
                    pe.wait_ge(s_c, emptied(ring_at(l, t, R_PT, 1)))
                    pe.sem_inc(M["passed"], 1)
                    for h in range(BH):
                        lo = 64 * (h % 2)
                        for w in range(4):
                            mm = nc.tensor.matmul(
                                ps[WIN * w:WIN * (w + 1), BANK * (6 + h % 2) + 64 * (h // 2):BANK * (6 + h % 2) + 64 * (h // 2 + 1)],
                                pt[lo:lo + 64, h // 2, WIN * w:WIN * (w + 1)],
                                v2[lo:lo + 64, p, w, 64 * (h // 2):64 * (h // 2 + 1)], start=True, stop=True)
                    mm.then_inc(s_pv, 1)
                    pe.wait_ge(s_co, n + 2)
                    turn(l, t, R_CT, lambda c: cn[:, c, :, :])
                    pe.wait_ge(s_c, emptied(ring_at(l, t, R_CT, 1)))
                    for c in range(PAIRS):
                        mm = nc.tensor.matmul(ring(0)[:, 0:P], w_o[:, c, :], ct[:, c, :],
                                              start=(c == 0), stop=(c == PAIRS - 1))
                    mm.then_inc(s_y, 1)

                def period(l, t1, p1, t, p):
                    nxt = (lambda: project(l, t1, p1)) if t1 is not None else (lambda: None)
                    if t is not None:
                        attend(l, t, p, nxt)
                    else:
                        nxt()

                def section(l):
                    pe.wait_ge(s_wq, 16 * (l + 1))
                    pe.wait_ge(s_wo, 16 * (l + 1))
                    periods(pe, l, period)
                    cols = lambda t, g: t[:, BANK * g:BANK * (g + 1)]
                    for g in range(G):
                        pe.wait_ge(s_x, 2 * G * l + 2 * g + 2)
                        nc.tensor.matmul(cols(ps, g), M["mean_w"][:], cols(xs, g), start=True, stop=True).then_inc(s_mean, 1)
                    for g in range(G):
                        pe.wait_ge(s_xq, G * l + g + 1)
                        nc.tensor.matmul(cols(ps, g), M["mean_w"][:], cols(xq, g), start=True, stop=True).then_inc(s_var, 1)
                    pe.wait_ge(s_wf, 64 * (l + 1))
                    pe.wait_ge(s_sd, G * (l + 1))
                    for g in range(G):
                        pe.wait_ge(s_xn, G * l + g + 1)
                        for c, (o, m) in enumerate(CH):
                            pe.wait_ge(s_ge, 3 * (G * l + g) + c + 1)
                            nc.tensor.matmul(ps[0:m, BANK * (1 + c):BANK * (2 + c)], w1[:, DI + o:DI + o + m], cols(xs, g),
                                             start=True, stop=True).then_inc(s_g, 1)
                            pe.wait_ge(s_h, 3 * (G * l + g) + c + 1)
                            nc.tensor.matmul(ps[0:m, BANK * (5 + c):BANK * (6 + c)], w1[:, o:o + m], cols(xs, g),
                                             start=True, stop=True).then_inc(s_a, 1)
                        pe.wait_ge(s_fo, G + G * l + g)
                        for c, (o, m) in enumerate(CH):
                            pe.wait_ge(s_h, 3 + 3 * (G * l + g) + c + 1)
                            mm = nc.tensor.matmul(ps[:, 0:BANK], w2[0:m, c, :], hid[0:m, c, :],
                                                  start=(c == 0), stop=(c == 2))
                        mm.then_inc(s_o, 1)
                layers(pe, section)

            @block.scalar
            def _(act):
                def stage(l, t1, p1):
                    n = TILES * l + t1
                    b, at = tile_at(t1)
                    act.wait_ge(s_v, 2 * n + 2)
                    for lo, sh in ((0, 1), (64, 0)):
                        src = xa[lo:lo + 64, ds(b, 1), ds(at + sh, P)].rearrange("p b t -> p (b t)")
                        nc.scalar.copy(xst[lo:lo + 64, p1, :], src).then_inc(s_xst, 1)

                def halo(l, t, p):
                    n = TILES * l + t
                    act.wait_ge(s_s, n + 1)
                    if isinstance(t, int) and t == 0:
                        act.wait_ge(s_c, emptied(160 * l - 1))
                    else:
                        act.wait_ge(s_c, emptied(160 * l + 2 + 10 * (t - 1) + R_TK + 1))
                    nc.scalar.copy(k_t[:, p, :, 0:WIN], k_t[:, 1 - p, :, P:P + WIN]).then_inc(s_halo, 1)

                def out_of_ring(l, pos, i, dst, src=None):
                    return nc.scalar.activation(dst, src if src is not None else ring(i), ACT.Identity).then_inc(s_c, 1)

                def first(l, t1, p1):
                    n = TILES * l + t1
                    for i in range(2):
                        act.wait_ge(s_q, 2 * n + i + 1)
                        nc.scalar.activation(sq[:, BH * i:BH * (i + 1), :], ps[:, 2 * BANK * i:2 * BANK * (i + 1)],
                                             ACT.Square).then_inc(s_sq, 1)
                    for i in range(2):
                        act.wait_ge(s_v, 4 + 2 * n + i + 1)
                        if i == 0:
                            act.wait_ge(s_v2, 256 * n + 512)
                        out_of_ring(l, None, i, vt[:, p1, i, :])

                def ring_out(l, t, kind, dst):
                    n = TILES * l + t
                    k = {R_TQ: 0, R_TK: 2, R_PT: 4, R_CT: 6}[kind]
                    for i in range(2):
                        act.wait_ge(s_f, 2 + 8 * n + k + i + 1)
                        out_of_ring(l, None, i, dst(i))

                def period(l, t1, p1, t, p):
                    if t is not None:
                        halo(l, t, p)
                    if t1 is not None:
                        stage(l, t1, p1)
                    if t is not None:
                        n = TILES * l + t
                        ring_out(l, t, R_TQ, lambda i: q_t[:, 4 * i:4 * i + 4, :])
                        ring_out(l, t, R_TK, lambda i: k_t[:, p, 4 * i:4 * i + 4, WIN:])
                    if t1 is not None:
                        first(l, t1, p1)
                    if t is not None:
                        act.wait_ge(s_sub, n + 1)
                        nc.scalar.activation(pe_[:].rearrange("p (c r) e -> p r c e", r=2),
                                             sm[:].rearrange("p (r c) e -> p r c e", r=2), ACT.Exp,
                                             scale=QK_SCALE).then_inc(s_e, 1)
                        ring_out(l, t, R_PT, lambda i: pt[:, 4 * i:4 * i + 4, :])
                        ring_out(l, t, R_CT, lambda i: ct[:, 4 * i:4 * i + 4, :])

                def section(l):
                    act.wait_ge(s_fo, G * (l + 1))
                    periods(act, l, period)
                    cols = lambda t, g: t[:, BANK * g:BANK * (g + 1)]
                    for g in range(G):
                        b, at = g * BANK // T, g * BANK % T
                        act.wait_ge(s_yo, TILES * l + 4 * g + 5)
                        for lo, sh in ((0, 1), (64, 0)):
                            nc.scalar.copy(xs[lo:lo + 64, BANK * g:BANK * (g + 1)],
                                                  xb[lo:lo + 64, b, at + sh:at + sh + BANK]).then_inc(s_x, 1)
                    for g in range(G):
                        act.wait_ge(s_xc, G * l + g + 1)
                        nc.scalar.activation(cols(xq, g), cols(xc, g), ACT.Square).then_inc(s_xq, 1)
                    for g in range(G):
                        act.wait_ge(s_var, G * l + g + 1)
                        nc.scalar.activation(cols(xq, g), cols(ps, g), ACT.Sqrt, bias=M["eps"][:]).then_inc(s_sd, 1)
                    act.wait_ge(s_wf, 64 * (l + 1))
                    for g in range(G):
                        for c, (o, m) in enumerate(CH):
                            act.wait_ge(s_g, 3 * (G * l + g) + c + 1)
                            act.wait_ge(s_h, 3 * (G * l + g) + c + 1)
                            nc.scalar.activation(gel[0:m, c, :], ps[0:m, BANK * (1 + c):BANK * (2 + c)], ACT.Gelu,
                                                 bias=b1[0:m, 3 + c:4 + c]).then_inc(s_ge, 1)
                act.wait_ge(s_const, 3)
                layers(act, section)

            @block.vector
            def _(dve):
                N_STEPS, S_STEPS, F_STEPS = 13 + 4, 3, 2 * G

                def normed(l, t1):
                    n = TILES * l + t1
                    st = Steps(dve, s_1, N_STEPS * n)
                    dve.wait_ge(s_sq, 2 * n + 2)
                    st.did(V.tensor_reduce(ss[:], sq[:], AX.X, ALU.add))
                    st.wait()
                    st.did(V.tensor_scalar(ss[:], ss[:], 1e-24, None, ALU.max))
                    st.wait()
                    st.did(V.tensor_scalar(yr[:].bitcast(I32), ss[:].bitcast(I32), -0.5, RSQRT_BITS, ALU.mult, ALU.add))
                    st.did(V.tensor_scalar(a_half[:], ss[:], -0.5, None, ALU.mult))
                    st.wait()
                    for _ in range(3):
                        st.did(V.tensor_tensor(tr[:], yr[:], yr[:], ALU.mult))
                        st.wait()
                        st.did(V.tensor_tensor(tr[:], tr[:], a_half[:], ALU.mult))
                        st.wait()
                        st.did(V.scalar_tensor_tensor(out=yr[:], in0=tr[:], scalar=1.5, in1=yr[:], op0=ALU.add, op1=ALU.mult))
                        st.wait()
                    dve.wait_ge(s_cos, 2 * n) if not (isinstance(t1, int) and t1 == 0) else None
                    for i in range(2):
                        V.tensor_tensor(qk[:, BH * i:BH * (i + 1), :],
                                        ps[:, 2 * BANK * i:2 * BANK * (i + 1)].rearrange("p (h e) -> p h e", e=BD),
                                        yr[:, BH * i:BH * (i + 1)].unsqueeze(2).to_broadcast([P, BH, BD]),
                                        ALU.mult).then_inc(s_qn, 1)
                    if not (isinstance(t1, int) and t1 == 0):
                        dve.wait_ge(s_f, 2 + 8 * (n - 1) + 4)
                    H2 = BD // 2
                    for i in range(2):
                        dve.wait_ge(s_qn, 2 * n + i + 3)
                        for a in range(2):
                            b = 1 - a
                            st.did(V.tensor_tensor(
                                rs[:, BH * i:BH * (i + 1), H2 * a:H2 * (a + 1)], qk[:, BH * i:BH * (i + 1), H2 * b:H2 * (b + 1)],
                                rot_l[:, 2 * i + 1, ds(t1 % QT, 1), H2 * a:H2 * (a + 1)].to_broadcast([P, BH, H2]), ALU.mult))
                    st.wait()
                    for i in range(2):
                        dve.wait_ge(s_cos, 2 * n + i + 1)
                        V.tensor_tensor(rs[:, BH * i:BH * (i + 1), :], rs[:, BH * i:BH * (i + 1), :],
                                        rc[:, BH * i:BH * (i + 1), :], ALU.add).then_inc(s_r, 1)
                    assert st.n == N_STEPS, st.n

                def softmax(l, t):
                    n = TILES * l + t
                    st = Steps(dve, s_2, S_STEPS * n)
                    dve.wait_ge(s_s, 2 + n + 1)
                    dve.wait_ge(s_e, n + 1)
                    V.tensor_tensor(sm[:], ps[:, BANK * 6:BANK * 8].rearrange("p (h e) -> p h e", e=2 * WIN),
                                    mask[:, ds(t % QT, 1), :].to_broadcast([P, BH, 2 * WIN]), ALU.min).then_inc(s_min, 1)
                    dve.wait_ge(s_min, n + 1)
                    st.did(V.tensor_reduce(mxb[:], sm[:], AX.X, ALU.max))
                    st.wait()
                    V.tensor_tensor(sm[:], sm[:], mxb[:].unsqueeze(2).to_broadcast([P, BH, 2 * WIN]),
                                    ALU.subtract).then_inc(s_sub, 1)

                def sums(l, t):
                    n = TILES * l + t
                    st = Steps(dve, s_2, S_STEPS * n)
                    st.n = 1
                    dve.wait_ge(s_e, n + 2)
                    st.did(V.tensor_reduce(sumb[:], pe_[:], AX.X, ALU.add))
                    st.wait()
                    st.did(V.reciprocal(rsum[:], sumb[:]))
                    st.wait()
                    dve.wait_ge(s_pv, 2 + n + 1)
                    for r in range(2):
                        ins = V.tensor_tensor(
                            cn[:, :, r, :], ps[:, BANK * (6 + r):BANK * (7 + r)].rearrange("p (c e) -> p c e", e=BD),
                            rsum[:].rearrange("p (c r) -> p r c", r=2)[:, r, :].unsqueeze(2).to_broadcast([P, PAIRS, BD]),
                            ALU.mult)
                    ins.then_inc(s_co, 1)

                def added(l, t):
                    n = TILES * l + t
                    b, at = tile_at(t)
                    dve.wait_ge(s_y, n + 1)
                    x = lambda s: s[:, ds(b, 1), ds(at + 1, P)].rearrange("p b t -> p (b t)")
                    V.tensor_tensor(x(xb), x(xa), ring(0)[:, 0:P], ALU.add).then_inc(s_yo, 1)

                def period(l, t1, p1, t, p):
                    if t is not None:
                        softmax(l, t)
                    if t1 is not None:
                        normed(l, t1)
                    if t is not None:
                        sums(l, t)
                        added(l, t)

                def section(l):
                    dve.wait_ge(s_rot, 4 * (l + 1))
                    periods(dve, l, period)
                    cols = lambda t, g: t[:, BANK * g:BANK * (g + 1)]
                    st = Steps(dve, s_rd, F_STEPS * l)
                    for g in range(G):
                        dve.wait_ge(s_mean, G * l + g + 1)
                        V.tensor_tensor(cols(xc, g), cols(xs, g), cols(ps, g), ALU.subtract).then_inc(s_xc, 1)
                    dve.wait_ge(s_wf, 64 * (l + 1))
                    for g in range(G):
                        dve.wait_ge(s_sd, G * l + g + 1)
                        st.did(V.reciprocal(cols(xq, g), cols(xq, g)))
                        st.wait()
                        st.did(V.tensor_tensor(cols(xc, g), cols(xc, g), cols(xq, g), ALU.mult))
                        st.wait()
                        V.tensor_scalar(cols(xs, g), cols(xc, g), vecs[:, 0:1], vecs[:, 1:2], ALU.mult, ALU.add).then_inc(s_xn, 1)
                    for g in range(G):
                        b, at = g * BANK // T, g * BANK % T
                        for c, (o, m) in enumerate(CH):
                            dve.wait_ge(s_ge, 3 + 3 * (G * l + g) + c + 1)
                            dve.wait_ge(s_a, 3 * (G * l + g) + c + 1)
                            dve.wait_ge(s_o, G * l + g + 1)
                            V.scalar_tensor_tensor(out=hid[0:m, c, :], in0=ps[0:m, BANK * (5 + c):BANK * (6 + c)],
                                                   scalar=b1[0:m, c:c + 1], in1=gel[0:m, c, :],
                                                   op0=ALU.add, op1=ALU.mult).then_inc(s_h, 1)
                        dve.wait_ge(s_o, 1 + G * l + g + 1)
                        V.scalar_tensor_tensor(out=xa[:, b, 1 + at:1 + at + BANK], in0=ps[:, 0:BANK], scalar=vecs[:, 2:3],
                                               in1=xb[:, b, 1 + at:1 + at + BANK], op0=ALU.add, op1=ALU.add).then_inc(s_fo, 1)
                dve.wait_ge(s_const, 3)
                layers(dve, section)


def join(nc, A, M, out):
    ps = M["ps"]
    V = nc.vector
    with ExitStack() as own:
        sb = lambda n, s: own.enter_context(nc.sbuf_tensor(n, s, F32))
        sem = lambda n: own.enter_context(nc.semaphore(n))
        x0, w, bias = sb("x_again", [P, TOK]), sb("w_out_a", [P, P]), sb("b_out_a", [P, 1])
        ct, y = sb("ctx_a_t", [P, TOK]), sb("y", [P, TOK])
        s_ld, s_t, s_te, s_y, s_1, s_out = (sem(n) for n in (
            "join_loads", "join_turned", "join_turned_out", "join_projected", "join_added", "join_stores"))
        col = lambda t, g: t[:, BANK * g:BANK * (g + 1)]
        with nc.Block() as block:

            @block.sync
            def _(sp):
                for t, a in ((x0, "x_t"), (w, "a_wo"), (bias, "a_bo")):
                    sp.dma_start(t[:], A[a]).then_inc(s_ld, 16)
                for g in range(G):
                    sp.wait_ge(s_1, 3 * g + 3)
                    sp.dma_start(out[:, BANK * g:BANK * (g + 1)], col(y, g)).then_inc(s_out, 16)
                sp.wait_ge(s_out, 16 * G)

            @block.tensor
            def _(pe):
                for g in range(G):
                    for t in range(4 * g, 4 * g + 4):
                        mm = nc.tensor.transpose(ps[:, P * t:P * (t + 1)], M["ctx"][:, t, :], M["ident"][:])
                    mm.then_inc(s_t, 1)
                pe.wait_ge(s_ld, 48)
                for g in range(G):
                    pe.wait_ge(s_te, g + 1)
                    nc.tensor.matmul(ps[:, BANK * (4 + g):BANK * (5 + g)], w[:], col(ct, g), start=True, stop=True).then_inc(s_y, 1)

            @block.scalar
            def _(act):
                for g in range(G):
                    act.wait_ge(s_t, g + 1)
                    nc.scalar.activation(col(ct, g), col(ps, g), ACT.Identity).then_inc(s_te, 1)

            @block.vector
            def _(dve):
                dve.wait_ge(s_ld, 48)
                for g in range(G):
                    b, at = g * BANK // T, g * BANK % T
                    dve.wait_ge(s_y, g + 1)
                    V.tensor_scalar(col(y, g), ps[:, BANK * (4 + g):BANK * (5 + g)], bias[:], None, ALU.add).then_inc(s_1, 1)
                    dve.wait_ge(s_1, 3 * g + 1)
                    V.tensor_tensor(col(y, g), col(y, g), col(x0, g), ALU.add).then_inc(s_1, 1)
                    dve.wait_ge(s_1, 3 * g + 2)
                    V.tensor_tensor(col(y, g), col(y, g), M["xa"][:, b, 1 + at:1 + at + BANK], ALU.add).then_inc(s_1, 1)


def build(nc, A, out):
    with ExitStack() as ctx:
        sb = lambda n, s, d=F32: ctx.enter_context(nc.sbuf_tensor(n, s, d))
        M = {
            "ps": ctx.enter_context(nc.psum_tensor("ps", [P, 8 * BANK], F32)),
            "ident": sb("ident", [P, P]), "mean_w": sb("mean_w", [P, P]), "eps": sb("eps", [P, 1]),
            "xa": sb("stream_a", [P, B, T + 1]), "ctx": sb("ctx_a", [P, TILES, P]),
        }
        M["passed"] = ctx.enter_context(nc.semaphore("waits_passed"))
        with ExitStack() as own:
            sa = lambda n, s, d=F32: own.enter_context(nc.sbuf_tensor(n, s, d))
            M.update({
                "hmask": sa("head_mask", [P, HEADS]), "iota8": sa("iota8", [P, 8]),
                "q_t": sa("q_t", [P, TOK]), "k_t": sa("k_t", [P, TOK]), "v": sa("v_a", [P, TILES, P]),
                "vh": sa("v_head", [P, 2, KBLK, HD + 1]), "flags": sa("flags", [P, UNITS]),
            })
            for name in ("pt_out", "pv_done", "ctx_out"):
                M[name] = own.enter_context(nc.semaphore(name))
            front(nc, own, A, M)
            topk_attention(nc, own, M)
            repair(nc, M)
        M["xb"] = sb("stream_b", [P, B, T + 1])
        with ExitStack() as own:
            local_transformer(nc, own, A, M)
        join(nc, A, M, out)


def _tables():
    import numpy as np

    f = np.float32
    half = np.arange(0, BD, 2, dtype=f)
    inv_freq = (f(1.0) / f(10000.0) ** (half / f(BD))).astype(f)
    t = np.arange(T, dtype=f)
    freqs = (t[:, None] * inv_freq[None, :]).astype(f)
    base = ((half + f(0.4 * BD)) / f(1.4 * BD)).astype(f)
    power = ((t - T // 2) / f(WIN // 2)).astype(f)
    scale = (base[None, :] ** power[:, None]).astype(f)
    cos, sin = np.cos(freqs), np.sin(freqs)
    both = lambda a, b: np.concatenate([a, b], -1)
    rot = np.stack([both(cos * scale, cos * scale), both(-sin * scale, sin * scale),
                    both(cos / scale, cos / scale), both(-sin / scale, sin / scale)], 0).astype(f)
    rot = rot.reshape(4, QT, P, BD).transpose(2, 0, 1, 3)
    i, j = np.arange(P)[:, None] % WIN, np.arange(2 * WIN)[None, :]
    seen = (j <= i + WIN) & (j >= i)
    big = np.where(seen, f(3.0e38), f(MASKED)).astype(f)
    masks = np.broadcast_to(big[:, None, :], (P, QT, 2 * WIN)).copy()
    masks[:WIN, 0, :WIN] = MASKED
    return {
        "c_hmask": (np.arange(P)[:, None] // HD == np.arange(HEADS)[None, :]).astype(f),
        "c_ident": np.eye(P, dtype=f),
        "c_iota8": np.broadcast_to(np.arange(8, dtype=f), (P, 8)),
        "b_rot": rot, "b_mask": masks,
    }


def _layout(inputs):
    import numpy as np

    v = {k: np.asarray(a) for k, a in inputs.items()}
    w, b = v["L0_attn_qkv_w"], v["L0_attn_qkv_b"]
    rows = lambda a: np.broadcast_to(a, (P,) + a.shape)
    wq = v["L0_ffn_Wqkv"]
    wv = wq[:, :, 2 * INNER:].reshape(DEPTH, P, PAIRS, 2, BD).transpose(0, 1, 3, 2, 4).reshape(DEPTH, P, INNER)
    qs, ks = v["L0_ffn_q_scale"], v["L0_ffn_k_scale"]
    scales = np.stack([qs, np.roll(qs, BD // 2, 1), ks, np.roll(ks, BD // 2, 1)], 1)
    w2 = np.zeros((DEPTH, 3 * P, P), np.float32)
    w2[:, :DI] = v["L0_ffn_W2"]
    b1 = np.zeros((DEPTH, 2, 3 * P), np.float32)
    b1[:, :, :DI] = v["L0_ffn_b1"].reshape(DEPTH, 2, DI)
    return {
        "x_t": v["L0_attn_x"].reshape(TOK, P).T, "a_w": w.T, "a_bq": b[:P, None], "a_bk": b[P:2 * P, None],
        "a_bv": rows(b[2 * P:]), "a_wo": v["L0_attn_out_w"].T, "a_bo": v["L0_attn_out_b"][:, None],
        "b_wqkv": np.concatenate([wq[:, :, :2 * INNER], wv], 2),
        "b_scales": np.broadcast_to(scales[:, None], (DEPTH, P, 4, BD)),
        "b_wo": v["L0_ffn_Wo"].reshape(DEPTH, PAIRS, P, P).transpose(0, 2, 1, 3),
        "b_w1": v["L0_ffn_W1"], "b_w2": w2.reshape(DEPTH, 3, P, P).transpose(0, 2, 1, 3),
        "b_b1": b1.reshape(DEPTH, 6, P).transpose(0, 2, 1),
        "b_vecs": np.stack([v["L0_ffn_ln_g"], v["L0_ffn_ln_b"], v["L0_ffn_b2"]], 2),
    }


def kernel(**inputs):
    import numpy as np
    import concourse.bacc as bacc
    from concourse.bass_utils import run_bass_kernel_spmd

    nc = bacc.Bacc("TRN2", target_bir_lowering=False, num_devices=1)
    arrays = {k: np.ascontiguousarray(a) for k, a in {**_layout(inputs), **_tables()}.items()}
    A = {k: nc.dram_tensor(k, a.shape, F32, kind="ExternalInput").ap() for k, a in arrays.items()}
    out = nc.dram_tensor("out_t", (P, TOK), F32, kind="ExternalOutput").ap()
    build(nc, A, out)
    r = run_bass_kernel_spmd(nc, [arrays], core_ids=[0])
    return np.ascontiguousarray(r.results[0]["out_t"].T).reshape(B, T, P)
```

```python
from contextlib import ExitStack

import concourse.bass as bass
from concourse import mybir

F32 = mybir.dt.float32
BF16 = mybir.dt.bfloat16
I32 = mybir.dt.int32
ALU = mybir.AluOpType
ACT = mybir.ActivationFunctionType
AX = mybir.AxisListType
ds = bass.ds

P = 128
BANK = 512
EPS = 1e-5

B, T = 2, 1024
TOK = B * T
TILES = TOK // P
HEADS, HD = 16, 8
K_TOP = int(0.7 * T)
FILL = -10000.0
GROUPS = B * HEADS
QT = T // P
HALF = QT // 2
KBLK = T // P
UNITS = GROUPS * QT
SC = 2.0 ** -40
EXP_SCALE = HD ** -0.5 / SC
Z = -0.5221
DENSITY = 0.3481
WINDOW = 8
SQRT_BITS = float(0x1fbd1df5)
NEXT_UP = 2.0 ** -24 * 1.0001


class Steps:

    def __init__(self, eng, sem, base=0):
        self.eng, self.sem, self.base, self.n = eng, sem, base, 0

    def did(self, ins):
        self.n += 1
        ins.then_inc(self.sem, 1)

    def wait(self):
        self.eng.wait_ge(self.sem, self.base + self.n)


def front(nc, ctx, A, M):
    sb = lambda n, s, d=F32: ctx.enter_context(nc.sbuf_tensor(n, s, d))
    sem = lambda n: ctx.enter_context(nc.semaphore(n))
    ps = M["ps"]
    with ExitStack() as own:
        osb = lambda n, s, d=F32: own.enter_context(nc.sbuf_tensor(n, s, d))
        x0 = osb("x0", [P, TOK])
        xc = osb("xc", [P, TOK])
        sq = osb("sq", [P, TOK])
        xn = osb("xn", [P, TOK])
        w = osb("w_qkv_a", [P, 3 * P])
        bq = osb("bq", [P, 1])
        bk = osb("bk", [P, 1])
        bqs = osb("bqs", [P, 1])
        bv = osb("bv", [P, P])
        s_ld = sem("front_loads")
        s_set = sem("front_constants")
        s_mean = sem("front_mean")
        s_xc = sem("front_centred")
        s_sq = sem("front_squared")
        s_var = sem("front_var")
        s_sd = sem("front_sd")
        s_rs = sem("front_rstd")
        s_xn = sem("front_normed")
        s_qk = sem("front_qk")
        s_qke = sem("front_qk_out")
        s_v = sem("front_v")
        s_ve = sem("front_v_out")
        s_end = sem("front_credits")
        G = TOK // BANK
        col = lambda t, g: t[:, BANK * g:BANK * (g + 1)]
        bank = lambda b: ps[:, BANK * b:BANK * (b + 1)]
        with nc.Block() as block:

            @block.sync
            def _(sp):
                loads = [(x0, A["x_t"]), (w, A["a_w"]), (bq, A["a_bq"]), (bk, A["a_bk"]), (bv, A["a_bv"]),
                         (M["hmask"], A["c_hmask"]), (M["ident"], A["c_ident"]), (M["iota8"], A["c_iota8"])]
                for t, a in loads:
                    sp.dma_start(t[:], a).then_inc(s_ld, 16)
                for name in ("pt_out", "pv_done", "ctx_out"):
                    sp.sem_inc(M[name], 2)
                sp.wait_ge(s_ld, 16 * len(loads))
                sp.nop().then_inc(s_end, 1)

            @block.vector
            def _(dve):
                nc.vector.memset(M["mean_w"][:], 1.0 / P).then_inc(s_set, 1)
                nc.vector.memset(M["eps"][:], EPS).then_inc(s_set, 1)
                nc.vector.memset(M["xa"][:], 0.0).then_inc(s_set, 1)
                nc.vector.memset(M["vh"][:], 1.0).then_inc(s_set, 1)
                nc.vector.memset(M["flags"][:], 0.0).then_inc(s_set, 1)
                dve.wait_ge(s_end, 1)
                nc.vector.tensor_scalar(bqs[:], bq[:], SC, None, ALU.mult).then_inc(s_set, 1)
                for g in range(G):
                    dve.wait_ge(s_mean, g + 1)
                    nc.vector.tensor_tensor(col(xc, g), col(x0, g), bank(g), ALU.subtract).then_inc(s_xc, 1)
                for g in range(G):
                    dve.wait_ge(s_sd, g + 1)
                    nc.vector.reciprocal(col(sq, g), col(sq, g)).then_inc(s_rs, 1)
                    dve.wait_ge(s_rs, g + 1)
                    nc.vector.tensor_tensor(col(xn, g), col(xc, g), col(sq, g), ALU.mult).then_inc(s_xn, 1)
                for g in range(G):
                    dve.wait_ge(s_v, 4 * g + 4)
                    nc.vector.tensor_tensor(
                        M["v"][:, 4 * g:4 * g + 4, :], bank(g).rearrange("p (t f) -> p t f", t=4),
                        bv[:].unsqueeze(1).to_broadcast([P, 4, P]), ALU.add).then_inc(s_ve, 1)

            @block.tensor
            def _(pe):
                pe.wait_ge(s_end, 1)
                pe.wait_ge(s_set, 1)
                for g in range(G):
                    nc.tensor.matmul(bank(g), M["mean_w"][:], col(x0, g), start=True, stop=True).then_inc(s_mean, 1)
                for g in range(G):
                    pe.wait_ge(s_sq, g + 1)
                    nc.tensor.matmul(bank(4 + g), M["mean_w"][:], col(sq, g), start=True, stop=True).then_inc(s_var, 1)
                for g in range(G):
                    pe.wait_ge(s_xn, g + 1)
                    nc.tensor.matmul(bank(g), w[:, 0:P], col(xn, g), start=True, stop=True).then_inc(s_qk, 1)
                    nc.tensor.matmul(bank(4 + g), w[:, P:2 * P], col(xn, g), start=True, stop=True).then_inc(s_qk, 1)
                for t in range(TILES):
                    if t % 4 == 0:
                        pe.wait_ge(s_qke, 2 * (t // 4) + 2)
                    nc.tensor.matmul(ps[:, P * t:P * (t + 1)], xn[:, P * t:P * (t + 1)], w[:, 2 * P:3 * P],
                                     start=True, stop=True).then_inc(s_v, 1)

            @block.scalar
            def _(act):
                act.wait_ge(s_set, 6)
                for g in range(G):
                    act.wait_ge(s_xc, g + 1)
                    nc.scalar.activation(col(sq, g), col(xc, g), ACT.Square).then_inc(s_sq, 1)
                for g in range(G):
                    act.wait_ge(s_var, g + 1)
                    nc.scalar.activation(col(sq, g), bank(4 + g), ACT.Sqrt, bias=M["eps"][:]).then_inc(s_sd, 1)
                for g in range(G):
                    act.wait_ge(s_qk, 2 * g + 2)
                    nc.scalar.activation(col(M["q_t"], g), bank(g), ACT.Identity, bias=bqs[:], scale=SC).then_inc(s_qke, 1)
                    nc.scalar.activation(col(M["k_t"], g), bank(4 + g), ACT.Identity, bias=bk[:]).then_inc(s_qke, 1)

            @block.gpsimd
            def _(pool):
                for g in range(G):
                    pool.wait_ge(s_xn, g + 1)
                    if g == 0:
                        pool.wait_ge(s_set, 3)
                    b, at = g * BANK // T, g * BANK % T
                    nc.gpsimd.tensor_copy(M["xa"][:, b, 1 + at:1 + at + BANK], col(xn, g))


def topk_attention(nc, ctx, M):
    ps = M["ps"]
    sem = lambda n: ctx.enter_context(nc.semaphore(n))
    s_qm = sem("qm_ready")
    s_vh = sem("vh_ready")
    s_sc = sem("scores_ready")
    s_ev = sem("scores_in_sbuf")
    s_nt = sem("threshold_ready")
    s_ct = sem("count_ready")
    s_mx = sem("exp_bias_ready")
    s_ex = sem("exp_ready")
    s_p = sem("probs_ready")
    s_pt = sem("probs_t_ready")
    s_h = sem("dve_head_steps")
    s_t = sem("dve_tail_steps")
    s_c = sem("dve_context_steps")
    s_pe, s_pv, s_cx = (M[n] for n in ("pt_out", "pv_done", "ctx_out"))
    with ExitStack() as own:
        sb = lambda n, s, d=F32: own.enter_context(nc.sbuf_tensor(n, s, d))
        S = sb("scores", [P, 2, QT, T])
        E = sb("exps", [P, QT, T])
        U = sb("signed", [P, 2, T])
        Y = sb("pushed", [P, 2, T])
        PT = sb("probs_t", [P, 2, KBLK, P])
        junk_a = sb("junk_act", [P, QT, T], BF16)
        junk_d = Y[:].bitcast(BF16).rearrange("p a (b t) -> p (a b) t", b=2)
        qm = sb("q_masked", [P, 2, T])
        st = lambda n: sb(n, [P, 2, QT])
        tot, cnt, mx, nb = (st(n) for n in ("row_sum", "count", "row_max", "exp_bias"))
        pt = sb("points", [P, 2, 4, 2, QT])
        step, diff, diff2 = (sb(n, [P, 2, QT]) for n in ("step", "diff", "diff_far"))
        sig, tmp = sb("sigma", [P, QT]), sb("tmp", [P, QT])
        cross = sb("crossed", [P, 2, QT], I32)
        side, sgn, x, nud, idx, idx2 = (st(n) for n in ("side", "sgn", "signed_thr", "nudged", "idx", "idx_next"))
        thr, num, kth, nxt, bad, tmp2 = (st(n) for n in ("thr", "exact_num", "kth", "next_value", "bad", "off"))
        bn = sb("bn", [P, 2, QT, 6])
        top8 = sb("top8", [P, QT, 8])
        hit = sb("hit", [P, HALF, 8])
        pick = sb("pick", [P, HALF, 8])
        rden = sb("rden", [P, 2, HALF])

        def sl(xy):
            return slice(HALF * xy, HALF * (xy + 1))

        def scores(pe, n, g):
            b = n // HEADS
            pe.wait_ge(s_qm, n + 1)
            for j in range(QT):
                if not (isinstance(n, int) and 8 * n + j < 2):
                    pe.wait_ge(s_ev, QT * n + j - 1)
                for h in range(2):
                    mm = nc.tensor.matmul(ps[:, BANK * (2 * (j % 2) + h):BANK * (2 * (j % 2) + h + 1)],
                                          qm[:, g, P * j:P * (j + 1)],
                                          M["k_t"][:, ds(b * T + BANK * h, BANK)], start=True, stop=True)
                mm.then_inc(s_sc, 1)

        def probs_t(pe, n, j):
            pe.wait_ge(s_p, QT * n + j + 1)
            for h in range(2):
                pe.wait_ge(s_pe, 2 * QT * n + 2 * j + h + 1)
                for c in range(4):
                    mm = nc.tensor.transpose(ps[:, BANK * (4 + h) + P * c:BANK * (4 + h) + P * (c + 1)],
                                             E[:, j, P * (4 * h + c):P * (4 * h + c + 1)], M["ident"][:])
                mm.then_inc(s_pt, 1)

        def pv(pe, n, g, j):
            if j == 0:
                pe.wait_ge(s_vh, n + 1)
            if j % HALF == 0:
                pe.wait_ge(s_cx, 2 * n + j // HALF + 1)
            pe.wait_ge(s_pe, 2 * QT * n + 2 * j + 4)
            o = BANK * (6 + j // HALF) + 16 * (j % HALF)
            for c in range(KBLK):
                mm = nc.tensor.matmul(ps[:, o:o + HD + 1], PT[:, j % 2, c, :], M["vh"][:, g, c, :],
                                      start=(c == 0), stop=(c == KBLK - 1))
            mm.then_inc(s_pv, 1)

        def pe_tail(pe, n, g):
            probs_t(pe, n, 0)
            for j in range(QT):
                if j + 1 < QT:
                    probs_t(pe, n, j + 1)
                pv(pe, n, g, j)

        def evacuate(act, n, g, xy):
            for j in range(HALF * xy, HALF * (xy + 1)):
                act.wait_ge(s_sc, QT * n + j + 1)
                nc.scalar.activation(S[:, g, j, :], ps[:, 2 * BANK * (j % 2):2 * BANK * (j % 2 + 1)], ACT.Identity,
                                     accum_out=tot[:, g, j:j + 1]).then_inc(s_ev, 1)

        def count(act, n, g, k):
            act.wait_ge(s_nt, 4 * n + k + 1)
            if not (isinstance(n, int) and n + k == 0):
                act.wait_ge(s_ct, 3 * n + k)
            for j in range(QT):
                ins = nc.scalar.activation(junk_a[:, j, :], S[:, g, j, :], ACT.Sign, bias=pt[:, g, k, 0, j:j + 1],
                                           accum_out=cnt[:, g, j:j + 1])
            ins.then_inc(s_ct, 1)

        def exps(act, n, g, xy):
            act.wait_ge(s_mx, n + 1)
            for j in range(HALF * xy, HALF * (xy + 1)):
                ins = nc.scalar.activation(E[:, j, :], S[:, g, j, :], ACT.Exp, bias=nb[:, g, j:j + 1], scale=EXP_SCALE)
            ins.then_inc(s_ex, 1)

        def evacuate_t(act, n, g, xy):
            for j in range(HALF * xy, HALF * (xy + 1)):
                act.wait_ge(s_pv, QT * n + j + 1)
                for h in range(2):
                    act.wait_ge(s_pt, 2 * QT * n + 2 * j + h + 1)
                    nc.scalar.activation(PT[:, j % 2, 4 * h:4 * h + 4, :], ps[:, BANK * (4 + h):BANK * (5 + h)],
                                         ACT.Identity).then_inc(s_pe, 1)

        def act_period(act, n1, g1, n, g):
            H = lambda f, *a: f(act, n1, g1, *a) if n1 is not None else None
            L = lambda f, *a: f(act, n, g, *a) if n is not None else None
            H(evacuate, 0)
            H(evacuate, 1)
            L(exps, 0)
            H(count, 0)
            L(exps, 1)
            H(count, 1)
            L(evacuate_t, 0)
            H(count, 2)
            L(evacuate_t, 1)

        V = nc.vector

        def first_threshold(dve, own_, n, g):
            for j in range(QT):
                dve.wait_ge(s_ev, QT * n + j + 1)
                ins = V.bn_stats(bn[:, g, j, :], S[:, g, j, 0:BANK])
            own_.did(ins)
            own_.wait()
            own_.did(V.tensor_tensor(sig[:], bn[:, g, :, 2], bn[:, g, :, 5], ALU.add))
            own_.wait()
            own_.did(V.tensor_scalar(sig[:].bitcast(I32), sig[:].bitcast(I32), 0.5,
                                     SQRT_BITS - 4.5 * 2 ** 23, ALU.mult, ALU.add))
            own_.wait()
            own_.did(V.tensor_scalar(tmp[:], sig[:], -Z, None, ALU.mult))
            own_.did(V.tensor_scalar(step[:, 0, :], sig[:], 1.0 / (2 * T * DENSITY), None, ALU.mult))
            own_.did(V.memset(step[:, 1, :], 1.0))
            own_.wait()
            V.scalar_tensor_tensor(out=pt[:, g, 0, 0, :], in0=tot[:, g, :], scalar=-1.0 / T, in1=tmp[:],
                                   op0=ALU.mult, op1=ALU.add).then_inc(s_nt, 1)

        def next_threshold(dve, own_, n, g, k):
            new, old = pt[:, g, k], pt[:, g, max(k - 1, 0)]
            dve.wait_ge(s_ct, 3 * n + k + 1)
            own_.did(V.tensor_scalar(pt[:, g, k, 1, :], cnt[:, g, :], float(T - 2 * K_TOP), None, ALU.add))
            own_.wait()
            if k > 0:
                own_.did(V.tensor_tensor(diff[:], new, old, ALU.subtract))
                own_.did(V.tensor_tensor(tmp[:], new[:, 1, :], old[:, 1, :], ALU.mult))
                own_.wait()
                own_.did(V.tensor_scalar(cross[:, k - 1, :], tmp[:], 0.0, None, ALU.is_lt))
                crossed = lambda c: cross[:, c, :].unsqueeze(1).to_broadcast([P, 2, QT])
                if k == 2:
                    own_.did(V.tensor_tensor(diff2[:], diff[:], step[:], ALU.add))
                    own_.wait()
                    dve.sem_inc(M["passed"], 1)
                    own_.did(V.copy_predicated(step[:], crossed(0), diff2[:]))
                own_.wait()
                dve.sem_inc(M["passed"], 1)
                own_.did(V.copy_predicated(step[:], crossed(k - 1), diff[:]))
                own_.wait()
            own_.did(V.reciprocal(tmp[:], step[:, 1, :]))
            own_.wait()
            own_.did(V.tensor_tensor(tmp[:], tmp[:], step[:, 0, :], ALU.mult))
            own_.wait()
            own_.did(V.tensor_tensor(tmp[:], tmp[:], pt[:, g, k, 1, :], ALU.mult))
            own_.wait()
            V.tensor_tensor(pt[:, g, k + 1, 0, :], pt[:, g, k, 0, :], tmp[:], ALU.subtract).then_inc(s_nt, 1)

        def row_max(dve, own_, n, g):
            for j in range(QT):
                ins = V.tensor_reduce(mx[:, g, j:j + 1], S[:, g, j, :], AX.X, ALU.max)
            own_.did(ins)
            own_.wait()
            V.tensor_scalar(nb[:, g, :], mx[:, g, :], -EXP_SCALE, None, ALU.mult).then_inc(s_mx, 1)

        def exact_count(dve, own_, n, g, xy):
            c = sl(xy)
            dve.wait_ge(s_nt, 4 * n + 4)
            own_.did(V.tensor_scalar(thr[:, g, c], pt[:, g, 3, 0, c], -1.0, None, ALU.mult))
            own_.wait()
            for j in range(HALF * xy, HALF * (xy + 1)):
                ins = V.tensor_scalar(junk_d[:, j % HALF, :], S[:, g, j, :], thr[:, g, j:j + 1], None, ALU.is_ge, ALU.add,
                                      accum_out=num[:, g, j:j + 1])
            own_.did(ins)
            own_.wait()
            own_.did(V.tensor_scalar(side[:, g, c], num[:, g, c], K_TOP - 0.5, None, ALU.is_ge))
            own_.wait()
            own_.did(V.tensor_scalar(sgn[:, g, c], side[:, g, c], -2.0, 1.0, ALU.mult, ALU.add))
            own_.wait()
            own_.did(V.tensor_tensor(x[:, g, c], sgn[:, g, c], thr[:, g, c], ALU.mult))
            own_.did(V.scalar_tensor_tensor(out=idx[:, g, c], in0=num[:, g, c], scalar=K_TOP - 0.5, in1=sgn[:, g, c],
                                            op0=ALU.subtract, op1=ALU.mult))
            own_.wait()
            own_.did(V.scalar_tensor_tensor(out=nud[:, g, c], in0=x[:, g, c], scalar=-1.0, in1=x[:, g, c],
                                            op0=ALU.mult, op1=ALU.max))
            own_.did(V.tensor_scalar(idx[:, g, c], idx[:, g, c], -1.0, -0.5, ALU.mult, ALU.add))
            own_.wait()
            own_.did(V.scalar_tensor_tensor(out=nud[:, g, c], in0=nud[:, g, c], scalar=NEXT_UP, in1=side[:, g, c],
                                            op0=ALU.mult, op1=ALU.mult))
            own_.did(V.tensor_tensor(idx2[:, g, c], idx[:, g, c], sgn[:, g, c], ALU.add))
            own_.wait()
            own_.did(V.tensor_tensor(nud[:, g, c], nud[:, g, c], x[:, g, c], ALU.add))
            own_.wait()

        def near_values(dve, own_, n, g, xy, pair):
            def signed(j):
                own_.did(V.tensor_scalar(U[:, j % 2, :], S[:, g, j, :], sgn[:, g, j:j + 1], None, ALU.mult))

            def pushed(j):
                own_.did(V.scalar_tensor_tensor(out=Y[:, j % 2, :], in0=U[:, j % 2, :], scalar=nud[:, g, j:j + 1],
                                                in1=U[:, j % 2, :], op0=ALU.is_ge, op1=ALU.subtract, reverse1=True))

            def largest(j):
                own_.did(V.max(top8[:, j, :], Y[:, j % 2, :]))

            j = HALF * xy
            if pair == 0:
                signed(j)
                signed(j + 1)
                own_.wait()
                pushed(j)
                pushed(j + 1)
                own_.wait()
                signed(j + 2)
                signed(j + 3)
                largest(j)
                largest(j + 1)
            else:
                own_.wait()
                pushed(j + 2)
                pushed(j + 3)
                own_.wait()
                own_.did(hits(g, xy, idx))
                largest(j + 2)
                largest(j + 3)

        def hits(g, xy, at):
            return V.tensor_tensor(hit[:], M["iota8"][:].unsqueeze(1).to_broadcast([P, HALF, 8]),
                                   at[:, g, sl(xy)].unsqueeze(2).to_broadcast([P, HALF, 8]), ALU.is_equal)

        def take(own_, g, xy, out):
            c = sl(xy)
            own_.did(V.tensor_tensor(pick[:], hit[:], top8[:, c, :], ALU.mult))
            own_.wait()
            own_.did(V.tensor_reduce(out[:, g, c], pick[:], AX.X, ALU.add))
            own_.wait()

        def select(dve, own_, n, g, xy):
            c = sl(xy)
            own_.wait()
            take(own_, g, xy, kth)
            own_.did(V.tensor_tensor(thr[:, g, c], kth[:, g, c], sgn[:, g, c], ALU.mult))
            own_.did(hits(g, xy, idx2))
            own_.wait()
            take(own_, g, xy, nxt)
            own_.did(V.tensor_tensor(bad[:, g, c], kth[:, g, c], nxt[:, g, c], ALU.is_equal))
            own_.did(V.tensor_tensor(tmp2[:, g, c], idx[:, g, c], side[:, g, c], ALU.subtract))
            own_.wait()
            for value, bound, op in ((tmp2, WINDOW - 1.5, ALU.is_gt),
                                     (mx, 2.0 ** -13, ALU.is_gt),
                                     (mx, 0.9 * FILL / EXP_SCALE, ALU.is_lt),
                                     (tot, -(2.0 ** -2), ALU.is_lt)):
                own_.did(V.scalar_tensor_tensor(out=bad[:, g, c], in0=value[:, g, c], scalar=bound, in1=bad[:, g, c],
                                                op0=op, op1=ALU.add))
                own_.wait()
            own_.did(V.scalar_tensor_tensor(out=M["flags"][:, ds(QT * n + HALF * xy, HALF)], in0=x[:, g, c],
                                            scalar=0.0, in1=bad[:, g, c], op0=ALU.is_equal, op1=ALU.add))

        def probs(dve, own_, n, g, xy):
            dve.wait_ge(s_ex, 2 * n + xy + 1)
            for j in range(HALF * xy, HALF * (xy + 1)):
                V.scalar_tensor_tensor(out=E[:, j, :], in0=S[:, g, j, :], scalar=thr[:, g, j:j + 1], in1=E[:, j, :],
                                       op0=ALU.is_ge, op1=ALU.mult).then_inc(s_p, 1)

        def context(dve, own_, n, g, xy):
            b, h = n // HEADS, n % HEADS
            dve.wait_ge(s_pv, 2 + QT * n + HALF * (xy + 1))
            out = ps[:, BANK * (6 + xy):BANK * (6 + xy) + 16 * HALF].rearrange("p (j e) -> p j e", j=HALF)
            own_.did(V.tensor_scalar(rden[:, xy, :], out[:, :, HD], 1e-30, None, ALU.max))
            own_.wait()
            own_.did(V.reciprocal(rden[:, xy, :], rden[:, xy, :]))
            own_.wait()
            V.tensor_tensor(M["ctx"][:, ds(b * QT + HALF * xy, HALF), ds(h * HD, HD)], out[:, :, 0:HD],
                            rden[:, xy, :].unsqueeze(2).to_broadcast([P, HALF, HD]), ALU.mult).then_inc(s_cx, 1)

        HEAD_STEPS = 6 + 4 + 8 + 10 + 1
        TAIL_STEPS = 2 * (11 + 3 * HALF + 14)

        def dve_period(dve, n1, g1, n, g, before, gb):
            head = Steps(dve, s_h, HEAD_STEPS * n1) if n1 is not None else None
            tail = Steps(dve, s_t, TAIL_STEPS * n) if n is not None else None
            late = Steps(dve, s_c, 4 * before) if before is not None else None
            H = lambda f, *a: f(dve, head, n1, g1, *a) if n1 is not None else None
            L = lambda f, *a: f(dve, tail, n, g, *a) if n is not None else None
            L(exact_count, 0)
            H(first_threshold)
            L(near_values, 0, 0)
            L(near_values, 0, 1)
            H(next_threshold, 0)
            L(select, 0)
            L(probs, 0)
            if before is not None:
                context(dve, late, before, gb, 0)
                context(dve, late, before, gb, 1)
            L(exact_count, 1)
            H(next_threshold, 1)
            L(near_values, 1, 0)
            L(near_values, 1, 1)
            L(select, 1)
            L(probs, 1)
            H(next_threshold, 2)
            H(row_max)
            assert head is None or head.n == HEAD_STEPS
            assert tail is None or tail.n == TAIL_STEPS

        with nc.Block() as block:

            @block.gpsimd
            def _(pool):
                def operands(n, g):
                    b, h = n // HEADS, n % HEADS
                    if not isinstance(n, int):
                        pool.wait_ge(s_sc, QT * n - QT)
                    nc.gpsimd.tensor_tensor(qm[:, g, :], M["q_t"][:, ds(b * T, T)],
                                            M["hmask"][:, ds(h, 1)].to_broadcast([P, T]),
                                            ALU.mult).then_inc(s_qm, 1)
                    if not isinstance(n, int):
                        pool.wait_ge(s_pv, QT * n - QT + 2)
                    nc.gpsimd.tensor_copy(M["vh"][:, g, :, 0:HD],
                                          M["v"][:, ds(b * QT, QT), ds(h * HD, HD)]).then_inc(s_vh, 1)

                operands(0, 0)
                operands(1, 1)
                with pool.Fori(1, GROUPS // 2) as i:
                    operands(2 * i, 0)
                    operands(2 * i + 1, 1)

            def periods(eng, Fori, period):
                period(0, 0, None, None, None, None)
                period(1, 1, 0, 0, None, None)
                with Fori(0, GROUPS // 2 - 1) as i:
                    period(2 * i + 2, 0, 2 * i + 1, 1, 2 * i, 0)
                    period(2 * i + 3, 1, 2 * i + 2, 0, 2 * i + 1, 1)
                period(None, None, GROUPS - 1, 1, GROUPS - 2, 0)

            @block.tensor
            def _(pe):
                def period(n1, g1, n, g, before, gb):
                    if n1 is not None:
                        scores(pe, n1, g1)
                    if n is not None:
                        pe_tail(pe, n, g)
                periods(pe, pe.Fori, period)

            @block.scalar
            def _(act):
                periods(act, act.Fori, lambda n1, g1, n, g, before, gb: act_period(act, n1, g1, n, g))

            @block.vector
            def _(dve):
                periods(dve, dve.Fori, lambda *a: dve_period(dve, *a))
                late = Steps(dve, s_c, 4 * (GROUPS - 1))
                context(dve, late, GROUPS - 1, 1, 0)
                context(dve, late, GROUPS - 1, 1, 1)


def repair(nc, M):
    ps = M["ps"]
    V = nc.vector
    DROP = T - K_TOP
    ROUNDS, AT = DROP // 8, DROP % 8
    FILL_SC = FILL / EXP_SCALE
    with ExitStack() as own:
        sb = lambda n, s, d=F32: own.enter_context(nc.sbuf_tensor(n, s, d))
        sem = lambda n: own.enter_context(nc.semaphore(n))
        marks, marked = sb("unit_marks", [1, UNITS], I32), sb("any_mark", [1, 1], I32)
        marks_f, marked_f = sb("unit_marks_f", [1, UNITS]), sb("any_mark_f", [1, 1])
        before, before_f = sb("marks_before", [1, UNITS], I32), sb("marks_before_f", [1, UNITS])
        qr, vr = sb("q_unit", [P, P]), sb("v_unit", [P, KBLK, HD + 1])
        S, W, X, E = (sb(n, [P, T]) for n in ("r_scores", "r_left", "r_sparse", "r_exps"))
        ones, rank, keep = (sb(n, [P, T]) for n in ("r_ones", "r_rank", "r_keep"))
        pt = sb("r_probs_t", [P, KBLK, P])
        t8 = sb("r_top8", [P, 8])
        thr, above, room, m, nb, rden = (sb(n, [P, 1]) for n in ("r_thr", "r_above", "r_room", "r_max", "r_bias", "r_den"))
        s_n = sem("marks_summed")
        s_m = sem("marks_ready")
        s_op = sem("r_operands")
        s_sc = sem("r_scores_ready")
        s_x = sem("r_sparse_ready")
        s_e = sem("r_exps_ready")
        s_t = sem("r_turned")
        s_te = sem("r_turned_out")
        s_pv = sem("r_products")
        s_d = sem("r_dve_steps")
        s_done = sem("r_unit_done")
        DVE_STEPS = 2 + 2 * ROUNDS + 12

        def units(eng, work):
            eng.wait_ge(s_m, 8)
            some = eng.value_load(marked[0:1, 0:1], min_val=0, max_val=1)
            with eng.If(some > 0):
                with eng.Fori(0, UNITS) as u:
                    mark = eng.value_load(marks[0:1, ds(u, 1)], min_val=0, max_val=1)
                    with eng.If(mark > 0):
                        work(u, eng.value_load(before[0:1, ds(u, 1)], min_val=0, max_val=UNITS - 1))
                    with eng.Else():
                        eng.sem_inc(M["passed"], 1)
                    eng.sem_inc(M["passed"], 1)
            with eng.Else():
                eng.sem_inc(M["passed"], 1)
            eng.sem_inc(M["passed"], 1)

        with nc.Block() as block:

            @block.gpsimd
            def _(pool):
                nc.gpsimd.memset(vr[:], 1.0).then_inc(s_m, 1)
                nc.gpsimd.memset(ones[:], 1.0).then_inc(s_m, 1)
                pool.sem_inc(s_done, 1)

                def work(u, k):
                    n, j = u // QT, u % QT
                    b, h = n // HEADS, n % HEADS
                    pool.wait_ge(s_done, k + 1)
                    nc.gpsimd.tensor_tensor(qr[:], M["q_t"][:, ds(b * T + j * P, P)],
                                            M["hmask"][:, ds(h, 1)].to_broadcast([P, P]), ALU.mult).then_inc(s_op, 1)
                    nc.gpsimd.tensor_copy(vr[:, :, 0:HD], M["v"][:, ds(b * QT, QT), ds(h * HD, HD)]).then_inc(s_op, 1)
                units(pool, work)

            @block.tensor
            def _(pe):
                nc.tensor.matmul(ps[0:1, 0:UNITS], M["mean_w"][:, 0:1], M["flags"][:], start=True, stop=True).then_inc(s_n, 1)

                def work(u, k):
                    n = u // QT
                    b = n // HEADS
                    pe.wait_ge(s_op, 2 * k + 2)
                    for h in range(2):
                        mm = nc.tensor.matmul(ps[:, BANK * h:BANK * (h + 1)], qr[:], M["k_t"][:, ds(b * T + BANK * h, BANK)],
                                              start=True, stop=True)
                    mm.then_inc(s_sc, 1)
                    pe.wait_ge(s_e, k + 1)
                    for c in range(KBLK):
                        mm = nc.tensor.transpose(ps[:, 2 * BANK + P * c:2 * BANK + P * (c + 1)], E[:, P * c:P * (c + 1)],
                                                 M["ident"][:])
                    mm.then_inc(s_t, 1)
                    pe.wait_ge(s_te, k + 1)
                    for c in range(KBLK):
                        mm = nc.tensor.matmul(ps[:, 4 * BANK:4 * BANK + HD + 1], pt[:, c, :], vr[:, c, :],
                                              start=(c == 0), stop=(c == KBLK - 1))
                    mm.then_inc(s_pv, 1)
                units(pe, work)

            @block.scalar
            def _(act):
                def work(u, k):
                    act.wait_ge(s_x, k + 1)
                    nc.scalar.activation(E[:], X[:], ACT.Exp, bias=nb[:], scale=EXP_SCALE).then_inc(s_e, 1)
                    act.wait_ge(s_t, k + 1)
                    nc.scalar.activation(pt[:], ps[:, 2 * BANK:4 * BANK], ACT.Identity).then_inc(s_te, 1)
                units(act, work)

            @block.sync
            def _(sp):
                sp.wait_ge(s_m, 8)

            @block.vector
            def _(dve):
                dve.wait_ge(s_n, 1)
                V.tensor_scalar(marks_f[:], ps[0:1, 0:UNITS], 0.0, None, ALU.is_gt).then_inc(s_m, 1)
                dve.wait_ge(s_m, 3)
                V.tensor_copy(marks[:], marks_f[:]).then_inc(s_m, 1)
                V.tensor_reduce(marked_f[:], marks_f[:], AX.X, ALU.max).then_inc(s_m, 1)
                V.tensor_tensor_scan(before_f[:], ones[0:1, 0:UNITS], marks_f[:], -1.0, ALU.mult, ALU.add).then_inc(s_m, 1)
                dve.wait_ge(s_m, 6)
                V.tensor_copy(marked[:], marked_f[:]).then_inc(s_m, 1)
                V.tensor_scalar(before[:], before_f[:], 0.0, None, ALU.max).then_inc(s_m, 1)

                def work(u, k):
                    n, j = u // QT, u % QT
                    b, h = n // HEADS, n % HEADS
                    st = Steps(dve, s_d, DVE_STEPS * k)

                    def ready():
                        st.wait()
                        dve.sem_inc(M["passed"], 1)
                    dve.wait_ge(s_sc, k + 1)
                    st.did(V.tensor_copy(S[:], ps[:, 0:T]))
                    ready()
                    st.did(V.tensor_scalar(W[:], S[:], -1.0, None, ALU.mult))
                    ready()
                    with dve.Fori(0, ROUNDS) as i:
                        dve.wait_ge(s_d, DVE_STEPS * k + 2 * i + 2)
                        dve.sem_inc(M["passed"], 1)
                        V.max(t8[:], W[:]).then_inc(s_d, 1)
                        dve.wait_ge(s_d, DVE_STEPS * k + 2 * i + 3)
                        dve.sem_inc(M["passed"], 1)
                        V.match_replace(out=W[:], in_to_replace=t8[:], in_values=W[:], imm_value=-3.0e38).then_inc(s_d, 1)
                    st.n += 2 * ROUNDS
                    ready()
                    st.did(V.max(t8[:], W[:]))
                    ready()
                    st.did(V.tensor_scalar(thr[:], t8[:, AT:AT + 1], -1.0, None, ALU.mult))
                    ready()
                    st.did(V.tensor_scalar(X[:], S[:], thr[:], None, ALU.is_gt, ALU.add, accum_out=above[:]))
                    st.did(V.tensor_scalar(keep[:], S[:], thr[:], None, ALU.is_equal))
                    ready()
                    st.did(V.tensor_scalar(room[:], above[:], -1.0, float(K_TOP), ALU.mult, ALU.add))
                    st.did(V.tensor_tensor_scan(rank[:], ones[:], keep[:], 0.0, ALU.mult, ALU.add))
                    ready()
                    st.did(V.scalar_tensor_tensor(out=keep[:], in0=rank[:], scalar=room[:], in1=keep[:],
                                                  op0=ALU.is_le, op1=ALU.mult))
                    ready()
                    st.did(V.tensor_tensor(keep[:], keep[:], X[:], ALU.add))
                    ready()
                    st.did(V.memset(X[:], FILL_SC))
                    ready()
                    V.copy_predicated(X[:], keep[:].bitcast(I32), S[:]).then_inc(s_d, 1)
                    st.n += 1
                    ready()
                    st.did(V.tensor_reduce(m[:], X[:], AX.X, ALU.max))
                    ready()
                    V.tensor_scalar(nb[:], m[:], -EXP_SCALE, None, ALU.mult).then_inc(s_x, 1)
                    dve.wait_ge(s_pv, k + 1)
                    out = ps[:, 4 * BANK:4 * BANK + HD + 1]
                    st.did(V.reciprocal(rden[:], out[:, HD:HD + 1]))
                    ready()
                    V.tensor_scalar(M["ctx"][:, ds(b * QT + j, 1), ds(h * HD, HD)].rearrange("p a e -> p (a e)"),
                                    out[:, 0:HD], rden[:], None, ALU.mult).then_inc(s_done, 1)
                    assert st.n == DVE_STEPS, st.n
                units(dve, work)


DEPTH = 6
BH, BD = 16, 64
INNER = BH * BD
WIN = 32
PAIRS = BH // 2
DI = int(P * 4 * 2 / 3)
CH = [(0, P), (P, P), (2 * P, DI - 2 * P)]
QK_SCALE = 8.0
MASKED = -1e30
G = TOK // BANK
RSQRT_BITS = float(0x5f3759df)
QK = 2 * INNER


def local_transformer(nc, ctx, A, M):
    ps = M["ps"]
    sem = lambda n: ctx.enter_context(nc.semaphore(n))
    xa, xb = M["xa"], M["xb"]
    V = nc.vector
    with ExitStack() as own:
        sb = lambda n, s, d=F32: own.enter_context(nc.sbuf_tensor(n, s, d))
        w_qkv = sb("w_qkv", [P, 3 * INNER])
        w_o = sb("w_o", [P, PAIRS, P])
        w1 = sb("w_1", [P, 2 * DI])
        w2 = sb("w_2", [P, 3, P])
        b1 = sb("b_1", [P, 6])
        vecs = sb("ln_g_ln_b_b2", [P, 3])
        scales = sb("qk_scales", [P, 4, BD])
        rot = sb("rotary", [P, 4, QT, BD])
        rot_l = sb("rotary_scaled", [P, 4, QT, BD])
        mask = sb("masks", [P, QT, 2 * WIN])
        xst = sb("x_tile", [P, 2, P])
        sq = sb("squares", [P, 2 * BH, BD])
        qk = sb("qk_normed", [P, 2 * BH, BD])
        rc = sb("qk_cos", [P, 2 * BH, BD])
        rs = sb("qk_sin", [P, 2 * BH, BD])
        ss, a_half, yr, tr = (sb(n, [P, 2 * BH]) for n in ("sum_sq", "neg_half", "rnorm", "newton"))
        q_t = sb("q_tt", [P, PAIRS, P])
        k_t = sb("k_tt", [P, 2, PAIRS, WIN + P])
        vt = sb("v_tok", [P, 2, 2, 512])
        v2 = sb("v_windows", [P, 2, 4, 512])
        sm = sb("sims", [P, BH, 2 * WIN])
        pe_ = sb("exps_b", [P, BH, 2 * WIN])
        pt = sb("exps_t", [P, PAIRS, P])
        cn = sb("ctx_b", [P, PAIRS, 2, BD])
        ct = sb("ctx_bt", [P, PAIRS, P])
        mxb, sumb, rsum = (sb(n, [P, BH]) for n in ("max_b", "sum_b", "rsum_b"))
        xs = sb("x_shifted", [P, TOK])
        xc = sb("x_centred", [P, TOK])
        xq = sb("x_square", [P, TOK])
        gel = sb("gelu", [P, 3, BANK])
        hid = sb("hidden", [P, 3, BANK])

        s_fix = sem("b_constants")
        s_const = sem("b_memsets")
        s_wq = sem("b_w_qkv")
        s_wo = sem("b_w_o")
        s_wf = sem("b_w_mlp")
        s_sc = sem("b_scales")
        s_rot = sem("b_rotary_ready")
        s_xst = sem("b_x_tile_ready")
        s_q = sem("b_qk_projected")
        s_v = sem("b_v_projected")
        s_sq = sem("b_squared")
        s_qn = sem("b_qk_normed")
        s_cos = sem("b_cos_ready")
        s_r = sem("b_rotated")
        s_f = sem("b_ring_filled")
        s_c = sem("b_ring_emptied")
        s_halo = sem("b_k_halo")
        s_s = sem("b_scores")
        s_min = sem("b_masked")
        s_sub = sem("b_less_max")
        s_e = sem("b_exps")
        s_v2 = (sem("b_v_windows_ready_even"), sem("b_v_windows_ready_odd"))
        s_pv = sem("b_pv")
        s_co = sem("b_ctx")
        s_y = sem("b_out_projected")
        s_yo = sem("b_attention_added")
        s_1 = sem("b_dve_norm_steps")
        s_2 = sem("b_dve_softmax_steps")
        s_x = sem("b_shifted")
        s_mean = sem("b_mean")
        s_xc = sem("b_centred")
        s_xq = sem("b_squares")
        s_var = sem("b_var")
        s_sd = sem("b_sd")
        s_rd = sem("b_dve_mlp_steps")
        s_xn = sem("b_ln_ready")
        s_g = sem("b_gate")
        s_a = sem("b_up")
        s_ge = sem("b_gelu")
        s_h = sem("b_hidden")
        s_o = sem("b_mlp_out")
        s_fo = sem("b_layer_done")

        tile_at = lambda t: (t // QT, (t % QT) * P)
        ring = lambda i: ps[:, BANK * (4 + i % 2):BANK * (5 + i % 2)]
        CREDIT = 12
        V_, CT_, PT_, TQ_, TK_ = "v", "ctx turned", "probs turned", "q turned", "k turned"
        USES = [(V_, 0), (V_, 1), (TQ_, 0), (TK_, 0)]
        for n_ in range(TILES + 1):
            in_period = ((V_, n_ + 2), (CT_, n_ - 1), (PT_, n_), (TQ_, n_ + 1), (TK_, n_ + 1))
            USES += [(what, t) for what, t in in_period if 0 <= t < TILES]
        PLACE = {use: 2 * i for i, use in enumerate(USES)}
        FILLS = {use: 2 * i for i, use in enumerate(u for u in USES if u[0] != V_)}

        def steady(table, step, what, t):
            return table[what, t] if isinstance(t, int) else table[what, 5] + step * (t - 5)

        def emptied(l, what, t, i):
            return 160 * l + steady(PLACE, 10, what, t) + i + 1 + CREDIT

        def filled(l, what, t, i):
            return 8 * TILES * l + steady(FILLS, 8, what, t) + i + 1 + 2

        def layers(eng, section):
            with eng.Fori(0, DEPTH) as l:
                section(l)

        def periods(eng, l, prologue, period, epilogue):
            prologue(l)
            period(l, 0, 0)
            period(l, 1, 1)
            with eng.Fori(0, TILES // 2 - 2) as i:
                period(l, 2 * i + 2, 0)
                period(l, 2 * i + 3, 1)
            period(l, TILES - 2, 0)
            period(l, TILES - 1, 1)
            epilogue(l)

        def within(t):
            return not isinstance(t, int) or 0 <= t < TILES

        with nc.Block() as block:

            @block.sync
            def _(sp):
                sp.dma_start(rot[:], A["b_rot"]).then_inc(s_fix, 16)
                sp.dma_start(mask[:], A["b_mask"]).then_inc(s_fix, 16)
                for s, k in ((s_v, 4), (s_qn, 2), (s_c, CREDIT), (s_yo, 1), (s_co, 1), (s_fo, G), (s_s, 2),
                             (s_f, 2), (s_pv, 2), (s_h, 3), (s_ge, 3), (s_o, 1), (s_e, 1),
                             (s_v2[0], 256), (s_v2[1], 256)):
                    sp.sem_inc(s, k)

                def weights_attention(l):
                    sp.dma_start(w_qkv[:], A["b_wqkv"][ds(l, 1)].rearrange("l p n -> (l p) n")).then_inc(s_wq, 16)
                    sp.dma_start(scales[:], A["b_scales"][ds(l, 1)].rearrange("l p a d -> (l p) a d")).then_inc(s_sc, 16)

                def weights_out(l):
                    sp.dma_start(w_o[:], A["b_wo"][ds(l, 1)].rearrange("l p c n -> (l p) c n")).then_inc(s_wo, 16)

                def weights_mlp(l):
                    for t, a in ((w1, "b_w1"), (w2, "b_w2"), (b1, "b_b1"), (vecs, "b_vecs")):
                        src = A[a][ds(l, 1)]
                        src = src.rearrange("l p c n -> (l p) c n") if a == "b_w2" else src.rearrange("l p n -> (l p) n")
                        sp.dma_start(t[:], src).then_inc(s_wf, 16)

                def v_windows(l, t1, p):
                    n = TILES * l + t1
                    sp.wait_ge(s_pv, n + 1)
                    sp.sem_inc(M["passed"], 1)
                    sp.wait_ge(s_c, emptied(l, V_, t1, 1))
                    for par in range(2):
                        for w in range(4):
                            lo = 64 * par
                            src = vt[WIN * w:WIN * (w + 1), p, par, :]
                            old = vt[WIN * (w - 1):WIN * w, p, par, :] if w else vt[3 * WIN:, 1 - p, par, :]
                            sp.dma_start(v2[lo + WIN:lo + 2 * WIN, p, w, :], src).then_inc(s_v2[p], 16)
                            sp.dma_start(v2[lo:lo + WIN, p, w, :], old).then_inc(s_v2[p], 16)

                weights_attention(0)
                weights_out(0)
                weights_mlp(0)
                sp.wait_ge(s_const, 3)

                def prologue(l):
                    v_windows(l, 0, 0)
                    v_windows(l, 1, 1)

                def period(l, t, p):
                    if within(t + 2):
                        v_windows(l, t + 2, p)

                def section(l):
                    periods(sp, l, prologue, period, lambda l: None)
                    sp.sem_inc(M["passed"], 1)
                    nxt = (l + 1) % DEPTH
                    sp.wait_ge(s_v, 4 + 2 * TILES * (l + 1))
                    sp.sem_inc(M["passed"], 1)
                    sp.wait_ge(s_rot, 4 * (l + 1))
                    sp.sem_inc(M["passed"], 1)
                    weights_attention(nxt)
                    sp.wait_ge(s_y, TILES * (l + 1))
                    sp.sem_inc(M["passed"], 1)
                    weights_out(nxt)
                    sp.wait_ge(s_fo, G + G * (l + 1))
                    sp.sem_inc(M["passed"], 1)
                    weights_mlp(nxt)
                layers(sp, section)
                sp.wait_ge(s_wq, 16 * (DEPTH + 1))
                sp.wait_ge(s_sc, 16 * (DEPTH + 1))
                sp.wait_ge(s_wo, 16 * (DEPTH + 1))
                sp.wait_ge(s_wf, 64 * (DEPTH + 1))

            @block.gpsimd
            def _(pool):
                nc.gpsimd.memset(k_t[:], 0.0).then_inc(s_const, 1)
                nc.gpsimd.memset(vt[:], 0.0).then_inc(s_const, 1)
                nc.gpsimd.memset(xb[:], 0.0).then_inc(s_const, 1)
                pool.wait_ge(s_fix, 32)
                pool.wait_ge(s_const, 3)

                def cosines(l, t1):
                    n = TILES * l + t1
                    for i in range(2):
                        pool.wait_ge(s_qn, 2 * n + i + 3)
                        if i == 0:
                            if not (isinstance(t1, int) and t1 == 0):
                                pool.wait_ge(s_r, 2 * n)
                        nc.gpsimd.tensor_tensor(
                            rc[:, BH * i:BH * (i + 1), :], qk[:, BH * i:BH * (i + 1), :],
                            rot_l[:, 2 * i, ds(t1 % QT, 1), :].to_broadcast([P, BH, BD]), ALU.mult).then_inc(s_cos, 1)

                def prologue(l):
                    cosines(l, 0)
                    cosines(l, 1)

                def period(l, t, p):
                    if within(t + 2):
                        cosines(l, t + 2)

                def section(l):
                    pool.wait_ge(s_sc, 16 * (l + 1))
                    pool.wait_ge(s_fo, G * (l + 1))
                    for i in range(4):
                        nc.gpsimd.tensor_tensor(rot_l[:, i], rot[:, i], scales[:, ds(i, 1), :].to_broadcast([P, QT, BD]),
                                                ALU.mult).then_inc(s_rot, 1)
                    pool.wait_ge(s_rot, 4 * (l + 1))
                    periods(pool, l, prologue, period, lambda l: None)
                layers(pool, section)

            @block.tensor
            def _(pe):
                def free(l, what, t, i):
                    pe.wait_ge(s_c, emptied(l, what, t, i) - 2)

                def project(l, t1, p1):
                    n = TILES * l + t1
                    pe.wait_ge(s_xst, 2 * n + 2)
                    for i in range(4):
                        if i % 2 == 0:
                            pe.wait_ge(s_qn, 2 * n + i // 2 + 1)
                        mm = nc.tensor.matmul(ps[:, BANK * i:BANK * (i + 1)], xst[:, p1, :],
                                              w_qkv[:, BANK * i:BANK * (i + 1)], start=True, stop=True)
                        if i % 2:
                            mm.then_inc(s_q, 1)
                    for i in range(2):
                        free(l, V_, t1, i)
                        nc.tensor.matmul(ring(i), xst[:, p1, :], w_qkv[:, QK + BANK * i:QK + BANK * (i + 1)],
                                         start=True, stop=True).then_inc(s_v, 1)

                def turn(l, t, kind, src):
                    for i in range(2):
                        free(l, kind, t, i)
                        for c in range(4):
                            mm = nc.tensor.transpose(ring(i)[:, P * c:P * (c + 1)], src(4 * i + c), M["ident"][:])
                        mm.then_inc(s_f, 1)

                def turn_qk(l, t):
                    n = TILES * l + t
                    pe.wait_ge(s_r, 2 * n + 1)
                    turn(l, t, TQ_, lambda c: rs[:, 2 * c:2 * c + 2, :])
                    pe.wait_ge(s_r, 2 * n + 2)
                    turn(l, t, TK_, lambda c: rs[:, BH + 2 * c:BH + 2 * c + 2, :])

                def windows(p, left, right):
                    for h in range(BH):
                        half = slice(64 * (h % 2), 64 * (h % 2) + 64)
                        at = BANK * (6 + h % 2) + 64 * (h // 2)
                        for w in range(4):
                            mm = nc.tensor.matmul(ps[WIN * w:WIN * (w + 1), at:at + 64], left(half, h // 2, w),
                                                  right(half, h // 2, w), start=True, stop=True)
                    return mm

                def scores(l, t, p):
                    n = TILES * l + t
                    pe.wait_ge(s_halo, n + 1)
                    pe.wait_ge(s_co, n + 1)
                    pe.wait_ge(s_c, emptied(l, TK_, t, 1))
                    pe.sem_inc(M["passed"], 1)
                    windows(p, lambda half, c, w: q_t[half, c, WIN * w:WIN * (w + 1)],
                            lambda half, c, w: k_t[half, p, c, WIN * w:WIN * (w + 2)]).then_inc(s_s, 1)

                def probs_v(l, t, p):
                    n = TILES * l + t
                    pe.wait_ge(s_min, n + 1)
                    pe.wait_ge(s_v2[p], 128 * (n - p) + 512)
                    pe.wait_ge(s_c, emptied(l, PT_, t, 1))
                    pe.sem_inc(M["passed"], 1)
                    windows(p, lambda half, c, w: pt[half, c, WIN * w:WIN * (w + 1)],
                            lambda half, c, w: v2[half, p, w, 64 * c:64 * (c + 1)]).then_inc(s_pv, 1)

                def turn_ctx(l, t):
                    pe.wait_ge(s_co, TILES * l + t + 2)
                    turn(l, t, CT_, lambda c: cn[:, c, :, :])

                def project_out(l, t, last):
                    pe.wait_ge(s_c, emptied(l, CT_, t, 1))
                    pe.wait_ge(s_c, emptied(l, *last, 0))
                    for c in range(PAIRS):
                        mm = nc.tensor.matmul(ring(0)[:, 0:P], w_o[:, c, :], ct[:, c, :],
                                              start=(c == 0), stop=(c == PAIRS - 1))
                    mm.then_inc(s_y, 1)

                def prologue(l):
                    project(l, 0, 0)
                    project(l, 1, 1)
                    turn_qk(l, 0)

                def period(l, t, p):
                    scores(l, t, p)
                    pe.wait_ge(s_yo, TILES * l + t) if not (isinstance(t, int) and t == 0) else None
                    if within(t + 2):
                        project(l, t + 2, p)
                    if within(t - 1):
                        turn_ctx(l, t - 1)
                    pe.wait_ge(s_e, TILES * l + t + 2)
                    turn(l, t, PT_, lambda c: pe_[:, 2 * c:2 * c + 2, :])
                    if within(t + 1):
                        turn_qk(l, t + 1)
                    probs_v(l, t, p)
                    if within(t - 1):
                        project_out(l, t - 1, (TK_, t + 1) if within(t + 1) else (PT_, t))

                def epilogue(l):
                    pe.wait_ge(s_yo, TILES * (l + 1))
                    turn_ctx(l, TILES - 1)
                    project_out(l, TILES - 1, (CT_, TILES - 1))

                def section(l):
                    pe.wait_ge(s_wq, 16 * (l + 1))
                    pe.wait_ge(s_wo, 16 * (l + 1))
                    periods(pe, l, prologue, period, epilogue)
                    cols = lambda t, g: t[:, BANK * g:BANK * (g + 1)]
                    for g in range(G):
                        pe.wait_ge(s_x, 2 * G * l + 2 * g + 2)
                        nc.tensor.matmul(cols(ps, g), M["mean_w"][:], cols(xs, g), start=True, stop=True).then_inc(s_mean, 1)
                    for g in range(G):
                        pe.wait_ge(s_xq, G * l + g + 1)
                        nc.tensor.matmul(cols(ps, g), M["mean_w"][:], cols(xq, g), start=True, stop=True).then_inc(s_var, 1)
                    pe.wait_ge(s_wf, 64 * (l + 1))
                    pe.wait_ge(s_sd, G * (l + 1))
                    for g in range(G):
                        pe.wait_ge(s_xn, G * l + g + 1)
                        for c, (o, m) in enumerate(CH):
                            pe.wait_ge(s_ge, 3 * (G * l + g) + c + 1)
                            nc.tensor.matmul(ps[0:m, BANK * (1 + c):BANK * (2 + c)], w1[:, DI + o:DI + o + m], cols(xs, g),
                                             start=True, stop=True).then_inc(s_g, 1)
                            pe.wait_ge(s_h, 3 * (G * l + g) + c + 1)
                            nc.tensor.matmul(ps[0:m, BANK * (5 + c):BANK * (6 + c)], w1[:, o:o + m], cols(xs, g),
                                             start=True, stop=True).then_inc(s_a, 1)
                        pe.wait_ge(s_fo, G + G * l + g)
                        for c, (o, m) in enumerate(CH):
                            pe.wait_ge(s_h, 3 + 3 * (G * l + g) + c + 1)
                            mm = nc.tensor.matmul(ps[:, 0:BANK], w2[0:m, c, :], hid[0:m, c, :],
                                                  start=(c == 0), stop=(c == 2))
                        mm.then_inc(s_o, 1)
                layers(pe, section)

            @block.scalar
            def _(act):
                def stage(l, t1, p1):
                    n = TILES * l + t1
                    b, at = tile_at(t1)
                    act.wait_ge(s_v, 2 * n + 2)
                    for lo, sh in ((0, 1), (64, 0)):
                        src = xa[lo:lo + 64, ds(b, 1), ds(at + sh, P)].rearrange("p b t -> p (b t)")
                        nc.scalar.copy(xst[lo:lo + 64, p1, :], src).then_inc(s_xst, 1)

                def halo(l, t, p):
                    n = TILES * l + t
                    act.wait_ge(s_s, n + 1)
                    if isinstance(t, int) and t == 0:
                        act.wait_ge(s_c, 160 * l + CREDIT)
                    else:
                        act.wait_ge(s_c, emptied(l, TK_, t - 1, 1))
                    nc.scalar.copy(k_t[:, p, :, 0:WIN], k_t[:, 1 - p, :, P:P + WIN]).then_inc(s_halo, 1)

                def out_of_ring(i, dst):
                    nc.scalar.activation(dst, ring(i), ACT.Identity).then_inc(s_c, 1)

                def squares(l, t, i):
                    act.wait_ge(s_q, 2 * (TILES * l + t) + i + 1)
                    nc.scalar.activation(sq[:, BH * i:BH * (i + 1), :], ps[:, 2 * BANK * i:2 * BANK * (i + 1)],
                                         ACT.Square).then_inc(s_sq, 1)

                def v_out(l, t, p):
                    n = TILES * l + t
                    act.wait_ge(s_v2[p], 128 * (n - p) + 256)
                    act.wait_ge(s_v2[1 - p], 128 * (n + p) + 256)
                    for i in range(2):
                        act.wait_ge(s_v, 4 + 2 * n + i + 1)
                        out_of_ring(i, vt[:, p, i, :])

                def turned_out(l, t, what, dst):
                    for i in range(2):
                        act.wait_ge(s_f, filled(l, what, t, i))
                        out_of_ring(i, dst(slice(4 * i, 4 * i + 4)))

                def exps(l, t):
                    act.wait_ge(s_sub, TILES * l + t + 1)
                    nc.scalar.activation(pe_[:].rearrange("p (c r) e -> p r c e", r=2),
                                         sm[:].rearrange("p (r c) e -> p r c e", r=2), ACT.Exp,
                                         scale=QK_SCALE).then_inc(s_e, 1)

                def qk_out(l, t, p):
                    turned_out(l, t, TQ_, lambda c: q_t[:, c, :])
                    turned_out(l, t, TK_, lambda c: k_t[:, p, c, WIN:])

                def prologue(l):
                    halo(l, 0, 0)
                    for t in range(2):
                        stage(l, t, t)
                        squares(l, t, 0)
                        squares(l, t, 1)
                        v_out(l, t, t)
                    qk_out(l, 0, 0)

                def period(l, t, p):
                    if within(t + 1):
                        halo(l, t + 1, 1 - p)
                    if within(t + 2):
                        stage(l, t + 2, p)
                        squares(l, t + 2, 0)
                    exps(l, t)
                    if within(t + 2):
                        v_out(l, t + 2, p)
                    if within(t - 1):
                        turned_out(l, t - 1, CT_, lambda c: ct[:, c, :])
                    if within(t + 2):
                        squares(l, t + 2, 1)
                    turned_out(l, t, PT_, lambda c: pt[:, c, :])
                    if within(t + 1):
                        qk_out(l, t + 1, 1 - p)

                def epilogue(l):
                    turned_out(l, TILES - 1, CT_, lambda c: ct[:, c, :])

                def section(l):
                    act.wait_ge(s_fo, G * (l + 1))
                    periods(act, l, prologue, period, epilogue)
                    cols = lambda t, g: t[:, BANK * g:BANK * (g + 1)]
                    for g in range(G):
                        b, at = g * BANK // T, g * BANK % T
                        act.wait_ge(s_yo, TILES * l + 4 * g + 5)
                        for lo, sh in ((0, 1), (64, 0)):
                            nc.scalar.copy(xs[lo:lo + 64, BANK * g:BANK * (g + 1)],
                                                  xb[lo:lo + 64, b, at + sh:at + sh + BANK]).then_inc(s_x, 1)
                    for g in range(G):
                        act.wait_ge(s_xc, G * l + g + 1)
                        nc.scalar.activation(cols(xq, g), cols(xc, g), ACT.Square).then_inc(s_xq, 1)
                    for g in range(G):
                        act.wait_ge(s_var, G * l + g + 1)
                        nc.scalar.activation(cols(xq, g), cols(ps, g), ACT.Sqrt, bias=M["eps"][:]).then_inc(s_sd, 1)
                    act.wait_ge(s_wf, 64 * (l + 1))
                    for g in range(G):
                        for c, (o, m) in enumerate(CH):
                            act.wait_ge(s_g, 3 * (G * l + g) + c + 1)
                            act.wait_ge(s_h, 3 * (G * l + g) + c + 1)
                            nc.scalar.activation(gel[0:m, c, :], ps[0:m, BANK * (1 + c):BANK * (2 + c)], ACT.Gelu,
                                                 bias=b1[0:m, 3 + c:4 + c]).then_inc(s_ge, 1)
                act.wait_ge(s_const, 3)
                layers(act, section)

            @block.vector
            def _(dve):
                N_STEPS, S_STEPS, F_STEPS = 13 + 4, 3, 2 * G

                def normed(l, t1):
                    n = TILES * l + t1
                    st = Steps(dve, s_1, N_STEPS * n)
                    dve.wait_ge(s_sq, 2 * n + 2)
                    st.did(V.tensor_reduce(ss[:], sq[:], AX.X, ALU.add))
                    st.wait()
                    st.did(V.tensor_scalar(ss[:], ss[:], 1e-24, None, ALU.max))
                    st.wait()
                    st.did(V.tensor_scalar(yr[:].bitcast(I32), ss[:].bitcast(I32), -0.5, RSQRT_BITS, ALU.mult, ALU.add))
                    st.did(V.tensor_scalar(a_half[:], ss[:], -0.5, None, ALU.mult))
                    st.wait()
                    for _ in range(3):
                        st.did(V.tensor_tensor(tr[:], yr[:], yr[:], ALU.mult))
                        st.wait()
                        st.did(V.tensor_tensor(tr[:], tr[:], a_half[:], ALU.mult))
                        st.wait()
                        st.did(V.scalar_tensor_tensor(out=yr[:], in0=tr[:], scalar=1.5, in1=yr[:], op0=ALU.add, op1=ALU.mult))
                        st.wait()
                    dve.wait_ge(s_cos, 2 * n) if not (isinstance(t1, int) and t1 == 0) else None
                    for i in range(2):
                        V.tensor_tensor(qk[:, BH * i:BH * (i + 1), :],
                                        ps[:, 2 * BANK * i:2 * BANK * (i + 1)].rearrange("p (h e) -> p h e", e=BD),
                                        yr[:, BH * i:BH * (i + 1)].unsqueeze(2).to_broadcast([P, BH, BD]),
                                        ALU.mult).then_inc(s_qn, 1)

                def rotated(l, t1):
                    n = TILES * l + t1
                    st = Steps(dve, s_1, N_STEPS * n)
                    st.n = 13
                    if not (isinstance(t1, int) and t1 == 0):
                        dve.wait_ge(s_f, filled(l, TK_, t1 - 1, 1))
                    H2 = BD // 2
                    for i in range(2):
                        dve.wait_ge(s_qn, 2 * n + i + 3)
                        for a in range(2):
                            b = 1 - a
                            st.did(V.tensor_tensor(
                                rs[:, BH * i:BH * (i + 1), H2 * a:H2 * (a + 1)], qk[:, BH * i:BH * (i + 1), H2 * b:H2 * (b + 1)],
                                rot_l[:, 2 * i + 1, ds(t1 % QT, 1), H2 * a:H2 * (a + 1)].to_broadcast([P, BH, H2]), ALU.mult))
                    st.wait()
                    for i in range(2):
                        dve.wait_ge(s_cos, 2 * n + i + 1)
                        V.tensor_tensor(rs[:, BH * i:BH * (i + 1), :], rs[:, BH * i:BH * (i + 1), :],
                                        rc[:, BH * i:BH * (i + 1), :], ALU.add).then_inc(s_r, 1)
                    assert st.n == N_STEPS, st.n

                def softmax(l, t):
                    n = TILES * l + t
                    st = Steps(dve, s_2, S_STEPS * n)
                    dve.wait_ge(s_s, 2 + n + 1)
                    dve.wait_ge(s_e, n + 1)
                    V.tensor_tensor(sm[:], ps[:, BANK * 6:BANK * 8].rearrange("p (h e) -> p h e", e=2 * WIN),
                                    mask[:, ds(t % QT, 1), :].to_broadcast([P, BH, 2 * WIN]), ALU.min).then_inc(s_min, 1)
                    dve.wait_ge(s_min, n + 1)
                    st.did(V.tensor_reduce(mxb[:], sm[:], AX.X, ALU.max))
                    st.wait()
                    V.tensor_tensor(sm[:], sm[:], mxb[:].unsqueeze(2).to_broadcast([P, BH, 2 * WIN]),
                                    ALU.subtract).then_inc(s_sub, 1)

                def row_sums(l, t):
                    n = TILES * l + t
                    st = Steps(dve, s_2, S_STEPS * n)
                    st.n = 1
                    dve.wait_ge(s_e, n + 2)
                    st.did(V.tensor_reduce(sumb[:], pe_[:], AX.X, ALU.add))
                    st.wait()
                    st.did(V.reciprocal(rsum[:], sumb[:]))

                def context(l, t):
                    n = TILES * l + t
                    dve.wait_ge(s_2, S_STEPS * (n + 1))
                    dve.wait_ge(s_pv, 2 + n + 1)
                    for r in range(2):
                        ins = V.tensor_tensor(
                            cn[:, :, r, :], ps[:, BANK * (6 + r):BANK * (7 + r)].rearrange("p (c e) -> p c e", e=BD),
                            rsum[:].rearrange("p (c r) -> p r c", r=2)[:, r, :].unsqueeze(2).to_broadcast([P, PAIRS, BD]),
                            ALU.mult)
                    ins.then_inc(s_co, 1)

                def added(l, t):
                    n = TILES * l + t
                    b, at = tile_at(t)
                    dve.wait_ge(s_y, n + 1)
                    x = lambda s: s[:, ds(b, 1), ds(at + 1, P)].rearrange("p b t -> p (b t)")
                    V.tensor_tensor(x(xb), x(xa), ring(0)[:, 0:P], ALU.add).then_inc(s_yo, 1)

                def prologue(l):
                    for t in range(2):
                        normed(l, t)
                        rotated(l, t)

                def period(l, t, p):
                    softmax(l, t)
                    row_sums(l, t)
                    if within(t + 2):
                        normed(l, t + 2)
                    context(l, t)
                    if within(t + 2):
                        rotated(l, t + 2)
                    if within(t - 1):
                        added(l, t - 1)

                def epilogue(l):
                    added(l, TILES - 1)

                def section(l):
                    dve.wait_ge(s_rot, 4 * (l + 1))
                    periods(dve, l, prologue, period, epilogue)
                    cols = lambda t, g: t[:, BANK * g:BANK * (g + 1)]
                    st = Steps(dve, s_rd, F_STEPS * l)
                    for g in range(G):
                        dve.wait_ge(s_mean, G * l + g + 1)
                        V.tensor_tensor(cols(xc, g), cols(xs, g), cols(ps, g), ALU.subtract).then_inc(s_xc, 1)
                    dve.wait_ge(s_wf, 64 * (l + 1))
                    for g in range(G):
                        dve.wait_ge(s_sd, G * l + g + 1)
                        st.did(V.reciprocal(cols(xq, g), cols(xq, g)))
                        st.wait()
                        st.did(V.tensor_tensor(cols(xc, g), cols(xc, g), cols(xq, g), ALU.mult))
                        st.wait()
                        V.tensor_scalar(cols(xs, g), cols(xc, g), vecs[:, 0:1], vecs[:, 1:2], ALU.mult, ALU.add).then_inc(s_xn, 1)
                    for g in range(G):
                        b, at = g * BANK // T, g * BANK % T
                        for c, (o, m) in enumerate(CH):
                            dve.wait_ge(s_ge, 3 + 3 * (G * l + g) + c + 1)
                            dve.wait_ge(s_a, 3 * (G * l + g) + c + 1)
                            dve.wait_ge(s_o, G * l + g + 1)
                            V.scalar_tensor_tensor(out=hid[0:m, c, :], in0=ps[0:m, BANK * (5 + c):BANK * (6 + c)],
                                                   scalar=b1[0:m, c:c + 1], in1=gel[0:m, c, :],
                                                   op0=ALU.add, op1=ALU.mult).then_inc(s_h, 1)
                        dve.wait_ge(s_o, 1 + G * l + g + 1)
                        V.scalar_tensor_tensor(out=xa[:, b, 1 + at:1 + at + BANK], in0=ps[:, 0:BANK], scalar=vecs[:, 2:3],
                                               in1=xb[:, b, 1 + at:1 + at + BANK], op0=ALU.add, op1=ALU.add).then_inc(s_fo, 1)
                dve.wait_ge(s_const, 3)
                layers(dve, section)


def join(nc, A, M, out):
    ps = M["ps"]
    V = nc.vector
    with ExitStack() as own:
        sb = lambda n, s: own.enter_context(nc.sbuf_tensor(n, s, F32))
        sem = lambda n: own.enter_context(nc.semaphore(n))
        x0, w, bias = sb("x_again", [P, TOK]), sb("w_out_a", [P, P]), sb("b_out_a", [P, 1])
        ct, y = sb("ctx_a_t", [P, TOK]), sb("y", [P, TOK])
        s_ld, s_t, s_te, s_y, s_1, s_out = (sem(n) for n in (
            "join_loads", "join_turned", "join_turned_out", "join_projected", "join_added", "join_stores"))
        col = lambda t, g: t[:, BANK * g:BANK * (g + 1)]
        with nc.Block() as block:

            @block.sync
            def _(sp):
                for t, a in ((x0, "x_t"), (w, "a_wo"), (bias, "a_bo")):
                    sp.dma_start(t[:], A[a]).then_inc(s_ld, 16)
                for g in range(G):
                    sp.wait_ge(s_1, 3 * g + 3)
                    sp.dma_start(out[:, BANK * g:BANK * (g + 1)], col(y, g)).then_inc(s_out, 16)
                sp.wait_ge(s_out, 16 * G)

            @block.tensor
            def _(pe):
                for g in range(G):
                    for t in range(4 * g, 4 * g + 4):
                        mm = nc.tensor.transpose(ps[:, P * t:P * (t + 1)], M["ctx"][:, t, :], M["ident"][:])
                    mm.then_inc(s_t, 1)
                pe.wait_ge(s_ld, 48)
                for g in range(G):
                    pe.wait_ge(s_te, g + 1)
                    nc.tensor.matmul(ps[:, BANK * (4 + g):BANK * (5 + g)], w[:], col(ct, g), start=True, stop=True).then_inc(s_y, 1)

            @block.scalar
            def _(act):
                for g in range(G):
                    act.wait_ge(s_t, g + 1)
                    nc.scalar.activation(col(ct, g), col(ps, g), ACT.Identity).then_inc(s_te, 1)

            @block.vector
            def _(dve):
                dve.wait_ge(s_ld, 48)
                for g in range(G):
                    b, at = g * BANK // T, g * BANK % T
                    dve.wait_ge(s_y, g + 1)
                    V.tensor_scalar(col(y, g), ps[:, BANK * (4 + g):BANK * (5 + g)], bias[:], None, ALU.add).then_inc(s_1, 1)
                    dve.wait_ge(s_1, 3 * g + 1)
                    V.tensor_tensor(col(y, g), col(y, g), col(x0, g), ALU.add).then_inc(s_1, 1)
                    dve.wait_ge(s_1, 3 * g + 2)
                    V.tensor_tensor(col(y, g), col(y, g), M["xa"][:, b, 1 + at:1 + at + BANK], ALU.add).then_inc(s_1, 1)


def build(nc, A, out):
    with ExitStack() as ctx:
        sb = lambda n, s, d=F32: ctx.enter_context(nc.sbuf_tensor(n, s, d))
        M = {
            "ps": ctx.enter_context(nc.psum_tensor("ps", [P, 8 * BANK], F32)),
            "ident": sb("ident", [P, P]), "mean_w": sb("mean_w", [P, P]), "eps": sb("eps", [P, 1]),
            "xa": sb("stream_a", [P, B, T + 1]), "ctx": sb("ctx_a", [P, TILES, P]),
        }
        M["passed"] = ctx.enter_context(nc.semaphore("waits_passed"))
        with ExitStack() as own:
            sa = lambda n, s, d=F32: own.enter_context(nc.sbuf_tensor(n, s, d))
            M.update({
                "hmask": sa("head_mask", [P, HEADS]), "iota8": sa("iota8", [P, 8]),
                "q_t": sa("q_t", [P, TOK]), "k_t": sa("k_t", [P, TOK]), "v": sa("v_a", [P, TILES, P]),
                "vh": sa("v_head", [P, 2, KBLK, HD + 1]), "flags": sa("flags", [P, UNITS]),
            })
            for name in ("pt_out", "pv_done", "ctx_out"):
                M[name] = own.enter_context(nc.semaphore(name))
            front(nc, own, A, M)
            topk_attention(nc, own, M)
            repair(nc, M)
        M["xb"] = sb("stream_b", [P, B, T + 1])
        with ExitStack() as own:
            local_transformer(nc, own, A, M)
        join(nc, A, M, out)


def _tables():
    import numpy as np

    f = np.float32
    half = np.arange(0, BD, 2, dtype=f)
    inv_freq = (f(1.0) / f(10000.0) ** (half / f(BD))).astype(f)
    t = np.arange(T, dtype=f)
    freqs = (t[:, None] * inv_freq[None, :]).astype(f)
    base = ((half + f(0.4 * BD)) / f(1.4 * BD)).astype(f)
    power = ((t - T // 2) / f(WIN // 2)).astype(f)
    scale = (base[None, :] ** power[:, None]).astype(f)
    cos, sin = np.cos(freqs), np.sin(freqs)
    both = lambda a, b: np.concatenate([a, b], -1)
    rot = np.stack([both(cos * scale, cos * scale), both(-sin * scale, sin * scale),
                    both(cos / scale, cos / scale), both(-sin / scale, sin / scale)], 0).astype(f)
    rot = rot.reshape(4, QT, P, BD).transpose(2, 0, 1, 3)
    i, j = np.arange(P)[:, None] % WIN, np.arange(2 * WIN)[None, :]
    seen = (j <= i + WIN) & (j >= i)
    big = np.where(seen, f(3.0e38), f(MASKED)).astype(f)
    masks = np.broadcast_to(big[:, None, :], (P, QT, 2 * WIN)).copy()
    masks[:WIN, 0, :WIN] = MASKED
    return {
        "c_hmask": (np.arange(P)[:, None] // HD == np.arange(HEADS)[None, :]).astype(f),
        "c_ident": np.eye(P, dtype=f),
        "c_iota8": np.broadcast_to(np.arange(8, dtype=f), (P, 8)),
        "b_rot": rot, "b_mask": masks,
    }


def _layout(inputs):
    import numpy as np

    v = {k: np.asarray(a) for k, a in inputs.items()}
    w, b = v["L0_attn_qkv_w"], v["L0_attn_qkv_b"]
    rows = lambda a: np.broadcast_to(a, (P,) + a.shape)
    wq = v["L0_ffn_Wqkv"]
    wv = wq[:, :, 2 * INNER:].reshape(DEPTH, P, PAIRS, 2, BD).transpose(0, 1, 3, 2, 4).reshape(DEPTH, P, INNER)
    qs, ks = v["L0_ffn_q_scale"], v["L0_ffn_k_scale"]
    scales = np.stack([qs, np.roll(qs, BD // 2, 1), ks, np.roll(ks, BD // 2, 1)], 1)
    w2 = np.zeros((DEPTH, 3 * P, P), np.float32)
    w2[:, :DI] = v["L0_ffn_W2"]
    b1 = np.zeros((DEPTH, 2, 3 * P), np.float32)
    b1[:, :, :DI] = v["L0_ffn_b1"].reshape(DEPTH, 2, DI)
    return {
        "x_t": v["L0_attn_x"].reshape(TOK, P).T, "a_w": w.T, "a_bq": b[:P, None], "a_bk": b[P:2 * P, None],
        "a_bv": rows(b[2 * P:]), "a_wo": v["L0_attn_out_w"].T, "a_bo": v["L0_attn_out_b"][:, None],
        "b_wqkv": np.concatenate([wq[:, :, :2 * INNER], wv], 2),
        "b_scales": np.broadcast_to(scales[:, None], (DEPTH, P, 4, BD)),
        "b_wo": v["L0_ffn_Wo"].reshape(DEPTH, PAIRS, P, P).transpose(0, 2, 1, 3),
        "b_w1": v["L0_ffn_W1"], "b_w2": w2.reshape(DEPTH, 3, P, P).transpose(0, 2, 1, 3),
        "b_b1": b1.reshape(DEPTH, 6, P).transpose(0, 2, 1),
        "b_vecs": np.stack([v["L0_ffn_ln_g"], v["L0_ffn_ln_b"], v["L0_ffn_b2"]], 2),
    }


def kernel(**inputs):
    import numpy as np
    import concourse.bacc as bacc
    from concourse.bass_utils import run_bass_kernel_spmd

    nc = bacc.Bacc("TRN2", target_bir_lowering=False, num_devices=1)
    arrays = {k: np.ascontiguousarray(a) for k, a in {**_layout(inputs), **_tables()}.items()}
    A = {k: nc.dram_tensor(k, a.shape, F32, kind="ExternalInput").ap() for k, a in arrays.items()}
    out = nc.dram_tensor("out_t", (P, TOK), F32, kind="ExternalOutput").ap()
    build(nc, A, out)
    r = run_bass_kernel_spmd(nc, [arrays], core_ids=[0])
    return np.ascontiguousarray(r.results[0]["out_t"].T).reshape(B, T, P)
```

```python
from contextlib import ExitStack

import concourse.bass as bass
from concourse import mybir

F32 = mybir.dt.float32
BF16 = mybir.dt.bfloat16
I32 = mybir.dt.int32
ALU = mybir.AluOpType
ACT = mybir.ActivationFunctionType
AX = mybir.AxisListType
ds = bass.ds

P = 128
BANK = 512
EPS = 1e-5

B, T = 2, 1024
TOK = B * T
TILES = TOK // P
HEADS, HD = 16, 8
K_TOP = int(0.7 * T)
FILL = -10000.0
GROUPS = B * HEADS
QT = T // P
HALF = QT // 2
KBLK = T // P
UNITS = GROUPS * QT
SC = 2.0 ** -40
EXP_SCALE = HD ** -0.5 / SC
Z = -0.5221
DENSITY = 0.3481
WINDOW = 8
SQRT_BITS = float(0x1fbd1df5)
NEXT_UP = 2.0 ** -24 * 1.0001


class Steps:

    def __init__(self, eng, sem, base=0):
        self.eng, self.sem, self.base, self.n = eng, sem, base, 0

    def did(self, ins):
        self.n += 1
        ins.then_inc(self.sem, 1)

    def wait(self):
        self.eng.wait_ge(self.sem, self.base + self.n)


def front(nc, ctx, A, M):
    sb = lambda n, s, d=F32: ctx.enter_context(nc.sbuf_tensor(n, s, d))
    sem = lambda n: ctx.enter_context(nc.semaphore(n))
    ps = M["ps"]
    with ExitStack() as own:
        osb = lambda n, s, d=F32: own.enter_context(nc.sbuf_tensor(n, s, d))
        x0 = osb("x0", [P, TOK])
        xc = osb("xc", [P, TOK])
        sq = osb("sq", [P, TOK])
        xn = osb("xn", [P, TOK])
        w = osb("w_qkv_a", [P, 3 * P])
        bq = osb("bq", [P, 1])
        bk = osb("bk", [P, 1])
        bqs = osb("bqs", [P, 1])
        bv = osb("bv", [P, P])
        s_ld = sem("front_loads")
        s_set = sem("front_constants")
        s_mean = sem("front_mean")
        s_xc = sem("front_centred")
        s_sq = sem("front_squared")
        s_var = sem("front_var")
        s_sd = sem("front_sd")
        s_rs = sem("front_rstd")
        s_xn = sem("front_normed")
        s_qk = sem("front_qk")
        s_qke = sem("front_qk_out")
        s_v = sem("front_v")
        s_ve = sem("front_v_out")
        s_end = sem("front_credits")
        G = TOK // BANK
        col = lambda t, g: t[:, BANK * g:BANK * (g + 1)]
        bank = lambda b: ps[:, BANK * b:BANK * (b + 1)]
        with nc.Block() as block:

            @block.sync
            def _(sp):
                loads = [(x0, A["x_t"]), (w, A["a_w"]), (bq, A["a_bq"]), (bk, A["a_bk"]), (bv, A["a_bv"]),
                         (M["hmask"], A["c_hmask"]), (M["ident"], A["c_ident"]), (M["iota8"], A["c_iota8"])]
                for t, a in loads:
                    sp.dma_start(t[:], a).then_inc(s_ld, 16)
                for name in ("pt_out", "pv_done", "ctx_out"):
                    sp.sem_inc(M[name], 2)
                sp.wait_ge(s_ld, 16 * len(loads))
                sp.nop().then_inc(s_end, 1)

            @block.vector
            def _(dve):
                nc.vector.memset(M["mean_w"][:], 1.0 / P).then_inc(s_set, 1)
                nc.vector.memset(M["eps"][:], EPS).then_inc(s_set, 1)
                nc.vector.memset(M["xa"][:], 0.0).then_inc(s_set, 1)
                nc.vector.memset(M["vh"][:], 1.0).then_inc(s_set, 1)
                nc.vector.memset(M["flags"][:], 0.0).then_inc(s_set, 1)
                dve.wait_ge(s_end, 1)
                nc.vector.tensor_scalar(bqs[:], bq[:], SC, None, ALU.mult).then_inc(s_set, 1)
                for g in range(G):
                    dve.wait_ge(s_mean, g + 1)
                    nc.vector.tensor_tensor(col(xc, g), col(x0, g), bank(g), ALU.subtract).then_inc(s_xc, 1)
                for g in range(G):
                    dve.wait_ge(s_sd, g + 1)
                    nc.vector.reciprocal(col(sq, g), col(sq, g)).then_inc(s_rs, 1)
                    dve.wait_ge(s_rs, g + 1)
                    nc.vector.tensor_tensor(col(xn, g), col(xc, g), col(sq, g), ALU.mult).then_inc(s_xn, 1)
                for g in range(G):
                    dve.wait_ge(s_v, 4 * g + 4)
                    nc.vector.tensor_tensor(
                        M["v"][:, 4 * g:4 * g + 4, :], bank(g).rearrange("p (t f) -> p t f", t=4),
                        bv[:].unsqueeze(1).to_broadcast([P, 4, P]), ALU.add).then_inc(s_ve, 1)

            @block.tensor
            def _(pe):
                pe.wait_ge(s_end, 1)
                pe.wait_ge(s_set, 1)
                for g in range(G):
                    nc.tensor.matmul(bank(g), M["mean_w"][:], col(x0, g), start=True, stop=True).then_inc(s_mean, 1)
                for g in range(G):
                    pe.wait_ge(s_sq, g + 1)
                    nc.tensor.matmul(bank(4 + g), M["mean_w"][:], col(sq, g), start=True, stop=True).then_inc(s_var, 1)
                for g in range(G):
                    pe.wait_ge(s_xn, g + 1)
                    nc.tensor.matmul(bank(g), w[:, 0:P], col(xn, g), start=True, stop=True).then_inc(s_qk, 1)
                    nc.tensor.matmul(bank(4 + g), w[:, P:2 * P], col(xn, g), start=True, stop=True).then_inc(s_qk, 1)
                for t in range(TILES):
                    if t % 4 == 0:
                        pe.wait_ge(s_qke, 2 * (t // 4) + 2)
                    nc.tensor.matmul(ps[:, P * t:P * (t + 1)], xn[:, P * t:P * (t + 1)], w[:, 2 * P:3 * P],
                                     start=True, stop=True).then_inc(s_v, 1)

            @block.scalar
            def _(act):
                act.wait_ge(s_set, 6)
                for g in range(G):
                    act.wait_ge(s_xc, g + 1)
                    nc.scalar.activation(col(sq, g), col(xc, g), ACT.Square).then_inc(s_sq, 1)
                for g in range(G):
                    act.wait_ge(s_var, g + 1)
                    nc.scalar.activation(col(sq, g), bank(4 + g), ACT.Sqrt, bias=M["eps"][:]).then_inc(s_sd, 1)
                for g in range(G):
                    act.wait_ge(s_qk, 2 * g + 2)
                    nc.scalar.activation(col(M["q_t"], g), bank(g), ACT.Identity, bias=bqs[:], scale=SC).then_inc(s_qke, 1)
                    nc.scalar.activation(col(M["k_t"], g), bank(4 + g), ACT.Identity, bias=bk[:]).then_inc(s_qke, 1)

            @block.gpsimd
            def _(pool):
                for g in range(G):
                    pool.wait_ge(s_xn, g + 1)
                    if g == 0:
                        pool.wait_ge(s_set, 3)
                    b, at = g * BANK // T, g * BANK % T
                    nc.gpsimd.tensor_copy(M["xa"][:, b, 1 + at:1 + at + BANK], col(xn, g))


def topk_attention(nc, ctx, M):
    ps = M["ps"]
    sem = lambda n: ctx.enter_context(nc.semaphore(n))
    s_qm = sem("qm_ready")
    s_vh = sem("vh_ready")
    s_sc = sem("scores_ready")
    s_ev = sem("scores_in_sbuf")
    s_nt = sem("threshold_ready")
    s_ct = sem("count_ready")
    s_mx = sem("exp_bias_ready")
    s_ex = sem("exp_ready")
    s_sg = sem("sign_ready")
    s_u = sem("signed_ready")
    s_yp = sem("pushed_ready")
    s_p = sem("probs_ready")
    s_pt = sem("probs_t_ready")
    s_h = sem("dve_head_steps")
    s_t = sem("dve_tail_steps")
    s_c = sem("dve_context_steps")
    s_pe, s_pv, s_cx = (M[n] for n in ("pt_out", "pv_done", "ctx_out"))
    with ExitStack() as own:
        sb = lambda n, s, d=F32: own.enter_context(nc.sbuf_tensor(n, s, d))
        S = sb("scores", [P, 2, QT, T])
        E = sb("exps", [P, QT, T])
        U = sb("signed", [P, 4, T])
        Y = sb("pushed", [P, 2, T])
        PT = sb("probs_t", [P, 2, KBLK, P])
        junk_a = sb("junk_act", [P, QT, T], BF16)
        junk_d = U[:].bitcast(BF16).rearrange("p a (b t) -> p (a b) t", b=2)
        qm = sb("q_masked", [P, 2, T])
        st = lambda n: sb(n, [P, 2, QT])
        tot, cnt, mx, nb = (st(n) for n in ("row_sum", "count", "row_max", "exp_bias"))
        pt = sb("points", [P, 2, 4, 2, QT])
        step, diff, diff2 = (sb(n, [P, 2, QT]) for n in ("step", "diff", "diff_far"))
        sig, tmp = sb("sigma", [P, QT]), sb("tmp", [P, QT])
        cross = sb("crossed", [P, 2, QT], I32)
        side, sgn, x, nud, idx, idx2 = (st(n) for n in ("side", "sgn", "signed_thr", "nudged", "idx", "idx_next"))
        thr, num, kth, nxt, flag, reach = (st(n) for n in ("thr", "exact_num", "kth", "next_value", "flag", "reach"))
        bn = sb("bn", [P, 2, QT, 6])
        top8 = sb("top8", [P, QT, 8])
        hit = sb("hit", [P, QT, 8])
        pick = sb("pick", [P, QT, 8])
        rden = sb("rden", [P, QT])

        def within(n):
            return not isinstance(n, int) or 0 <= n < GROUPS

        def scores(pe, n, g, tiles):
            b = n // HEADS
            pe.wait_ge(s_qm, n + 1)
            for j in tiles:
                if not (isinstance(n, int) and 8 * n + j < 2):
                    pe.wait_ge(s_ev, QT * n + j - 1)
                for h in range(2):
                    mm = nc.tensor.matmul(ps[:, BANK * (2 * (j % 2) + h):BANK * (2 * (j % 2) + h + 1)],
                                          qm[:, g, P * j:P * (j + 1)],
                                          M["k_t"][:, ds(b * T + BANK * h, BANK)], start=True, stop=True)
                mm.then_inc(s_sc, 1)

        def probs_t(pe, n, j):
            pe.wait_ge(s_p, QT * n + j + 1)
            for h in range(2):
                pe.wait_ge(s_pe, 2 * QT * n + 2 * j + h + 1)
                for c in range(4):
                    mm = nc.tensor.transpose(ps[:, BANK * (4 + h) + P * c:BANK * (4 + h) + P * (c + 1)],
                                             E[:, j, P * (4 * h + c):P * (4 * h + c + 1)], M["ident"][:])
                mm.then_inc(s_pt, 1)

        def pv(pe, n, g, j):
            if j == 0:
                pe.wait_ge(s_vh, n + 1)
            if j == 0:
                pe.wait_ge(s_cx, n + 2)
            pe.wait_ge(s_pe, 2 * QT * n + 2 * j + 4)
            o = BANK * (6 + j // HALF) + 16 * (j % HALF)
            for c in range(KBLK):
                mm = nc.tensor.matmul(ps[:, o:o + HD + 1], PT[:, j % 2, c, :], M["vh"][:, g, c, :],
                                      start=(c == 0), stop=(c == KBLK - 1))
            mm.then_inc(s_pv, 1)

        def turn_ahead(pe, n, g, tiles):
            for j in tiles:
                if j < QT:
                    probs_t(pe, n, j)
                if j > 0:
                    pv(pe, n, g, j - 1)

        AHEAD = 2

        def pe_period(pe, n, g):
            if within(n + 2):
                scores(pe, n + 2, g, range(0, 2))
            if within(n - 1):
                turn_ahead(pe, n - 1, 1 - g, range(AHEAD, QT + 1))
            for j, last in ((0, 5), (1, QT)):
                if within(n + 2):
                    scores(pe, n + 2, g, range(2 + 3 * j, last))
                if within(n):
                    turn_ahead(pe, n, g, (j,))

        def evacuate(act, n, g, tiles):
            for j in tiles:
                if not (isinstance(n, int) and n < 2):
                    act.wait_ge(s_p, QT * n - 2 * QT + j + 1)
                act.wait_ge(s_sc, QT * n + j + 1)
                nc.scalar.activation(S[:, g, j, :], ps[:, 2 * BANK * (j % 2):2 * BANK * (j % 2 + 1)], ACT.Identity,
                                     accum_out=tot[:, g, j:j + 1]).then_inc(s_ev, 1)

        def count(act, n, g, k, tiles):
            if tiles[0] == 0:
                act.wait_ge(s_nt, 4 * n + k + 1)
                if not (isinstance(n, int) and n + k == 0):
                    act.wait_ge(s_ct, 3 * n + k)
            for j in tiles:
                ins = nc.scalar.activation(junk_a[:, j, :], S[:, g, j, :], ACT.Sign, bias=pt[:, g, k, 0, j:j + 1],
                                           accum_out=cnt[:, g, j:j + 1])
            if tiles[-1] == QT - 1:
                ins.then_inc(s_ct, 1)

        def exps(act, n, g, j):
            act.wait_ge(s_mx, n + 1)
            nc.scalar.activation(E[:, j, :], S[:, g, j, :], ACT.Exp, bias=nb[:, g, j:j + 1],
                                 scale=EXP_SCALE).then_inc(s_ex, 1)

        def evacuate_t(act, n, j):
            act.wait_ge(s_pv, QT * n + j + 1)
            for h in range(2):
                act.wait_ge(s_pt, 2 * QT * n + 2 * j + h + 1)
                nc.scalar.activation(PT[:, j % 2, 4 * h:4 * h + 4, :], ps[:, BANK * (4 + h):BANK * (5 + h)],
                                     ACT.Identity).then_inc(s_pe, 1)

        def signed(act, n, g, tiles):
            for j in tiles:
                act.wait_ge(s_sg, n + 1)
                if not (isinstance(n, int) and n == 0 and j < 4):
                    act.wait_ge(s_yp, QT * n + j - 3)
                nc.scalar.activation(U[:, j % 4, :], S[:, g, j, :], ACT.Identity, scale=sgn[:, g, j:j + 1]).then_inc(s_u, 1)

        ONE, TWO, TILE, SIGN = range(4)
        PLAN = ((TILE, 3), (ONE, 4), (TILE, 1), (ONE, 4), (SIGN, 4), (TILE, 1), (TWO, 2), (SIGN, 2), (TILE, 1),
                (TWO, 1), (SIGN, 2), (TILE, 1), (TWO, 5), (TILE, 1))

        def act_period(act, n, g):
            done = [0] * 4
            for what, m in PLAN:
                tiles = range(done[what], done[what] + m)
                done[what] += m
                if what in (ONE, TWO) and within(n + 1):
                    count(act, n + 1, 1 - g, what, tiles)
                elif what == SIGN and within(n):
                    signed(act, n, g, tiles)
                elif what == TILE:
                    for j in tiles:
                        if within(n - 1) and j >= AHEAD:
                            evacuate_t(act, n - 1, j)
                        if within(n):
                            exps(act, n, g, j)
            for j in range(QT):
                if within(n + 2):
                    evacuate(act, n + 2, g, (j,))
                if within(n + 1):
                    count(act, n + 1, 1 - g, 2, (j,))
                if within(n) and j in (4, QT - 1):
                    evacuate_t(act, n, 0 if j == 4 else 1)

        V = nc.vector

        def first_threshold(dve, own_, n, g):
            for j in range(QT):
                dve.wait_ge(s_ev, QT * n + j + 1)
                ins = V.bn_stats(bn[:, g, j, :], S[:, g, j, 0:P])
            own_.did(ins)
            own_.wait()
            own_.did(V.tensor_tensor(sig[:], bn[:, g, :, 2], bn[:, g, :, 5], ALU.add))
            own_.wait()
            own_.did(V.tensor_scalar(sig[:].bitcast(I32), sig[:].bitcast(I32), 0.5,
                                     SQRT_BITS - 3.5 * 2 ** 23, ALU.mult, ALU.add))
            own_.wait()
            own_.did(V.tensor_scalar(tmp[:], sig[:], -Z, None, ALU.mult))
            own_.did(V.tensor_scalar(step[:, 0, :], sig[:], 1.0 / (2 * T * DENSITY), None, ALU.mult))
            own_.did(V.memset(step[:, 1, :], 1.0))
            own_.wait()
            V.scalar_tensor_tensor(out=pt[:, g, 0, 0, :], in0=tot[:, g, :], scalar=-1.0 / T, in1=tmp[:],
                                   op0=ALU.mult, op1=ALU.add).then_inc(s_nt, 1)

        def next_threshold(dve, own_, n, g, k):
            new, old = pt[:, g, k], pt[:, g, max(k - 1, 0)]
            dve.wait_ge(s_ct, 3 * n + k + 1)
            own_.did(V.tensor_scalar(pt[:, g, k, 1, :], cnt[:, g, :], float(T - 2 * K_TOP), None, ALU.add))
            own_.wait()
            if k > 0:
                own_.did(V.tensor_tensor(diff[:], new, old, ALU.subtract))
                own_.did(V.tensor_tensor(tmp[:], new[:, 1, :], old[:, 1, :], ALU.mult))
                own_.wait()
                own_.did(V.tensor_scalar(cross[:, k - 1, :], tmp[:], 0.0, None, ALU.is_lt))
                crossed = lambda c: cross[:, c, :].unsqueeze(1).to_broadcast([P, 2, QT])
                if k == 2:
                    own_.did(V.tensor_tensor(diff2[:], diff[:], step[:], ALU.add))
                    own_.wait()
                    dve.sem_inc(M["passed"], 1)
                    own_.did(V.copy_predicated(step[:], crossed(0), diff2[:]))
                own_.wait()
                dve.sem_inc(M["passed"], 1)
                own_.did(V.copy_predicated(step[:], crossed(k - 1), diff[:]))
                own_.wait()
            own_.did(V.reciprocal(tmp[:], step[:, 1, :]))
            own_.wait()
            own_.did(V.tensor_tensor(tmp[:], tmp[:], step[:, 0, :], ALU.mult))
            own_.wait()
            own_.did(V.tensor_tensor(tmp[:], tmp[:], pt[:, g, k, 1, :], ALU.mult))
            own_.wait()
            V.tensor_tensor(pt[:, g, k + 1, 0, :], pt[:, g, k, 0, :], tmp[:], ALU.subtract).then_inc(s_nt, 1)

        def row_max(dve, own_, n, g):
            for j in range(QT):
                ins = V.tensor_reduce(mx[:, g, j:j + 1], S[:, g, j, :], AX.X, ALU.max)
            own_.did(ins)
            own_.wait()
            V.tensor_scalar(nb[:, g, :], mx[:, g, :], -EXP_SCALE, None, ALU.mult).then_inc(s_mx, 1)

        def exact_count(dve, own_, n, g):
            c = slice(0, QT)
            dve.wait_ge(s_nt, 4 * n + 4)
            own_.did(V.tensor_scalar(thr[:, g, c], pt[:, g, 3, 0, c], -1.0, None, ALU.mult))
            own_.wait()
            for j in range(QT):
                ins = V.tensor_scalar(junk_d[:, j, :], S[:, g, j, :], thr[:, g, j:j + 1], None, ALU.is_ge, ALU.add,
                                      accum_out=num[:, g, j:j + 1])
            own_.did(ins)
            own_.wait()
            own_.did(V.tensor_scalar(side[:, g, c], num[:, g, c], K_TOP - 0.5, None, ALU.is_ge))
            own_.wait()
            V.tensor_scalar(sgn[:, g, c], side[:, g, c], -2.0, 1.0, ALU.mult, ALU.add).then_inc(s_sg, 1)
            dve.wait_ge(s_sg, n + 1)
            own_.did(V.tensor_tensor(x[:, g, c], sgn[:, g, c], thr[:, g, c], ALU.mult))
            own_.did(V.scalar_tensor_tensor(out=idx[:, g, c], in0=num[:, g, c], scalar=K_TOP - 0.5, in1=sgn[:, g, c],
                                            op0=ALU.subtract, op1=ALU.mult))
            own_.wait()
            own_.did(V.scalar_tensor_tensor(out=nud[:, g, c], in0=x[:, g, c], scalar=-1.0, in1=x[:, g, c],
                                            op0=ALU.mult, op1=ALU.max))
            own_.did(V.tensor_scalar(idx[:, g, c], idx[:, g, c], -1.0, -0.5, ALU.mult, ALU.add))
            own_.wait()
            own_.did(V.scalar_tensor_tensor(out=nud[:, g, c], in0=nud[:, g, c], scalar=NEXT_UP, in1=side[:, g, c],
                                            op0=ALU.mult, op1=ALU.mult))
            own_.did(V.tensor_tensor(idx2[:, g, c], idx[:, g, c], sgn[:, g, c], ALU.add))
            own_.wait()
            own_.did(V.tensor_tensor(nud[:, g, c], nud[:, g, c], x[:, g, c], ALU.add))
            own_.wait()

        def near_values(dve, own_, n, g, batch):
            def pushed(j):
                dve.wait_ge(s_u, QT * n + j + 1)
                V.scalar_tensor_tensor(out=Y[:, j % 2, :], in0=U[:, j % 4, :], scalar=nud[:, g, j:j + 1],
                                       in1=U[:, j % 4, :], op0=ALU.is_ge, op1=ALU.subtract,
                                       reverse1=True).then_inc(s_yp, 1)

            def largest(j):
                own_.did(V.max(top8[:, j, :], Y[:, j % 2, :]))

            def both(step, b):
                step(2 * b)
                step(2 * b + 1)

            if batch == 0:
                both(pushed, 0)
            dve.wait_ge(s_yp, QT * n + 2 * batch + 2)
            dve.sem_inc(M["passed"], 1)
            both(largest, batch)
            own_.wait()
            if batch < QT // 2 - 1:
                both(pushed, batch + 1)

        def hits(g, at):
            return V.tensor_tensor(hit[:], M["iota8"][:].unsqueeze(1).to_broadcast([P, QT, 8]),
                                   at[:, g, :].unsqueeze(2).to_broadcast([P, QT, 8]), ALU.is_equal)

        def select(dve, own_, n, g):
            own_.did(hits(g, idx))
            own_.wait()
            own_.did(V.tensor_tensor(pick[:], hit[:], top8[:], ALU.mult))
            own_.wait()
            own_.did(V.tensor_reduce(kth[:, g, :], pick[:], AX.X, ALU.add))
            own_.wait()
            own_.did(V.tensor_tensor(thr[:, g, :], kth[:, g, :], sgn[:, g, :], ALU.mult))
            own_.wait()

        def flag_step(own_, n, g, step):
            flag_if = lambda value, bound, op: V.scalar_tensor_tensor(
                out=flag[:, g, :], in0=value[:, g, :], scalar=bound, in1=flag[:, g, :], op0=op, op1=ALU.add)
            if step == 0:
                own_.did(hits(g, idx2))
                own_.did(V.tensor_scalar(flag[:, g, :], tot[:, g, :], -(2.0 ** -2), None, ALU.is_lt))
            elif step == 1:
                own_.did(V.tensor_tensor(pick[:], hit[:], top8[:], ALU.mult))
                own_.did(V.tensor_tensor(reach[:, g, :], idx[:, g, :], side[:, g, :], ALU.subtract))
            elif step == 2:
                own_.did(V.tensor_reduce(nxt[:, g, :], pick[:], AX.X, ALU.add))
                own_.did(flag_if(reach, WINDOW - 1.5, ALU.is_gt))
            elif step == 3:
                own_.did(V.tensor_tensor(nxt[:, g, :], kth[:, g, :], nxt[:, g, :], ALU.is_equal))
                own_.did(flag_if(mx, 2.0 ** -13, ALU.is_gt))
            elif step == 4:
                own_.did(flag_if(nxt, 0.5, ALU.is_gt))
            elif step == 5:
                own_.did(flag_if(mx, 0.9 * FILL / EXP_SCALE, ALU.is_lt))
            elif step == 6:
                own_.did(V.scalar_tensor_tensor(out=M["flags"][:, ds(QT * n, QT)], in0=x[:, g, :],
                                                scalar=0.0, in1=flag[:, g, :], op0=ALU.is_equal, op1=ALU.add))

        def probs(dve, own_, n, g):
            for j in range(QT):
                flag_step(own_, n, g, j)
                dve.wait_ge(s_ex, QT * n + j + 1)
                V.scalar_tensor_tensor(out=E[:, j, :], in0=S[:, g, j, :], scalar=thr[:, g, j:j + 1], in1=E[:, j, :],
                                       op0=ALU.is_ge, op1=ALU.mult).then_inc(s_p, 1)
                own_.wait()

        def context(dve, own_, n):
            b, h = n // HEADS, n % HEADS
            dve.wait_ge(s_pv, 2 + QT * n + QT)
            out = ps[:, BANK * 6:BANK * 8].rearrange("p (x c) -> p x c", x=2)[:, :, 0:16 * HALF]
            out = out.rearrange("p x (j e) -> p x j e", e=16)
            den = rden[:].rearrange("p (x j) -> p x j", x=2)
            own_.did(V.tensor_scalar(den, out[:, :, :, HD], 1e-30, None, ALU.max))
            own_.wait()
            own_.did(V.reciprocal(rden[:], rden[:]))
            own_.wait()
            for xy in range(2):
                ins = V.tensor_tensor(M["ctx"][:, ds(b * QT + HALF * xy, HALF), ds(h * HD, HD)], out[:, xy, :, 0:HD],
                                      den[:, xy, :].unsqueeze(2).to_broadcast([P, HALF, HD]), ALU.mult)
            ins.then_inc(s_cx, 1)

        FIRST_STEPS = 6
        HEAD_STEPS = FIRST_STEPS + 4 + 8 + 10 + 1
        TAIL_STEPS = 10 + QT + 4 + 11

        def dve_period(dve, n, g):
            head = Steps(dve, s_h, HEAD_STEPS * (n + 1)) if within(n + 1) else None
            following = Steps(dve, s_h, HEAD_STEPS * (n + 2)) if within(n + 2) else None
            tail = Steps(dve, s_t, TAIL_STEPS * n) if within(n) else None
            late = Steps(dve, s_c, 2 * (n - 1)) if within(n - 1) else None
            H = lambda f, *a: f(dve, head, n + 1, 1 - g, *a) if head else None
            L = lambda f, *a: f(dve, tail, n, g, *a) if tail else None
            if head:
                head.n = FIRST_STEPS
            L(exact_count)
            H(next_threshold, 0)
            L(near_values, 0)
            L(near_values, 1)
            L(near_values, 2)
            L(near_values, 3)
            L(select)
            H(next_threshold, 1)
            L(probs)
            if late:
                context(dve, late, n - 1)
            H(row_max)
            H(next_threshold, 2)
            if following:
                first_threshold(dve, following, n + 2, g)
                assert following.n == FIRST_STEPS
            assert head is None or head.n == HEAD_STEPS, head.n
            assert tail is None or tail.n == TAIL_STEPS, tail.n

        with nc.Block() as block:

            @block.gpsimd
            def _(pool):
                def q_masked(n, g):
                    if not isinstance(n, int) or n > 1:
                        pool.wait_ge(s_sc, QT * n - QT)
                    nc.gpsimd.tensor_tensor(qm[:, g, :], M["q_t"][:, ds((n // HEADS) * T, T)],
                                            M["hmask"][:, ds(n % HEADS, 1)].to_broadcast([P, T]),
                                            ALU.mult).then_inc(s_qm, 1)

                def v_head(n, g):
                    if not isinstance(n, int) or n > 1:
                        pool.wait_ge(s_pv, QT * n - QT + 2)
                    nc.gpsimd.tensor_copy(M["vh"][:, g, :, 0:HD],
                                          M["v"][:, ds((n // HEADS) * QT, QT), ds((n % HEADS) * HD, HD)]).then_inc(s_vh, 1)

                q_masked(0, 0)
                q_masked(1, 1)
                v_head(0, 0)
                q_masked(2, 0)
                v_head(1, 1)
                with pool.Fori(1, GROUPS // 2 - 1) as i:
                    q_masked(2 * i + 1, 1)
                    v_head(2 * i, 0)
                    q_masked(2 * i + 2, 0)
                    v_head(2 * i + 1, 1)
                q_masked(GROUPS - 1, 1)
                v_head(GROUPS - 2, 0)
                v_head(GROUPS - 1, 1)

            def periods(Fori, period):
                for n in range(-2, 2):
                    period(n, n % 2)
                with Fori(0, GROUPS // 2 - 2) as i:
                    period(2 * i + 2, 0)
                    period(2 * i + 3, 1)
                for n in range(GROUPS - 2, GROUPS + 1):
                    period(n, n % 2)

            @block.tensor
            def _(pe):
                periods(pe.Fori, lambda n, g: pe_period(pe, n, g))

            @block.scalar
            def _(act):
                periods(act.Fori, lambda n, g: act_period(act, n, g))

            @block.vector
            def _(dve):
                periods(dve.Fori, lambda n, g: dve_period(dve, n, g))


def repair(nc, M):
    ps = M["ps"]
    V = nc.vector
    DROP = T - K_TOP
    ROUNDS, AT = DROP // 8, DROP % 8
    FILL_SC = FILL / EXP_SCALE
    with ExitStack() as own:
        sb = lambda n, s, d=F32: own.enter_context(nc.sbuf_tensor(n, s, d))
        sem = lambda n: own.enter_context(nc.semaphore(n))
        marks, marked = sb("unit_marks", [1, UNITS], I32), sb("any_mark", [1, 1], I32)
        marks_f, marked_f = sb("unit_marks_f", [1, UNITS]), sb("any_mark_f", [1, 1])
        before, before_f = sb("marks_before", [1, UNITS], I32), sb("marks_before_f", [1, UNITS])
        qr, vr = sb("q_unit", [P, P]), sb("v_unit", [P, KBLK, HD + 1])
        S, W, X, E = (sb(n, [P, T]) for n in ("r_scores", "r_left", "r_sparse", "r_exps"))
        ones, rank, keep = (sb(n, [P, T]) for n in ("r_ones", "r_rank", "r_keep"))
        pt = sb("r_probs_t", [P, KBLK, P])
        t8 = sb("r_top8", [P, 8])
        thr, above, room, m, nb, rden = (sb(n, [P, 1]) for n in ("r_thr", "r_above", "r_room", "r_max", "r_bias", "r_den"))
        s_n = sem("marks_summed")
        s_m = sem("marks_ready")
        s_op = sem("r_operands")
        s_sc = sem("r_scores_ready")
        s_x = sem("r_sparse_ready")
        s_e = sem("r_exps_ready")
        s_t = sem("r_turned")
        s_te = sem("r_turned_out")
        s_pv = sem("r_products")
        s_d = sem("r_dve_steps")
        s_done = sem("r_unit_done")
        DVE_STEPS = 2 + 2 * ROUNDS + 12

        def units(eng, work):
            eng.wait_ge(s_m, 8)
            some = eng.value_load(marked[0:1, 0:1], min_val=0, max_val=1)
            with eng.If(some > 0):
                with eng.Fori(0, UNITS) as u:
                    mark = eng.value_load(marks[0:1, ds(u, 1)], min_val=0, max_val=1)
                    with eng.If(mark > 0):
                        work(u, eng.value_load(before[0:1, ds(u, 1)], min_val=0, max_val=UNITS - 1))
                    with eng.Else():
                        eng.sem_inc(M["passed"], 1)
                    eng.sem_inc(M["passed"], 1)
            with eng.Else():
                eng.sem_inc(M["passed"], 1)
            eng.sem_inc(M["passed"], 1)

        with nc.Block() as block:

            @block.gpsimd
            def _(pool):
                nc.gpsimd.memset(vr[:], 1.0).then_inc(s_m, 1)
                nc.gpsimd.memset(ones[:], 1.0).then_inc(s_m, 1)
                pool.sem_inc(s_done, 1)

                def work(u, k):
                    n, j = u // QT, u % QT
                    b, h = n // HEADS, n % HEADS
                    pool.wait_ge(s_done, k + 1)
                    nc.gpsimd.tensor_tensor(qr[:], M["q_t"][:, ds(b * T + j * P, P)],
                                            M["hmask"][:, ds(h, 1)].to_broadcast([P, P]), ALU.mult).then_inc(s_op, 1)
                    nc.gpsimd.tensor_copy(vr[:, :, 0:HD], M["v"][:, ds(b * QT, QT), ds(h * HD, HD)]).then_inc(s_op, 1)
                units(pool, work)

            @block.tensor
            def _(pe):
                nc.tensor.matmul(ps[0:1, 0:UNITS], M["mean_w"][:, 0:1], M["flags"][:], start=True, stop=True).then_inc(s_n, 1)

                def work(u, k):
                    n = u // QT
                    b = n // HEADS
                    pe.wait_ge(s_op, 2 * k + 2)
                    for h in range(2):
                        mm = nc.tensor.matmul(ps[:, BANK * h:BANK * (h + 1)], qr[:], M["k_t"][:, ds(b * T + BANK * h, BANK)],
                                              start=True, stop=True)
                    mm.then_inc(s_sc, 1)
                    pe.wait_ge(s_e, k + 1)
                    for c in range(KBLK):
                        mm = nc.tensor.transpose(ps[:, 2 * BANK + P * c:2 * BANK + P * (c + 1)], E[:, P * c:P * (c + 1)],
                                                 M["ident"][:])
                    mm.then_inc(s_t, 1)
                    pe.wait_ge(s_te, k + 1)
                    for c in range(KBLK):
                        mm = nc.tensor.matmul(ps[:, 4 * BANK:4 * BANK + HD + 1], pt[:, c, :], vr[:, c, :],
                                              start=(c == 0), stop=(c == KBLK - 1))
                    mm.then_inc(s_pv, 1)
                units(pe, work)

            @block.scalar
            def _(act):
                def work(u, k):
                    act.wait_ge(s_x, k + 1)
                    nc.scalar.activation(E[:], X[:], ACT.Exp, bias=nb[:], scale=EXP_SCALE).then_inc(s_e, 1)
                    act.wait_ge(s_t, k + 1)
                    nc.scalar.activation(pt[:], ps[:, 2 * BANK:4 * BANK], ACT.Identity).then_inc(s_te, 1)
                units(act, work)

            @block.sync
            def _(sp):
                sp.wait_ge(s_m, 8)

            @block.vector
            def _(dve):
                dve.wait_ge(s_n, 1)
                V.tensor_scalar(marks_f[:], ps[0:1, 0:UNITS], 0.0, None, ALU.is_gt).then_inc(s_m, 1)
                dve.wait_ge(s_m, 3)
                V.tensor_copy(marks[:], marks_f[:]).then_inc(s_m, 1)
                V.tensor_reduce(marked_f[:], marks_f[:], AX.X, ALU.max).then_inc(s_m, 1)
                V.tensor_tensor_scan(before_f[:], ones[0:1, 0:UNITS], marks_f[:], -1.0, ALU.mult, ALU.add).then_inc(s_m, 1)
                dve.wait_ge(s_m, 6)
                V.tensor_copy(marked[:], marked_f[:]).then_inc(s_m, 1)
                V.tensor_scalar(before[:], before_f[:], 0.0, None, ALU.max).then_inc(s_m, 1)

                def work(u, k):
                    n, j = u // QT, u % QT
                    b, h = n // HEADS, n % HEADS
                    st = Steps(dve, s_d, DVE_STEPS * k)

                    def ready():
                        st.wait()
                        dve.sem_inc(M["passed"], 1)
                    dve.wait_ge(s_sc, k + 1)
                    st.did(V.tensor_copy(S[:], ps[:, 0:T]))
                    ready()
                    st.did(V.tensor_scalar(W[:], S[:], -1.0, None, ALU.mult))
                    ready()
                    with dve.Fori(0, ROUNDS) as i:
                        dve.wait_ge(s_d, DVE_STEPS * k + 2 * i + 2)
                        dve.sem_inc(M["passed"], 1)
                        V.max(t8[:], W[:]).then_inc(s_d, 1)
                        dve.wait_ge(s_d, DVE_STEPS * k + 2 * i + 3)
                        dve.sem_inc(M["passed"], 1)
                        V.match_replace(out=W[:], in_to_replace=t8[:], in_values=W[:], imm_value=-3.0e38).then_inc(s_d, 1)
                    st.n += 2 * ROUNDS
                    ready()
                    st.did(V.max(t8[:], W[:]))
                    ready()
                    st.did(V.tensor_scalar(thr[:], t8[:, AT:AT + 1], -1.0, None, ALU.mult))
                    ready()
                    st.did(V.tensor_scalar(X[:], S[:], thr[:], None, ALU.is_gt, ALU.add, accum_out=above[:]))
                    st.did(V.tensor_scalar(keep[:], S[:], thr[:], None, ALU.is_equal))
                    ready()
                    st.did(V.tensor_scalar(room[:], above[:], -1.0, float(K_TOP), ALU.mult, ALU.add))
                    st.did(V.tensor_tensor_scan(rank[:], ones[:], keep[:], 0.0, ALU.mult, ALU.add))
                    ready()
                    st.did(V.scalar_tensor_tensor(out=keep[:], in0=rank[:], scalar=room[:], in1=keep[:],
                                                  op0=ALU.is_le, op1=ALU.mult))
                    ready()
                    st.did(V.tensor_tensor(keep[:], keep[:], X[:], ALU.add))
                    ready()
                    st.did(V.memset(X[:], FILL_SC))
                    ready()
                    V.copy_predicated(X[:], keep[:].bitcast(I32), S[:]).then_inc(s_d, 1)
                    st.n += 1
                    ready()
                    st.did(V.tensor_reduce(m[:], X[:], AX.X, ALU.max))
                    ready()
                    V.tensor_scalar(nb[:], m[:], -EXP_SCALE, None, ALU.mult).then_inc(s_x, 1)
                    dve.wait_ge(s_pv, k + 1)
                    out = ps[:, 4 * BANK:4 * BANK + HD + 1]
                    st.did(V.reciprocal(rden[:], out[:, HD:HD + 1]))
                    ready()
                    V.tensor_scalar(M["ctx"][:, ds(b * QT + j, 1), ds(h * HD, HD)].rearrange("p a e -> p (a e)"),
                                    out[:, 0:HD], rden[:], None, ALU.mult).then_inc(s_done, 1)
                    assert st.n == DVE_STEPS, st.n
                units(dve, work)


DEPTH = 6
BH, BD = 16, 64
INNER = BH * BD
WIN = 32
PAIRS = BH // 2
DI = int(P * 4 * 2 / 3)
CH = [(0, P), (P, P), (2 * P, DI - 2 * P)]
QK_SCALE = 8.0
MASKED = -1e30
G = TOK // BANK
RSQRT_BITS = float(0x5f3759df)
QK = 2 * INNER


def local_transformer(nc, ctx, A, M):
    ps = M["ps"]
    sem = lambda n: ctx.enter_context(nc.semaphore(n))
    xa, xb = M["xa"], M["xb"]
    V = nc.vector
    with ExitStack() as own:
        sb = lambda n, s, d=F32: own.enter_context(nc.sbuf_tensor(n, s, d))
        w_qkv = sb("w_qkv", [P, 3 * INNER])
        w_o = sb("w_o", [P, PAIRS, P])
        w1 = sb("w_1", [P, 2 * DI])
        w2 = sb("w_2", [P, 3, P])
        b1 = sb("b_1", [P, 6])
        vecs = sb("ln_g_ln_b_b2", [P, 3])
        scales = sb("qk_scales", [P, 4, BD])
        V_SLOTS = 4
        rot = sb("rotary", [P, 4, QT, BD])
        rot_l = sb("rotary_scaled", [P, 4, QT, BD])
        mask = sb("masks", [P, QT, 2 * WIN])
        xst = sb("x_tile", [P, 2, P])
        sq = sb("squares", [P, 2 * BH, BD])
        qk = sb("qk_normed", [P, 2 * BH, BD])
        rc = sb("qk_cos", [P, 2 * BH, BD])
        rs = sb("qk_sin", [P, 2 * BH, BD])
        ss, a_half, yr, tr = (sb(n, [P, 2 * BH]) for n in ("sum_sq", "neg_half", "rnorm", "newton"))
        q_t = sb("q_tt", [P, PAIRS, P])
        k_t = sb("k_tt", [P, 2, PAIRS, WIN + P])
        vt = sb("v_tok", [P, V_SLOTS, 2, 512])
        v2 = sb("v_windows", [P, 2, 4, 512])
        sm = sb("sims", [P, BH, 2 * WIN])
        pe_ = sb("exps_b", [P, BH, 2 * WIN])
        pt = sb("exps_t", [P, PAIRS, P])
        cn = sb("ctx_b", [P, PAIRS, 2, BD])
        ct = sb("ctx_bt", [P, PAIRS, P])
        mxb, sumb, rsum = (sb(n, [P, BH]) for n in ("max_b", "sum_b", "rsum_b"))
        xs = sb("x_shifted", [P, TOK])
        xc = sb("x_centred", [P, TOK])
        xq = sb("x_square", [P, TOK])
        gel = sb("gelu", [P, 3, BANK])
        hid = sb("hidden", [P, 2, 3, BANK])

        s_fix = sem("b_constants")
        s_const = sem("b_memsets")
        s_wq = sem("b_w_qkv")
        s_wo = sem("b_w_o")
        s_wf = sem("b_w_mlp")
        s_sc = sem("b_scales")
        s_rot = sem("b_rotary_ready")
        s_xst = sem("b_x_tile_ready")
        s_q = sem("b_qk_projected")
        s_v = sem("b_v_projected")
        s_sq = sem("b_squared")
        s_qn = sem("b_qk_normed")
        s_cos = sem("b_cos_ready")
        s_r = sem("b_q_rotated")
        s_sin = sem("b_k_sin_ready")
        s_rk = sem("b_k_rotated")
        s_f = sem("b_ring_filled")
        s_c = sem("b_ring_emptied")
        s_halo = sem("b_k_halo")
        s_s = sem("b_scores")
        s_min = sem("b_masked")
        s_sub = sem("b_less_max")
        s_e = sem("b_exps")
        s_v2 = (sem("b_v_windows_ready_even"), sem("b_v_windows_ready_odd"))
        s_pv = sem("b_pv")
        s_co = sem("b_ctx")
        s_y = sem("b_out_projected")
        s_yo = sem("b_attention_added")
        s_1 = sem("b_dve_norm_steps")
        s_2 = sem("b_dve_softmax_steps")
        s_x = sem("b_shifted")
        s_mean = sem("b_mean")
        s_xc = sem("b_centred")
        s_xq = sem("b_squares")
        s_var = sem("b_var")
        s_sd = sem("b_sd")
        s_rd = sem("b_rstd")
        s_ln = sem("b_ln_scaled")
        s_xn = sem("b_ln_ready")
        s_g = sem("b_gate")
        s_a = sem("b_up")
        s_ge = sem("b_gelu")
        s_h = sem("b_hidden")
        s_o = sem("b_mlp_out")
        s_fo = sem("b_layer_done")

        tile_at = lambda t: (t // QT, (t % QT) * P)
        ring = lambda i: ps[:, BANK * (4 + i % 2):BANK * (5 + i % 2)]
        CREDIT = 12
        V2_CREDIT = 768
        V_, CT_, PT_, TQ_, TK_ = "v", "ctx turned", "probs turned", "q turned", "k turned"
        USES = [(V_, 0), (V_, 1), (TQ_, 0), (TK_, 0)]
        for n_ in range(TILES + 1):
            in_period = ((CT_, n_ - 1), (V_, n_ + 2), (PT_, n_), (TQ_, n_ + 1), (TK_, n_ + 1))
            USES += [(what, t) for what, t in in_period if 0 <= t < TILES]
        PLACE = {use: 2 * i for i, use in enumerate(USES)}
        FILLS = {use: 2 * i for i, use in enumerate(u for u in USES if u[0] != V_)}

        def steady(table, step, what, t):
            return table[what, t] if isinstance(t, int) else table[what, 5] + step * (t - 5)

        def emptied(l, what, t, i):
            return 160 * l + steady(PLACE, 10, what, t) + i + 1 + CREDIT

        def filled(l, what, t, i):
            return 8 * TILES * l + steady(FILLS, 8, what, t) + i + 1 + 2

        H2 = BD // 2

        def layers(eng, section):
            with eng.Fori(0, DEPTH) as l:
                section(l)

        def periods(eng, l, prologue, period, epilogue):
            prologue(l)
            period(l, 0, 0)
            period(l, 1, 1)
            with eng.Fori(0, TILES // 2 - 2) as i:
                period(l, 2 * i + 2, 0)
                period(l, 2 * i + 3, 1)
            period(l, TILES - 2, 0)
            period(l, TILES - 1, 1)
            epilogue(l)

        cols = lambda t, g: t[:, BANK * g:BANK * (g + 1)]
        EARLY = range(G - 1)
        LATE = G - 1
        norm_bank = lambda g: cols(ps, g if g < LATE else 4)

        def within(t):
            return not isinstance(t, int) or 0 <= t < TILES

        with nc.Block() as block:

            @block.sync
            def _(sp):
                sp.dma_start(rot[:], A["b_rot"]).then_inc(s_fix, 16)
                sp.dma_start(mask[:], A["b_mask"]).then_inc(s_fix, 16)
                for s, k in ((s_v, 4), (s_qn, 2), (s_c, CREDIT), (s_yo, 1), (s_co, 1), (s_fo, G), (s_s, 2),
                             (s_f, 2), (s_pv, 2), (s_h, 3), (s_ge, 3), (s_o, 2), (s_e, 1),
                             (s_v2[0], V2_CREDIT), (s_v2[1], V2_CREDIT)):
                    sp.sem_inc(s, k)

                def weights_attention(l):
                    sp.dma_start(w_qkv[:], A["b_wqkv"][ds(l, 1)].rearrange("l p n -> (l p) n")).then_inc(s_wq, 16)
                    sp.dma_start(scales[:], A["b_scales"][ds(l, 1)].rearrange("l p a d -> (l p) a d")).then_inc(s_sc, 16)

                def weights_out(l):
                    sp.dma_start(w_o[:], A["b_wo"][ds(l, 1)].rearrange("l p c n -> (l p) c n")).then_inc(s_wo, 16)

                def weights_mlp(l):
                    for t, a in ((w1, "b_w1"), (w2, "b_w2"), (b1, "b_b1"), (vecs, "b_vecs")):
                        src = A[a][ds(l, 1)]
                        src = src.rearrange("l p c n -> (l p) c n") if a == "b_w2" else src.rearrange("l p n -> (l p) n")
                        sp.dma_start(t[:], src).then_inc(s_wf, 16)

                def v_windows(l, t1, p):
                    n = TILES * l + t1
                    sp.wait_ge(s_pv, n + 1)
                    sp.sem_inc(M["passed"], 1)
                    sp.wait_ge(s_c, emptied(l, V_, t1, 1))
                    for par in range(2):
                        for w in range(4):
                            lo = 64 * par
                            src = vt[WIN * w:WIN * (w + 1), ds(t1 % V_SLOTS, 1), par, :]
                            old = (vt[WIN * (w - 1):WIN * w, ds(t1 % V_SLOTS, 1), par, :] if w
                                   else vt[3 * WIN:, ds((t1 + V_SLOTS - 1) % V_SLOTS, 1), par, :])
                            sp.dma_start(v2[lo + WIN:lo + 2 * WIN, p, w:w + 1, :], src).then_inc(s_v2[p], 16)
                            sp.dma_start(v2[lo:lo + WIN, p, w:w + 1, :], old).then_inc(s_v2[p], 16)

                weights_attention(0)
                weights_out(0)
                weights_mlp(0)
                sp.wait_ge(s_const, 3)

                def prologue(l):
                    v_windows(l, 0, 0)
                    v_windows(l, 1, 1)

                def period(l, t, p):
                    if within(t + 2):
                        v_windows(l, t + 2, p)

                def section(l):
                    periods(sp, l, prologue, period, lambda l: None)
                    sp.sem_inc(M["passed"], 1)
                    nxt = (l + 1) % DEPTH
                    sp.wait_ge(s_v, 4 + 2 * TILES * (l + 1))
                    sp.sem_inc(M["passed"], 1)
                    sp.wait_ge(s_rot, 4 * (l + 1))
                    sp.sem_inc(M["passed"], 1)
                    weights_attention(nxt)
                    sp.wait_ge(s_y, TILES * (l + 1))
                    sp.sem_inc(M["passed"], 1)
                    weights_out(nxt)
                    sp.wait_ge(s_fo, G + G * (l + 1))
                    sp.sem_inc(M["passed"], 1)
                    weights_mlp(nxt)
                layers(sp, section)
                sp.wait_ge(s_wq, 16 * (DEPTH + 1))
                sp.wait_ge(s_sc, 16 * (DEPTH + 1))
                sp.wait_ge(s_wo, 16 * (DEPTH + 1))
                sp.wait_ge(s_wf, 64 * (DEPTH + 1))

            @block.gpsimd
            def _(pool):
                nc.gpsimd.memset(k_t[:], 0.0).then_inc(s_const, 1)
                nc.gpsimd.memset(vt[:], 0.0).then_inc(s_const, 1)
                nc.gpsimd.memset(xb[:], 0.0).then_inc(s_const, 1)
                pool.wait_ge(s_fix, 32)
                pool.wait_ge(s_const, 3)

                def rotated_k(l, t1):
                    n = TILES * l + t1
                    if not (isinstance(t1, int) and t1 == 0):
                        pool.wait_ge(s_r, n)
                    pool.wait_ge(s_qn, 2 * n + 3)
                    nc.gpsimd.tensor_tensor(rc[:, 0:BH, :], qk[:, 0:BH, :],
                                            rot_l[:, 0, ds(t1 % QT, 1), :].to_broadcast([P, BH, BD]), ALU.mult).then_inc(s_cos, 1)
                    pool.wait_ge(s_qn, 2 * n + 4)
                    if not (isinstance(t1, int) and t1 == 0):
                        pool.wait_ge(s_rk, n)
                        pool.wait_ge(s_f, filled(l, TK_, t1 - 1, 1))
                    nc.gpsimd.tensor_tensor(rc[:, BH:, :], qk[:, BH:, :],
                                            rot_l[:, 2, ds(t1 % QT, 1), :].to_broadcast([P, BH, BD]), ALU.mult).then_inc(s_sin, 1)
                    for a in range(2):
                        nc.gpsimd.tensor_tensor(
                            rs[:, BH:, H2 * a:H2 * (a + 1)], qk[:, BH:, H2 * (1 - a):H2 * (2 - a)],
                            rot_l[:, 3, ds(t1 % QT, 1), H2 * a:H2 * (a + 1)].to_broadcast([P, BH, H2]), ALU.mult).then_inc(s_sin, 1)
                    pool.wait_ge(s_sin, 3 * n + 3)
                    nc.gpsimd.tensor_tensor(rs[:, BH:, :], rs[:, BH:, :], rc[:, BH:, :], ALU.add).then_inc(s_rk, 1)

                def prologue(l):
                    rotated_k(l, 0)
                    rotated_k(l, 1)

                def period(l, t, p):
                    if within(t + 2):
                        rotated_k(l, t + 2)

                def section(l):
                    pool.wait_ge(s_sc, 16 * (l + 1))
                    pool.wait_ge(s_yo, TILES * l + 1)
                    for i in range(4):
                        nc.gpsimd.tensor_tensor(rot_l[:, i], rot[:, i], scales[:, ds(i, 1), :].to_broadcast([P, QT, BD]),
                                                ALU.mult).then_inc(s_rot, 1)
                    pool.wait_ge(s_rot, 4 * (l + 1))
                    periods(pool, l, prologue, period, lambda l: None)
                    pool.wait_ge(s_wf, 64 * (l + 1))
                    for g in range(G):
                        pool.wait_ge(s_rd, G * l + g + 1)
                        nc.gpsimd.tensor_tensor(cols(xc, g), cols(xc, g), cols(xq, g), ALU.mult).then_inc(s_ln, 1)
                        pool.wait_ge(s_ln, G * l + g + 1)
                        pool.sem_inc(M["passed"], 1)
                        nc.gpsimd.tensor_scalar(cols(xs, g), cols(xc, g), vecs[:, 0:1], vecs[:, 1:2],
                                                ALU.mult, ALU.add).then_inc(s_xn, 1)
                layers(pool, section)

            @block.tensor
            def _(pe):
                def free(l, what, t, i):
                    pe.wait_ge(s_c, emptied(l, what, t, i) - 2)

                def project(l, t1, p1, between=lambda i: None):
                    n = TILES * l + t1
                    pe.wait_ge(s_xst, 2 * n + 2)
                    for i in range(4):
                        if i % 2 == 0:
                            pe.wait_ge(s_qn, 2 * n + i // 2 + 1)
                        mm = nc.tensor.matmul(ps[:, BANK * i:BANK * (i + 1)], xst[:, p1, :],
                                              w_qkv[:, BANK * i:BANK * (i + 1)], start=True, stop=True)
                        if i % 2:
                            mm.then_inc(s_q, 1)
                            between(i // 2)
                    for i in range(2):
                        free(l, V_, t1, i)
                        nc.tensor.matmul(ring(i), xst[:, p1, :], w_qkv[:, QK + BANK * i:QK + BANK * (i + 1)],
                                         start=True, stop=True).then_inc(s_v, 1)

                def turn(l, t, kind, src, halves=(0, 1)):
                    for i in halves:
                        free(l, kind, t, i)
                        for c in range(4):
                            mm = nc.tensor.transpose(ring(i)[:, P * c:P * (c + 1)], src(4 * i + c), M["ident"][:])
                        mm.then_inc(s_f, 1)

                def turn_q(l, t):
                    pe.wait_ge(s_r, TILES * l + t + 1)
                    turn(l, t, TQ_, lambda c: rs[:, 2 * c:2 * c + 2, :])

                def turn_k(l, t, halves=(0, 1)):
                    pe.wait_ge(s_rk, TILES * l + t + 1)
                    turn(l, t, TK_, lambda c: rs[:, BH + 2 * c:BH + 2 * c + 2, :], halves)

                def windows(left, right, heads=range(BH)):
                    for h in heads:
                        half = slice(64 * (h % 2), 64 * (h % 2) + 64)
                        at = BANK * (6 + h % 2) + 64 * (h // 2)
                        for w in range(4):
                            mm = nc.tensor.matmul(ps[WIN * w:WIN * (w + 1), at:at + 64], left(half, h // 2, w),
                                                  right(half, h // 2, w), start=True, stop=True)
                    return mm

                def scores(l, t, p):
                    n = TILES * l + t
                    pe.wait_ge(s_halo, n + 1)
                    pe.wait_ge(s_co, n + 1)
                    pe.wait_ge(s_c, emptied(l, TK_, t, 1))
                    pe.sem_inc(M["passed"], 1)
                    windows(lambda half, c, w: q_t[half, c, WIN * w:WIN * (w + 1)],
                            lambda half, c, w: k_t[half, p, c, WIN * w:WIN * (w + 2)]).then_inc(s_s, 1)

                def probs_v(l, t, p, *between):
                    n = TILES * l + t
                    pe.wait_ge(s_min, n + 1)
                    pe.wait_ge(s_v2[p], 128 * (n - p) + 256 + V2_CREDIT)
                    pe.wait_ge(s_c, emptied(l, PT_, t, 1))
                    pe.sem_inc(M["passed"], 1)
                    cuts = (0, BH // 2, 3 * BH // 4, BH) if between else (0, BH)
                    for i in range(len(cuts) - 1):
                        mm = windows(lambda half, c, w: pt[half, c, WIN * w:WIN * (w + 1)],
                                     lambda half, c, w: v2[half, p, w, 64 * c:64 * (c + 1)], range(cuts[i], cuts[i + 1]))
                        if i < len(between):
                            between[i]()
                    mm.then_inc(s_pv, 1)

                def turn_ctx(l, t, halves=(0, 1)):
                    pe.wait_ge(s_co, TILES * l + t + 2)
                    turn(l, t, CT_, lambda c: cn[:, c, :, :], halves)

                def project_out(l, t, last):
                    pe.wait_ge(s_c, emptied(l, CT_, t, 1))
                    pe.wait_ge(s_c, emptied(l, *last, 0))
                    for c in range(PAIRS):
                        mm = nc.tensor.matmul(ring(0)[:, 0:P], w_o[:, c, :], ct[:, c, :],
                                              start=(c == 0), stop=(c == PAIRS - 1))
                    mm.then_inc(s_y, 1)

                def mean(l, g):
                    pe.wait_ge(s_x, 2 * G * l + 2 * g + 2)
                    nc.tensor.matmul(norm_bank(g), M["mean_w"][:], cols(xs, g), start=True, stop=True).then_inc(s_mean, 1)

                def variance(l, g):
                    pe.wait_ge(s_xq, G * l + g + 1)
                    nc.tensor.matmul(norm_bank(g), M["mean_w"][:], cols(xq, g), start=True, stop=True).then_inc(s_var, 1)

                def prologue(l):
                    project(l, 0, 0)
                    project(l, 1, 1)
                    turn_q(l, 0)
                    turn_k(l, 0)

                def period(l, t, p):
                    scores(l, t, p)

                    def ctx_half(i):
                        if within(t - 1):
                            if i == 0:
                                pe.wait_ge(s_yo, TILES * l + t)
                            turn_ctx(l, t - 1, (i,))

                    if within(t + 2):
                        project(l, t + 2, p, ctx_half)
                    else:
                        ctx_half(0)
                        ctx_half(1)
                    if isinstance(t, int) and t == TILES - 2:
                        pe.wait_ge(s_qn, 2 * TILES * (l + 1) + 2)
                        for g in EARLY:
                            mean(l, g)
                    if isinstance(t, int) and t == TILES - 1:
                        for g in EARLY:
                            variance(l, g)
                    pe.wait_ge(s_e, TILES * l + t + 2)
                    turn(l, t, PT_, lambda c: pe_[:, 2 * c:2 * c + 2, :])
                    if within(t + 1):
                        turn_q(l, t + 1)
                        probs_v(l, t, p, lambda: turn_k(l, t + 1, (0,)), lambda: turn_k(l, t + 1, (1,)))
                    else:
                        probs_v(l, t, p)
                    if within(t - 1):
                        project_out(l, t - 1, (TK_, t + 1) if within(t + 1) else (PT_, t))

                def epilogue(l):
                    pe.wait_ge(s_yo, TILES * (l + 1))
                    turn_ctx(l, TILES - 1)
                    project_out(l, TILES - 1, (CT_, TILES - 1))

                def section(l):
                    pe.wait_ge(s_wq, 16 * (l + 1))
                    pe.wait_ge(s_wo, 16 * (l + 1))
                    periods(pe, l, prologue, period, epilogue)
                    pe.wait_ge(s_wf, 64 * (l + 1))
                    pe.wait_ge(s_sd, G * l + LATE)
                    up(l, 0)
                    mean(l, LATE)
                    up(l, 1)
                    variance(l, LATE)
                    down(l, 0)
                    for g in range(2, G):
                        up(l, g)
                        down(l, g - 1)
                    down(l, G - 1)

                def up(l, g):
                    pe.wait_ge(s_xn, G * l + g + 1)
                    for c, (o, m) in enumerate(CH):
                        pe.wait_ge(s_ge, 3 * (G * l + g) + c + 1)
                        nc.tensor.matmul(ps[0:m, BANK * (1 + c):BANK * (2 + c)], w1[:, DI + o:DI + o + m], cols(xs, g),
                                         start=True, stop=True).then_inc(s_g, 1)
                        pe.wait_ge(s_h, 3 * (G * l + g) + c + 1)
                        nc.tensor.matmul(ps[0:m, BANK * (5 + c):BANK * (6 + c)], w1[:, o:o + m], cols(xs, g),
                                         start=True, stop=True).then_inc(s_a, 1)

                def down(l, g):
                    pe.wait_ge(s_fo, G + G * l + g)
                    for c, (o, m) in enumerate(CH):
                        pe.wait_ge(s_h, 3 + 3 * (G * l + g) + c + 1)
                        mm = nc.tensor.matmul(ps[:, 0:BANK], w2[0:m, c, :], hid[0:m, g % 2, c, :],
                                              start=(c == 0), stop=(c == 2))
                    mm.then_inc(s_o, 1)
                layers(pe, section)

            @block.scalar
            def _(act):
                def stage(l, t1, p1):
                    n = TILES * l + t1
                    b, at = tile_at(t1)
                    act.wait_ge(s_v, 2 * n + 2)
                    for lo, sh in ((0, 1), (64, 0)):
                        src = xa[lo:lo + 64, ds(b, 1), ds(at + sh, P)].rearrange("p b t -> p (b t)")
                        nc.scalar.copy(xst[lo:lo + 64, p1, :], src).then_inc(s_xst, 1)

                def halo(l, t, p):
                    n = TILES * l + t
                    act.wait_ge(s_s, n + 1)
                    if isinstance(t, int) and t == 0:
                        act.wait_ge(s_c, 160 * l + CREDIT)
                    else:
                        act.wait_ge(s_c, emptied(l, TK_, t - 1, 1))
                    nc.scalar.copy(k_t[:, p, :, 0:WIN], k_t[:, 1 - p, :, P:P + WIN]).then_inc(s_halo, 1)

                def out_of_ring(i, dst):
                    nc.scalar.activation(dst, ring(i), ACT.Identity).then_inc(s_c, 1)

                def squares(l, t, i):
                    act.wait_ge(s_q, 2 * (TILES * l + t) + i + 1)
                    nc.scalar.activation(sq[:, BH * i:BH * (i + 1), :], ps[:, 2 * BANK * i:2 * BANK * (i + 1)],
                                         ACT.Square).then_inc(s_sq, 1)

                def v_out(l, t, p, halves=(0, 1)):
                    n = TILES * l + t
                    act.wait_ge(s_v2[p], 128 * (n - p) - 256 + V2_CREDIT)
                    act.wait_ge(s_v2[1 - p], 128 * (n + p) - 256 + V2_CREDIT)
                    for i in halves:
                        act.wait_ge(s_v, 4 + 2 * n + i + 1)
                        out_of_ring(i, vt[:, ds(t % V_SLOTS, 1), i, :])

                def turned_out(l, t, what, dst, halves=(0, 1)):
                    for i in halves:
                        act.wait_ge(s_f, filled(l, what, t, i))
                        out_of_ring(i, dst(slice(4 * i, 4 * i + 4)))

                def exps(l, t):
                    act.wait_ge(s_sub, TILES * l + t + 1)
                    nc.scalar.activation(pe_[:].rearrange("p (c r) e -> p r c e", r=2),
                                         sm[:].rearrange("p (r c) e -> p r c e", r=2), ACT.Exp,
                                         scale=QK_SCALE).then_inc(s_e, 1)

                def qk_out(l, t, p):
                    turned_out(l, t, TQ_, lambda c: q_t[:, c, :])
                    turned_out(l, t, TK_, lambda c: k_t[:, p, c, WIN:])

                def prologue(l):
                    halo(l, 0, 0)
                    for t in range(2):
                        stage(l, t, t)
                        squares(l, t, 0)
                        squares(l, t, 1)
                        v_out(l, t, t)
                    qk_out(l, 0, 0)

                def period(l, t, p):
                    if within(t + 1):
                        halo(l, t + 1, 1 - p)
                    if within(t + 2):
                        stage(l, t + 2, p)
                    if isinstance(t, int) and t == TILES - 2:
                        for g in EARLY:
                            shifted(l, g)
                    if within(t - 1):
                        turned_out(l, t - 1, CT_, lambda c: ct[:, c, :], (0,))
                    if within(t + 2):
                        squares(l, t + 2, 0)
                    exps(l, t)
                    if within(t - 1):
                        turned_out(l, t - 1, CT_, lambda c: ct[:, c, :], (1,))
                    if within(t + 2):
                        v_out(l, t + 2, p, (0,))
                        squares(l, t + 2, 1)
                        v_out(l, t + 2, p, (1,))
                    turned_out(l, t, PT_, lambda c: pt[:, c, :])
                    if within(t + 1):
                        qk_out(l, t + 1, 1 - p)
                    if not within(t + 2):
                        for g in EARLY:
                            (squared if t == TILES - 2 else deviation)(l, g)

                def epilogue(l):
                    turned_out(l, TILES - 1, CT_, lambda c: ct[:, c, :])

                def section(l):
                    act.wait_ge(s_fo, G * (l + 1))
                    periods(act, l, prologue, period, epilogue)
                    shifted(l, LATE)
                    act.wait_ge(s_wf, 64 * (l + 1))
                    gelus(l, 0)
                    squared(l, LATE)
                    gelus(l, 1)
                    deviation(l, LATE)
                    for g in range(2, G):
                        gelus(l, g)

                def shifted(l, g):
                    b, at = g * BANK // T, g * BANK % T
                    act.wait_ge(s_yo, TILES * l + 4 * g + 5)
                    for lo, sh in ((0, 1), (64, 0)):
                        nc.scalar.copy(xs[lo:lo + 64, BANK * g:BANK * (g + 1)],
                                       xb[lo:lo + 64, b, at + sh:at + sh + BANK]).then_inc(s_x, 1)

                def squared(l, g):
                    act.wait_ge(s_xc, G * l + g + 1)
                    nc.scalar.activation(cols(xq, g), cols(xc, g), ACT.Square).then_inc(s_xq, 1)

                def deviation(l, g):
                    act.wait_ge(s_var, G * l + g + 1)
                    nc.scalar.activation(cols(xq, g), norm_bank(g), ACT.Sqrt, bias=M["eps"][:]).then_inc(s_sd, 1)

                def gelus(l, g):
                    for c, (o, m) in enumerate(CH):
                        act.wait_ge(s_g, 3 * (G * l + g) + c + 1)
                        act.wait_ge(s_h, 3 * (G * l + g) + c + 1)
                        nc.scalar.activation(gel[0:m, c, :], ps[0:m, BANK * (1 + c):BANK * (2 + c)], ACT.Gelu,
                                             bias=b1[0:m, 3 + c:4 + c]).then_inc(s_ge, 1)
                act.wait_ge(s_const, 3)
                layers(act, section)

            @block.vector
            def _(dve):
                N_STEPS, S_STEPS = 13 + 2, 3

                def norms(l, t1):
                    n = TILES * l + t1
                    st = Steps(dve, s_1, N_STEPS * n)
                    dve.wait_ge(s_sq, 2 * n + 2)
                    st.did(V.tensor_reduce(ss[:], sq[:], AX.X, ALU.add))
                    st.wait()
                    st.did(V.tensor_scalar(ss[:], ss[:], 1e-24, None, ALU.max))
                    st.wait()
                    st.did(V.tensor_scalar(yr[:].bitcast(I32), ss[:].bitcast(I32), -0.5, RSQRT_BITS, ALU.mult, ALU.add))
                    st.did(V.tensor_scalar(a_half[:], ss[:], -0.5, None, ALU.mult))
                    st.wait()
                    for _ in range(3):
                        st.did(V.tensor_tensor(tr[:], yr[:], yr[:], ALU.mult))
                        st.wait()
                        st.did(V.tensor_tensor(tr[:], tr[:], a_half[:], ALU.mult))
                        st.wait()
                        st.did(V.scalar_tensor_tensor(out=yr[:], in0=tr[:], scalar=1.5, in1=yr[:], op0=ALU.add, op1=ALU.mult))
                        st.wait()
                    if not (isinstance(t1, int) and t1 == 0):
                        dve.wait_ge(s_cos, n)
                        dve.wait_ge(s_rk, n)

                def normed(l, t1, i):
                    dve.wait_ge(s_1, N_STEPS * (TILES * l + t1) + 13)
                    V.tensor_tensor(qk[:, BH * i:BH * (i + 1), :],
                                    ps[:, 2 * BANK * i:2 * BANK * (i + 1)].rearrange("p (h e) -> p h e", e=BD),
                                    yr[:, BH * i:BH * (i + 1)].unsqueeze(2).to_broadcast([P, BH, BD]),
                                    ALU.mult).then_inc(s_qn, 1)

                def rotated_q(l, t1):
                    n = TILES * l + t1
                    st = Steps(dve, s_1, N_STEPS * n)
                    st.n = 13
                    if not (isinstance(t1, int) and t1 == 0):
                        dve.wait_ge(s_f, filled(l, TQ_, t1 - 1, 1))
                    dve.wait_ge(s_qn, 2 * n + 3)
                    for a in range(2):
                        st.did(V.tensor_tensor(
                            rs[:, 0:BH, H2 * a:H2 * (a + 1)], qk[:, 0:BH, H2 * (1 - a):H2 * (2 - a)],
                            rot_l[:, 1, ds(t1 % QT, 1), H2 * a:H2 * (a + 1)].to_broadcast([P, BH, H2]), ALU.mult))
                    st.wait()
                    dve.wait_ge(s_cos, n + 1)
                    V.tensor_tensor(rs[:, 0:BH, :], rs[:, 0:BH, :], rc[:, 0:BH, :], ALU.add).then_inc(s_r, 1)
                    assert st.n == N_STEPS, st.n

                def softmax(l, t):
                    n = TILES * l + t
                    st = Steps(dve, s_2, S_STEPS * n)
                    dve.wait_ge(s_s, 2 + n + 1)
                    dve.wait_ge(s_e, n + 1)
                    V.tensor_tensor(sm[:], ps[:, BANK * 6:BANK * 8].rearrange("p (h e) -> p h e", e=2 * WIN),
                                    mask[:, ds(t % QT, 1), :].to_broadcast([P, BH, 2 * WIN]), ALU.min).then_inc(s_min, 1)
                    dve.wait_ge(s_min, n + 1)
                    st.did(V.tensor_reduce(mxb[:], sm[:], AX.X, ALU.max))
                    st.wait()
                    V.tensor_tensor(sm[:], sm[:], mxb[:].unsqueeze(2).to_broadcast([P, BH, 2 * WIN]),
                                    ALU.subtract).then_inc(s_sub, 1)

                def row_sums(l, t):
                    n = TILES * l + t
                    st = Steps(dve, s_2, S_STEPS * n)
                    st.n = 1
                    dve.wait_ge(s_e, n + 2)
                    st.did(V.tensor_reduce(sumb[:], pe_[:], AX.X, ALU.add))
                    st.wait()
                    st.did(V.reciprocal(rsum[:], sumb[:]))

                def context(l, t):
                    n = TILES * l + t
                    dve.wait_ge(s_2, S_STEPS * (n + 1))
                    dve.wait_ge(s_pv, 2 + n + 1)
                    for r in range(2):
                        ins = V.tensor_tensor(
                            cn[:, :, r, :], ps[:, BANK * (6 + r):BANK * (7 + r)].rearrange("p (c e) -> p c e", e=BD),
                            rsum[:].rearrange("p (c r) -> p r c", r=2)[:, r, :].unsqueeze(2).to_broadcast([P, PAIRS, BD]),
                            ALU.mult)
                    ins.then_inc(s_co, 1)

                def added(l, t):
                    n = TILES * l + t
                    b, at = tile_at(t)
                    dve.wait_ge(s_y, n + 1)
                    x = lambda s: s[:, ds(b, 1), ds(at + 1, P)].rearrange("p b t -> p (b t)")
                    V.tensor_tensor(x(xb), x(xa), ring(0)[:, 0:P], ALU.add).then_inc(s_yo, 1)

                def prologue(l):
                    for t in range(2):
                        norms(l, t)
                        normed(l, t, 0)
                        normed(l, t, 1)
                        rotated_q(l, t)

                def period(l, t, p):
                    softmax(l, t)
                    row_sums(l, t)
                    if within(t + 2):
                        norms(l, t + 2)
                        normed(l, t + 2, 0)
                    elif t == TILES - 2:
                        for g in EARLY:
                            centred(l, g)
                    else:
                        rstd(l, 0)
                    context(l, t)
                    if within(t + 2):
                        normed(l, t + 2, 1)
                    if within(t - 1):
                        added(l, t - 1)
                    if within(t + 2):
                        rotated_q(l, t + 2)

                def epilogue(l):
                    rstd(l, 1)
                    added(l, TILES - 1)

                def section(l):
                    dve.wait_ge(s_rot, 4 * (l + 1))
                    periods(dve, l, prologue, period, epilogue)
                    dve.wait_ge(s_wf, 64 * (l + 1))
                    hidden(l, 0)
                    centred(l, LATE)
                    rstd(l, 2)
                    hidden(l, 1)
                    mlp_added(l, 0)
                    rstd(l, LATE)
                    hidden(l, 2)
                    mlp_added(l, 1)
                    hidden(l, 3)
                    mlp_added(l, 2)
                    mlp_added(l, 3)

                def centred(l, g):
                    dve.wait_ge(s_mean, G * l + g + 1)
                    V.tensor_tensor(cols(xc, g), cols(xs, g), norm_bank(g), ALU.subtract).then_inc(s_xc, 1)

                def rstd(l, g):
                    dve.wait_ge(s_sd, G * l + g + 1)
                    V.reciprocal(cols(xq, g), cols(xq, g)).then_inc(s_rd, 1)

                def hidden(l, g):
                    dve.wait_ge(s_o, G * l + g + 1)
                    for c, (o, m) in enumerate(CH):
                        dve.wait_ge(s_ge, 3 + 3 * (G * l + g) + c + 1)
                        dve.wait_ge(s_a, 3 * (G * l + g) + c + 1)
                        V.scalar_tensor_tensor(out=hid[0:m, g % 2, c, :], in0=ps[0:m, BANK * (5 + c):BANK * (6 + c)],
                                               scalar=b1[0:m, c:c + 1], in1=gel[0:m, c, :],
                                               op0=ALU.add, op1=ALU.mult).then_inc(s_h, 1)

                def mlp_added(l, g):
                    b, at = g * BANK // T, g * BANK % T
                    dve.wait_ge(s_o, 2 + G * l + g + 1)
                    V.scalar_tensor_tensor(out=xa[:, b, 1 + at:1 + at + BANK], in0=ps[:, 0:BANK], scalar=vecs[:, 2:3],
                                           in1=xb[:, b, 1 + at:1 + at + BANK], op0=ALU.add, op1=ALU.add).then_inc(s_fo, 1)
                dve.wait_ge(s_const, 3)
                layers(dve, section)


def join(nc, A, M, out):
    ps = M["ps"]
    V = nc.vector
    with ExitStack() as own:
        sb = lambda n, s: own.enter_context(nc.sbuf_tensor(n, s, F32))
        sem = lambda n: own.enter_context(nc.semaphore(n))
        x0, w, bias = sb("x_again", [P, TOK]), sb("w_out_a", [P, P]), sb("b_out_a", [P, 1])
        ct, y = sb("ctx_a_t", [P, TOK]), sb("y", [P, TOK])
        s_ld, s_t, s_te, s_y, s_1, s_out = (sem(n) for n in (
            "join_loads", "join_turned", "join_turned_out", "join_projected", "join_added", "join_stores"))
        col = lambda t, g: t[:, BANK * g:BANK * (g + 1)]
        with nc.Block() as block:

            @block.sync
            def _(sp):
                for t, a in ((x0, "x_t"), (w, "a_wo"), (bias, "a_bo")):
                    sp.dma_start(t[:], A[a]).then_inc(s_ld, 16)
                for g in range(G):
                    sp.wait_ge(s_1, 3 * g + 3)
                    sp.dma_start(out[:, BANK * g:BANK * (g + 1)], col(y, g)).then_inc(s_out, 16)
                sp.wait_ge(s_out, 16 * G)

            @block.tensor
            def _(pe):
                for g in range(G):
                    for t in range(4 * g, 4 * g + 4):
                        mm = nc.tensor.transpose(ps[:, P * t:P * (t + 1)], M["ctx"][:, t, :], M["ident"][:])
                    mm.then_inc(s_t, 1)
                pe.wait_ge(s_ld, 48)
                for g in range(G):
                    pe.wait_ge(s_te, g + 1)
                    nc.tensor.matmul(ps[:, BANK * (4 + g):BANK * (5 + g)], w[:], col(ct, g), start=True, stop=True).then_inc(s_y, 1)

            @block.scalar
            def _(act):
                for g in range(G):
                    act.wait_ge(s_t, g + 1)
                    nc.scalar.activation(col(ct, g), col(ps, g), ACT.Identity).then_inc(s_te, 1)

            @block.vector
            def _(dve):
                dve.wait_ge(s_ld, 48)
                for g in range(G):
                    b, at = g * BANK // T, g * BANK % T
                    dve.wait_ge(s_y, g + 1)
                    V.tensor_scalar(col(y, g), ps[:, BANK * (4 + g):BANK * (5 + g)], bias[:], None, ALU.add).then_inc(s_1, 1)
                    dve.wait_ge(s_1, 3 * g + 1)
                    V.tensor_tensor(col(y, g), col(y, g), col(x0, g), ALU.add).then_inc(s_1, 1)
                    dve.wait_ge(s_1, 3 * g + 2)
                    V.tensor_tensor(col(y, g), col(y, g), M["xa"][:, b, 1 + at:1 + at + BANK], ALU.add).then_inc(s_1, 1)


def build(nc, A, out):
    with ExitStack() as ctx:
        sb = lambda n, s, d=F32: ctx.enter_context(nc.sbuf_tensor(n, s, d))
        M = {
            "ps": ctx.enter_context(nc.psum_tensor("ps", [P, 8 * BANK], F32)),
            "ident": sb("ident", [P, P]), "mean_w": sb("mean_w", [P, P]), "eps": sb("eps", [P, 1]),
            "xa": sb("stream_a", [P, B, T + 1]), "ctx": sb("ctx_a", [P, TILES, P]),
        }
        M["passed"] = ctx.enter_context(nc.semaphore("waits_passed"))
        with ExitStack() as own:
            sa = lambda n, s, d=F32: own.enter_context(nc.sbuf_tensor(n, s, d))
            M.update({
                "hmask": sa("head_mask", [P, HEADS]), "iota8": sa("iota8", [P, 8]),
                "q_t": sa("q_t", [P, TOK]), "k_t": sa("k_t", [P, TOK]), "v": sa("v_a", [P, TILES, P]),
                "vh": sa("v_head", [P, 2, KBLK, HD + 1]), "flags": sa("flags", [P, UNITS]),
            })
            for name in ("pt_out", "pv_done", "ctx_out"):
                M[name] = own.enter_context(nc.semaphore(name))
            front(nc, own, A, M)
            topk_attention(nc, own, M)
            repair(nc, M)
        M["xb"] = sb("stream_b", [P, B, T + 1])
        with ExitStack() as own:
            local_transformer(nc, own, A, M)
        join(nc, A, M, out)


def _tables():
    import numpy as np

    f = np.float32
    half = np.arange(0, BD, 2, dtype=f)
    inv_freq = (f(1.0) / f(10000.0) ** (half / f(BD))).astype(f)
    t = np.arange(T, dtype=f)
    freqs = (t[:, None] * inv_freq[None, :]).astype(f)
    base = ((half + f(0.4 * BD)) / f(1.4 * BD)).astype(f)
    power = ((t - T // 2) / f(WIN // 2)).astype(f)
    scale = (base[None, :] ** power[:, None]).astype(f)
    cos, sin = np.cos(freqs), np.sin(freqs)
    both = lambda a, b: np.concatenate([a, b], -1)
    rot = np.stack([both(cos * scale, cos * scale), both(-sin * scale, sin * scale),
                    both(cos / scale, cos / scale), both(-sin / scale, sin / scale)], 0).astype(f)
    rot = rot.reshape(4, QT, P, BD).transpose(2, 0, 1, 3)
    i, j = np.arange(P)[:, None] % WIN, np.arange(2 * WIN)[None, :]
    seen = (j <= i + WIN) & (j >= i)
    big = np.where(seen, f(3.0e38), f(MASKED)).astype(f)
    masks = np.broadcast_to(big[:, None, :], (P, QT, 2 * WIN)).copy()
    masks[:WIN, 0, :WIN] = MASKED
    return {
        "c_hmask": (np.arange(P)[:, None] // HD == np.arange(HEADS)[None, :]).astype(f),
        "c_ident": np.eye(P, dtype=f),
        "c_iota8": np.broadcast_to(np.arange(8, dtype=f), (P, 8)),
        "b_rot": rot, "b_mask": masks,
    }


def _layout(inputs):
    import numpy as np

    v = {k: np.asarray(a) for k, a in inputs.items()}
    w, b = v["L0_attn_qkv_w"], v["L0_attn_qkv_b"]
    rows = lambda a: np.broadcast_to(a, (P,) + a.shape)
    wq = v["L0_ffn_Wqkv"]
    wv = wq[:, :, 2 * INNER:].reshape(DEPTH, P, PAIRS, 2, BD).transpose(0, 1, 3, 2, 4).reshape(DEPTH, P, INNER)
    qs, ks = v["L0_ffn_q_scale"], v["L0_ffn_k_scale"]
    scales = np.stack([qs, np.roll(qs, BD // 2, 1), ks, np.roll(ks, BD // 2, 1)], 1)
    w2 = np.zeros((DEPTH, 3 * P, P), np.float32)
    w2[:, :DI] = v["L0_ffn_W2"]
    b1 = np.zeros((DEPTH, 2, 3 * P), np.float32)
    b1[:, :, :DI] = v["L0_ffn_b1"].reshape(DEPTH, 2, DI)
    return {
        "x_t": v["L0_attn_x"].reshape(TOK, P).T, "a_w": w.T, "a_bq": b[:P, None], "a_bk": b[P:2 * P, None],
        "a_bv": rows(b[2 * P:]), "a_wo": v["L0_attn_out_w"].T, "a_bo": v["L0_attn_out_b"][:, None],
        "b_wqkv": np.concatenate([wq[:, :, :2 * INNER], wv], 2),
        "b_scales": np.broadcast_to(scales[:, None], (DEPTH, P, 4, BD)),
        "b_wo": v["L0_ffn_Wo"].reshape(DEPTH, PAIRS, P, P).transpose(0, 2, 1, 3),
        "b_w1": v["L0_ffn_W1"], "b_w2": w2.reshape(DEPTH, 3, P, P).transpose(0, 2, 1, 3),
        "b_b1": b1.reshape(DEPTH, 6, P).transpose(0, 2, 1),
        "b_vecs": np.stack([v["L0_ffn_ln_g"], v["L0_ffn_ln_b"], v["L0_ffn_b2"]], 2),
    }


def kernel(**inputs):
    import numpy as np
    import concourse.bacc as bacc
    from concourse.bass_utils import run_bass_kernel_spmd

    nc = bacc.Bacc("TRN2", target_bir_lowering=False, num_devices=1)
    arrays = {k: np.ascontiguousarray(a) for k, a in {**_layout(inputs), **_tables()}.items()}
    A = {k: nc.dram_tensor(k, a.shape, F32, kind="ExternalInput").ap() for k, a in arrays.items()}
    out = nc.dram_tensor("out_t", (P, TOK), F32, kind="ExternalOutput").ap()
    build(nc, A, out)
    r = run_bass_kernel_spmd(nc, [arrays], core_ids=[0])
    return np.ascontiguousarray(r.results[0]["out_t"].T).reshape(B, T, P)
```
